# Optimizing a Trainium2 kernel written in Bass

```python
import numpy as np
import jax
import jax.numpy as jnp

def _softmax(x, axis=-1):
    return jax.nn.softmax(x, axis=axis)

def _gelu(x):
    return jax.nn.gelu(x, approximate=True)

def _silu(x):
    return jax.nn.silu(x)

def _sigmoid(x):
    return jax.nn.sigmoid(x)

def _layernorm(x, axis=-1, eps=1e-05):
    m = jnp.mean(x, axis=axis, keepdims=True)
    v = jnp.var(x, axis=axis, keepdims=True)
    return (x - m) / jnp.sqrt(v + eps)

def _scatter_add(tgt, idx, src, axis=0):
    return tgt.at[idx].add(src)

def _segment_sum(src, seg, n):
    return jax.ops.segment_sum(src, seg, n)
kernel_name = 'mk_decoder_postln_d1_seqx_r4_0534ae'

def setup_inputs(seed: int=0):
    np.random.seed(seed)
    _w = jnp.asarray

    def _rec_inputs():
        import jax
        import jax.numpy as jnp
        _rk = jax.random.key(seed)
        x = -0.0002928 + 1 * jax.random.normal(jax.random.fold_in(_rk, 1), (8, 256, 256), jnp.float32)
        _lenS = 256 - jax.random.randint(jax.random.fold_in(_rk, 7), (8,), 0, max(1, 256 // 4) + 1, jnp.int32)
        _lenS2 = 256 - jax.random.randint(jax.random.fold_in(_rk, 8), (8,), 0, max(1, 256 // 4) + 1, jnp.int32)
        _ctx_1024P = jax.random.normal(jax.random.fold_in(_rk, 11), (8, 16, 256), jnp.float32)
        _ctx_1024c = jax.random.dirichlet(jax.random.fold_in(_rk, 511), 0.3 * jnp.ones((16,), jnp.float32), (8, 256))
        _ctx_1024t = jnp.einsum('bsk,bkd->bsd', _ctx_1024c, _ctx_1024P)
        _ctx_1024t = _ctx_1024t * jax.lax.rsqrt(jnp.mean(jnp.square(_ctx_1024t)) + 1e-12) * 0.953939
        ctx_1024 = -1.39393e-06 + 0.999914 * (_ctx_1024t + 0.3 * jax.random.normal(jax.random.fold_in(_rk, 611), (8, 256, 256), jnp.float32))
        _validS = jnp.arange(256)[None, :] < _lenS[:, None]
        _validS2 = jnp.arange(256)[None, :] < _lenS2[:, None]
        _causal = jnp.tril(jnp.ones((256, 256), dtype=bool))
        mask_BxS2_bf1 = jnp.ones((8, 256), dtype=bool)
        return (x, ctx_1024, mask_BxS2_bf1)
    x, ctx_1024, mask_BxS2_bf1 = _rec_inputs()

    def _L0_attn_setup():
        import jax, jax.numpy as jnp
        import numpy as np
        import math
        N_HEAD = 16
        V_HEAD = 32
        NOPE = 32
        ROPE_D = 64
        KEEP = 64
        EPS = 1e-06

        def _freqs(T, dim=ROPE_D, theta=10000.0):
            f = 1.0 / theta ** (jnp.arange(0, dim, 2, dtype=jnp.float32) / dim)
            t = jnp.arange(T, dtype=jnp.float32)
            a = jnp.outer(t, f)
            return (jnp.cos(a), jnp.sin(a))

        def _rope(x, cos, sin):
            S = x.shape[-2]
            c = cos[:S][None, None]
            s = sin[:S][None, None]
            x1, x2 = jnp.split(x, 2, axis=-1)
            return jnp.concatenate([x1 * c - x2 * s, x1 * s + x2 * c], axis=-1)

        def _rms(x, g, eps=EPS):
            return x * jax.lax.rsqrt(jnp.mean(x * x, axis=-1, keepdims=True) + eps) * g

        def _attn(q, k, v, causal):
            scale = 1.0 / math.sqrt(q.shape[-1])
            s = jnp.einsum('bhqd,bhkd->bhqk', q, k) * scale
            if causal:
                Tq, Tk = (s.shape[-2], s.shape[-1])
                mask = jnp.tril(jnp.ones((Tq, Tk), dtype=bool))
                s = jnp.where(mask, s, jnp.finfo(s.dtype).min)
            return jnp.einsum('bhqk,bhkd->bhqd', jax.nn.softmax(s, axis=-1), v)

        def _forward(x, w_cq, g_qnorm, w_dq_nope, w_dq_rope, w_ckv, g_kvnorm, w_dk_nope, w_dv, w_krope, w_imp, w_selk, w_selv, w_wink, w_winv, w_gate, w_proj):
            B, T, C = x.shape
            cos, sin = _freqs(T)
            nq = _rms(x @ w_cq, g_qnorm)
            q_nope = (nq @ w_dq_nope).reshape(B, T, N_HEAD, NOPE).transpose(0, 2, 1, 3)
            q_rope = (nq @ w_dq_rope).reshape(B, T, N_HEAD, ROPE_D).transpose(0, 2, 1, 3)
            q_rope = _rope(q_rope, cos, sin)
            q = jnp.concatenate([q_nope, q_rope], axis=-1)
            gate = jax.nn.softmax((x @ w_gate).mean(axis=1), axis=-1)
            ckv = _rms(x @ w_ckv, g_kvnorm)
            k_nope = (ckv @ w_dk_nope).reshape(B, T, N_HEAD, NOPE).transpose(0, 2, 1, 3)
            v1 = (ckv @ w_dv).reshape(B, T, N_HEAD, V_HEAD).transpose(0, 2, 1, 3)
            k_rope = (x @ w_krope).reshape(B, T, 1, ROPE_D).transpose(0, 2, 1, 3) / N_HEAD
            k_rope = _rope(k_rope, cos, sin)
            k1 = jnp.concatenate([k_nope, jnp.broadcast_to(k_rope, (B, N_HEAD, T, ROPE_D))], axis=-1)
            scores = (x @ w_imp)[..., 0]
            _, idx = jax.lax.top_k(scores, KEEP)
            idx = jnp.sort(idx, axis=1)
            sel = jnp.take_along_axis(x, idx[:, :, None], axis=1)
            ks = (sel @ w_selk).reshape(B, KEEP, N_HEAD, NOPE + ROPE_D).transpose(0, 2, 1, 3)
            vs = (sel @ w_selv).reshape(B, KEEP, N_HEAD, V_HEAD).transpose(0, 2, 1, 3)
            ks = jnp.concatenate([ks[..., :NOPE], _rope(ks[..., NOPE:], cos, sin)], axis=-1)
            kw = (x @ w_wink).reshape(B, T, N_HEAD, NOPE + ROPE_D).transpose(0, 2, 1, 3)
            vw = (x @ w_winv).reshape(B, T, N_HEAD, V_HEAD).transpose(0, 2, 1, 3)
            kw = jnp.concatenate([kw[..., :NOPE], _rope(kw[..., NOPE:], cos, sin)], axis=-1)
            a1 = _attn(q, k1, v1, causal=True)
            a2 = _attn(q, ks, vs, causal=False)
            a3 = _attn(q, kw, vw, causal=True)
            g = gate[:, :, None, None, None]
            out = g[:, 0] * a1 + g[:, 1] * a2 + g[:, 2] * a3
            out = out.transpose(0, 2, 1, 3).reshape(B, T, N_HEAD * V_HEAD)
            return out @ w_proj
        key = jax.random.key(seed)
        ks = jax.random.split(key, 20)
        B, T, C = (2, 256, 256)
        q_lora, kv_lora = (96, 32)
        std = 0.02

        def w(k, shape):
            return jax.random.normal(k, shape, dtype=jnp.float32) * std
        return {'x': jax.random.normal(ks[0], (B, T, C), dtype=jnp.float32), 'w_cq': w(ks[1], (C, q_lora)), 'g_qnorm': jnp.ones((q_lora,), jnp.float32), 'w_dq_nope': w(ks[2], (q_lora, N_HEAD * NOPE)), 'w_dq_rope': w(ks[3], (q_lora, N_HEAD * ROPE_D)), 'w_ckv': w(ks[4], (C, kv_lora)), 'g_kvnorm': jnp.ones((kv_lora,), jnp.float32), 'w_dk_nope': w(ks[5], (kv_lora, N_HEAD * NOPE)), 'w_dv': w(ks[6], (kv_lora, N_HEAD * V_HEAD)), 'w_krope': w(ks[7], (C, ROPE_D)), 'w_imp': w(ks[8], (C, 1)), 'w_selk': w(ks[9], (C, N_HEAD * (NOPE + ROPE_D))), 'w_selv': w(ks[10], (C, N_HEAD * V_HEAD)), 'w_wink': w(ks[11], (C, N_HEAD * (NOPE + ROPE_D))), 'w_winv': w(ks[12], (C, N_HEAD * V_HEAD)), 'w_gate': w(ks[13], (C, 3)), 'w_proj': w(ks[14], (N_HEAD * V_HEAD, C))}
    _L0_attn_all = _L0_attn_setup()
    _L0_attn_in = {k: v for k, v in _L0_attn_all.items() if k in ('w_cq', 'g_qnorm', 'w_dq_nope', 'w_dq_rope', 'w_ckv', 'g_kvnorm', 'w_dk_nope', 'w_dv', 'w_krope', 'w_imp', 'w_selk', 'w_selv', 'w_wink', 'w_winv', 'w_gate', 'w_proj')}
    del _L0_attn_all

    def _L0_xattn_setup():
        import jax, jax.numpy as jnp
        import numpy as np
        N_HEADS = 16
        D_MODEL = 256
        HEAD_DIM = D_MODEL // N_HEADS
        MASK_FILL = -100000000.0

        def _split_heads(x):
            B, S, _ = x.shape
            return x.reshape(B, S, N_HEADS, HEAD_DIM).transpose(0, 2, 1, 3)
        key = jax.random.key(seed)
        ks = jax.random.split(key, 12)
        B, L, P = (2, 512, 512)
        s = 1.0 / np.sqrt(D_MODEL).astype(np.float32)
        inp = {'q': jax.random.normal(ks[0], (B, L, D_MODEL), dtype=jnp.float32), 'k': jax.random.normal(ks[1], (B, P, D_MODEL), dtype=jnp.float32), 'v': jax.random.normal(ks[2], (B, P, D_MODEL), dtype=jnp.float32), 'attention_mask': jnp.ones((B, P), dtype=bool), 'Wq': jax.random.normal(ks[3], (D_MODEL, D_MODEL), dtype=jnp.float32) * s, 'bq': jnp.zeros((D_MODEL,), dtype=jnp.float32), 'Wk': jax.random.normal(ks[4], (D_MODEL, D_MODEL), dtype=jnp.float32) * s, 'bk': jnp.zeros((D_MODEL,), dtype=jnp.float32), 'Wv': jax.random.normal(ks[5], (D_MODEL, D_MODEL), dtype=jnp.float32) * s, 'bv': jnp.zeros((D_MODEL,), dtype=jnp.float32), 'Wo': jax.random.normal(ks[6], (D_MODEL, D_MODEL), dtype=jnp.float32) * s, 'bo': jnp.zeros((D_MODEL,), dtype=jnp.float32)}
        return inp
    _L0_xattn_all = _L0_xattn_setup()
    _L0_xattn_in = {k: v for k, v in _L0_xattn_all.items() if k in ('Wq', 'bq', 'Wk', 'bk', 'Wv', 'bv', 'Wo', 'bo')}
    del _L0_xattn_all

    def _L0_ffn_setup():
        import jax, jax.numpy as jnp
        import numpy as np
        EMBED = 256
        NUM_EXPERTS = 8
        ACTIVE = 2
        HIDDEN = 4 * EMBED
        key = jax.random.key(seed)
        ks = jax.random.split(key, 7)
        B, T = (4, 256)
        s1 = 1.0 / np.sqrt(EMBED)
        s2 = 1.0 / np.sqrt(HIDDEN)
        return {'x': jax.random.normal(ks[0], (B, T, EMBED), dtype=jnp.float32), 'W1': jax.random.uniform(ks[1], (NUM_EXPERTS, EMBED, HIDDEN), jnp.float32, -s1, s1), 'b1': jax.random.uniform(ks[2], (NUM_EXPERTS, HIDDEN), jnp.float32, -s1, s1), 'W2': jax.random.uniform(ks[3], (NUM_EXPERTS, HIDDEN, EMBED), jnp.float32, -s2, s2), 'b2': jax.random.uniform(ks[4], (NUM_EXPERTS, EMBED), jnp.float32, -s2, s2), 'Wr': jax.random.uniform(ks[5], (EMBED, NUM_EXPERTS), jnp.float32, -s1, s1), 'br': jax.random.uniform(ks[6], (NUM_EXPERTS,), jnp.float32, -s1, s1)}
    _L0_ffn_all = _L0_ffn_setup()
    _L0_ffn_in = {k: v for k, v in _L0_ffn_all.items() if k in ('W1', 'b1', 'W2', 'b2', 'Wr', 'br')}
    del _L0_ffn_all
    return {'x': x, 'ctx_1024': ctx_1024, 'mask_BxS2_bf1': mask_BxS2_bf1, 'L0_attn_w_cq': _L0_attn_in['w_cq'], 'L0_attn_g_qnorm': _L0_attn_in['g_qnorm'], 'L0_attn_w_dq_nope': _L0_attn_in['w_dq_nope'], 'L0_attn_w_dq_rope': _L0_attn_in['w_dq_rope'], 'L0_attn_w_ckv': _L0_attn_in['w_ckv'], 'L0_attn_g_kvnorm': _L0_attn_in['g_kvnorm'], 'L0_attn_w_dk_nope': _L0_attn_in['w_dk_nope'], 'L0_attn_w_dv': _L0_attn_in['w_dv'], 'L0_attn_w_krope': _L0_attn_in['w_krope'], 'L0_attn_w_imp': _L0_attn_in['w_imp'], 'L0_attn_w_selk': _L0_attn_in['w_selk'], 'L0_attn_w_selv': _L0_attn_in['w_selv'], 'L0_attn_w_wink': _L0_attn_in['w_wink'], 'L0_attn_w_winv': _L0_attn_in['w_winv'], 'L0_attn_w_gate': _L0_attn_in['w_gate'], 'L0_attn_w_proj': _L0_attn_in['w_proj'], 'L0_xattn_Wq': _L0_xattn_in['Wq'], 'L0_xattn_bq': _L0_xattn_in['bq'], 'L0_xattn_Wk': _L0_xattn_in['Wk'], 'L0_xattn_bk': _L0_xattn_in['bk'], 'L0_xattn_Wv': _L0_xattn_in['Wv'], 'L0_xattn_bv': _L0_xattn_in['bv'], 'L0_xattn_Wo': _L0_xattn_in['Wo'], 'L0_xattn_bo': _L0_xattn_in['bo'], 'L0_ffn_W1': _L0_ffn_in['W1'], 'L0_ffn_b1': _L0_ffn_in['b1'], 'L0_ffn_W2': _L0_ffn_in['W2'], 'L0_ffn_b2': _L0_ffn_in['b2'], 'L0_ffn_Wr': _L0_ffn_in['Wr'], 'L0_ffn_br': _L0_ffn_in['br']}

def reference(x, ctx_1024, mask_BxS2_bf1, L0_attn_w_cq, L0_attn_g_qnorm, L0_attn_w_dq_nope, L0_attn_w_dq_rope, L0_attn_w_ckv, L0_attn_g_kvnorm, L0_attn_w_dk_nope, L0_attn_w_dv, L0_attn_w_krope, L0_attn_w_imp, L0_attn_w_selk, L0_attn_w_selv, L0_attn_w_wink, L0_attn_w_winv, L0_attn_w_gate, L0_attn_w_proj, L0_xattn_Wq, L0_xattn_bq, L0_xattn_Wk, L0_xattn_bk, L0_xattn_Wv, L0_xattn_bv, L0_xattn_Wo, L0_xattn_bo, L0_ffn_W1, L0_ffn_b1, L0_ffn_W2, L0_ffn_b2, L0_ffn_Wr, L0_ffn_br):
    import jax
    import jax.numpy as jnp

    def _L0_attn_ref(x, w_cq, g_qnorm, w_dq_nope, w_dq_rope, w_ckv, g_kvnorm, w_dk_nope, w_dv, w_krope, w_imp, w_selk, w_selv, w_wink, w_winv, w_gate, w_proj):
        import jax, jax.numpy as jnp
        import numpy as np
        import math
        N_HEAD = 16
        V_HEAD = 32
        NOPE = 32
        ROPE_D = 64
        KEEP = 64
        EPS = 1e-06

        def _freqs(T, dim=ROPE_D, theta=10000.0):
            f = 1.0 / theta ** (jnp.arange(0, dim, 2, dtype=jnp.float32) / dim)
            t = jnp.arange(T, dtype=jnp.float32)
            a = jnp.outer(t, f)
            return (jnp.cos(a), jnp.sin(a))

        def _rope(x, cos, sin):
            S = x.shape[-2]
            c = cos[:S][None, None]
            s = sin[:S][None, None]
            x1, x2 = jnp.split(x, 2, axis=-1)
            return jnp.concatenate([x1 * c - x2 * s, x1 * s + x2 * c], axis=-1)

        def _rms(x, g, eps=EPS):
            return x * jax.lax.rsqrt(jnp.mean(x * x, axis=-1, keepdims=True) + eps) * g

        def _attn(q, k, v, causal):
            scale = 1.0 / math.sqrt(q.shape[-1])
            s = jnp.einsum('bhqd,bhkd->bhqk', q, k) * scale
            if causal:
                Tq, Tk = (s.shape[-2], s.shape[-1])
                mask = jnp.tril(jnp.ones((Tq, Tk), dtype=bool))
                s = jnp.where(mask, s, jnp.finfo(s.dtype).min)
            return jnp.einsum('bhqk,bhkd->bhqd', jax.nn.softmax(s, axis=-1), v)

        def _forward(x, w_cq, g_qnorm, w_dq_nope, w_dq_rope, w_ckv, g_kvnorm, w_dk_nope, w_dv, w_krope, w_imp, w_selk, w_selv, w_wink, w_winv, w_gate, w_proj):
            B, T, C = x.shape
            cos, sin = _freqs(T)
            nq = _rms(x @ w_cq, g_qnorm)
            q_nope = (nq @ w_dq_nope).reshape(B, T, N_HEAD, NOPE).transpose(0, 2, 1, 3)
            q_rope = (nq @ w_dq_rope).reshape(B, T, N_HEAD, ROPE_D).transpose(0, 2, 1, 3)
            q_rope = _rope(q_rope, cos, sin)
            q = jnp.concatenate([q_nope, q_rope], axis=-1)
            gate = jax.nn.softmax((x @ w_gate).mean(axis=1), axis=-1)
            ckv = _rms(x @ w_ckv, g_kvnorm)
            k_nope = (ckv @ w_dk_nope).reshape(B, T, N_HEAD, NOPE).transpose(0, 2, 1, 3)
            v1 = (ckv @ w_dv).reshape(B, T, N_HEAD, V_HEAD).transpose(0, 2, 1, 3)
            k_rope = (x @ w_krope).reshape(B, T, 1, ROPE_D).transpose(0, 2, 1, 3) / N_HEAD
            k_rope = _rope(k_rope, cos, sin)
            k1 = jnp.concatenate([k_nope, jnp.broadcast_to(k_rope, (B, N_HEAD, T, ROPE_D))], axis=-1)
            scores = (x @ w_imp)[..., 0]
            _, idx = jax.lax.top_k(scores, KEEP)
            idx = jnp.sort(idx, axis=1)
            sel = jnp.take_along_axis(x, idx[:, :, None], axis=1)
            ks = (sel @ w_selk).reshape(B, KEEP, N_HEAD, NOPE + ROPE_D).transpose(0, 2, 1, 3)
            vs = (sel @ w_selv).reshape(B, KEEP, N_HEAD, V_HEAD).transpose(0, 2, 1, 3)
            ks = jnp.concatenate([ks[..., :NOPE], _rope(ks[..., NOPE:], cos, sin)], axis=-1)
            kw = (x @ w_wink).reshape(B, T, N_HEAD, NOPE + ROPE_D).transpose(0, 2, 1, 3)
            vw = (x @ w_winv).reshape(B, T, N_HEAD, V_HEAD).transpose(0, 2, 1, 3)
            kw = jnp.concatenate([kw[..., :NOPE], _rope(kw[..., NOPE:], cos, sin)], axis=-1)
            a1 = _attn(q, k1, v1, causal=True)
            a2 = _attn(q, ks, vs, causal=False)
            a3 = _attn(q, kw, vw, causal=True)
            g = gate[:, :, None, None, None]
            out = g[:, 0] * a1 + g[:, 1] * a2 + g[:, 2] * a3
            out = out.transpose(0, 2, 1, 3).reshape(B, T, N_HEAD * V_HEAD)
            return out @ w_proj
        return _forward(x, w_cq, g_qnorm, w_dq_nope, w_dq_rope, w_ckv, g_kvnorm, w_dk_nope, w_dv, w_krope, w_imp, w_selk, w_selv, w_wink, w_winv, w_gate, w_proj)

    def _L0_xattn_ref(q, k, v, attention_mask, Wq, bq, Wk, bk, Wv, bv, Wo, bo):
        import jax, jax.numpy as jnp
        import numpy as np
        N_HEADS = 16
        D_MODEL = 256
        HEAD_DIM = D_MODEL // N_HEADS
        MASK_FILL = -100000000.0

        def _split_heads(x):
            B, S, _ = x.shape
            return x.reshape(B, S, N_HEADS, HEAD_DIM).transpose(0, 2, 1, 3)
        qm = _split_heads(q @ Wq.T + bq)
        km = _split_heads(k @ Wk.T + bk)
        vm = _split_heads(v @ Wv.T + bv)
        scores = jnp.einsum('bnlh,bnph->bnlp', qm, km) / np.sqrt(HEAD_DIM).astype(np.float32)
        mask = attention_mask[:, None, None, :]
        scores = jnp.where(mask, scores, MASK_FILL)
        attn = jax.nn.softmax(scores, axis=-1)
        out = jnp.einsum('bnlp,bnph->bnlh', attn, vm)
        B, _, L, _ = out.shape
        out = out.transpose(0, 2, 1, 3).reshape(B, L, D_MODEL)
        return out @ Wo.T + bo

    def _L0_ffn_ref(x, W1, b1, W2, b2, Wr, br):
        import jax, jax.numpy as jnp
        import numpy as np
        EMBED = 256
        NUM_EXPERTS = 8
        ACTIVE = 2
        HIDDEN = 4 * EMBED
        scores = x @ Wr + br
        topk_scores, indices = jax.lax.top_k(scores, ACTIVE)
        one_hot = jax.nn.one_hot(indices, NUM_EXPERTS, dtype=scores.dtype)
        mask = jnp.einsum('btke,btk->bte', one_hot, topk_scores)
        router_output = jax.nn.softmax(mask, axis=-1)
        h = jax.nn.relu(jnp.einsum('btd,edh->bteh', x, W1) + b1)
        expert_outputs = jnp.einsum('bteh,ehd->bted', h, W2) + b2
        return jnp.einsum('bte,bted->btd', router_output, expert_outputs)
    x = _layernorm(x + _L0_attn_ref(x, L0_attn_w_cq, L0_attn_g_qnorm, L0_attn_w_dq_nope, L0_attn_w_dq_rope, L0_attn_w_ckv, L0_attn_g_kvnorm, L0_attn_w_dk_nope, L0_attn_w_dv, L0_attn_w_krope, L0_attn_w_imp, L0_attn_w_selk, L0_attn_w_selv, L0_attn_w_wink, L0_attn_w_winv, L0_attn_w_gate, L0_attn_w_proj), axis=-1)
    x = _layernorm(x + _L0_xattn_ref(x, ctx_1024, ctx_1024, mask_BxS2_bf1, L0_xattn_Wq, L0_xattn_bq, L0_xattn_Wk, L0_xattn_bk, L0_xattn_Wv, L0_xattn_bv, L0_xattn_Wo, L0_xattn_bo), axis=-1)
    x = _layernorm(x + _L0_ffn_ref(x, L0_ffn_W1, L0_ffn_b1, L0_ffn_W2, L0_ffn_b2, L0_ffn_Wr, L0_ffn_br), axis=-1)
    return x

_drawn_inputs = setup_inputs


def setup_inputs(seed=0):
    import zlib

    import numpy as np

    out = dict(_drawn_inputs(seed))
    spreads = {'L0_attn_g_qnorm': (1.0, 0.6),
     'L0_attn_g_kvnorm': (1.0, 0.6),
     'L0_xattn_bq': (0.0, 0.387),
     'L0_xattn_bk': (0.0, 2.0),
     'L0_xattn_bv': (0.0, 0.1),
     'L0_xattn_bo': (0.0, 0.1)}
    factors = {'L0_attn_w_cq': 8.0,
     'L0_attn_w_dq_nope': 8.0,
     'L0_attn_w_dq_rope': 8.0,
     'L0_attn_w_ckv': 8.0,
     'L0_attn_w_dk_nope': 8.0,
     'L0_attn_w_dv': 8.0,
     'L0_attn_w_krope': 21.97,
     'L0_attn_w_imp': 8.0,
     'L0_attn_w_selk': 8.0,
     'L0_attn_w_selv': 8.0,
     'L0_attn_w_wink': 8.0,
     'L0_attn_w_winv': 8.0,
     'L0_attn_w_gate': 8.0,
     'L0_attn_w_proj': 5.849,
     'L0_ffn_b1': 8.0,
     'L0_ffn_b2': 7.651,
     'L0_ffn_br': 8.0}
    for name, (base, spread) in spreads.items():
        noise = np.random.default_rng([zlib.crc32(name.encode()), seed]).standard_normal(out[name].shape)
        drawn = base * np.exp(spread * noise) if base else spread * noise
        out[name] = jnp.asarray(drawn.astype(out[name].dtype))
    for name, factor in factors.items():
        out[name] = (out[name] * factor).astype(out[name].dtype)
    return out
```

```python
from contextlib import ExitStack

import numpy as np

import concourse.bass as bass
from concourse import mybir

F32 = mybir.dt.float32
F32R = mybir.dt.float32r
BF16 = mybir.dt.bfloat16
U8 = mybir.dt.uint8
ALU = mybir.AluOpType
ACT = mybir.ActivationFunctionType
AX = mybir.AxisListType.X

P = 128
NB, T, C = 8, 256, 256
NT = T // P
NC = C // P
NH = 16
HD = 32
QK = 3 * HD
HW = NH * HD
QL, KL = 96, 32
KEEP = 64
RP = 2 * HD
PA = QL + KL + RP + 3
XD = 16
SLOTS = 8
NE, HID = 8, 1024
NTOK = NB * T
TILES = NTOK // P
NHT = HID // P
CONSTS = 13
DVE_CHAIN = 50
CH = 512
NCH = NTOK // CH
LOW = -3.0e38
MASK_FILL = -1.0e8
ATT_SCALE = 1.0 / float(np.sqrt(np.float32(QK)))
X_SCALE = 1.0 / float(np.sqrt(np.float32(XD)))
LN_EPS, RMS_EPS = 1e-5, 1e-6

SEG = [(0, 0, 128, 128, 0, 0), (0, 128, 64, 0, 1, 1), (0, 192, 256, 0, 1, 2),
       (1, 0, 64, 0, 0, 1), (1, 64, 128, 128, 0, 2), (1, 192, 256, 0, 1, 0)]
SEG_AT = [0, 128, 192, 448, 512, 640]
SW = 896


PRIMED = 1


def prime(eng, sems):
    for s in sems:
        eng.sem_inc(s, PRIMED)


class Signal:

    def __init__(self, sem, per, base=0):
        self.sem, self.per, self.base = sem, per, base

    def at(self, i, k):
        return i * self.per + (k + self.base)


class BankPlan:

    def __init__(self, full, free):
        self.full, self.free = full, free
        self.place, self.count = {}, {}

    def add(self, name, bank):
        self.place[name] = (bank, self.count.get(bank, 0))
        self.count[bank] = self.count.get(bank, 0) + 1

    def bank(self, name):
        return self.place[name][0]

    def full_sem(self, name):
        return self.full[self.bank(name)]

    def free_sem(self, name):
        return self.free[self.bank(name)]

    def before(self, name, i):
        b, k = self.place[name]
        return i * self.count[b] + (k + PRIMED)

    def after(self, name, i):
        return self.before(name, i) + 1

    def turns(self, bank, i):
        return i * self.count[bank] + PRIMED


class Chain:

    def __init__(self, sem, per=0, i=0):
        self.sem, self.per, self.i, self.n = sem, per, i, 0

    def step(self):
        self.n += 1
        return self.sem

    def value(self):
        return self.i * self.per + self.n

    def close(self):
        assert self.n == self.per, (self.n, self.per)


def block_plan(full, free):
    plan = BankPlan(full, free)
    s = 0

    def ring(name):
        nonlocal s
        plan.add(name, f"S{s % 4}")
        s += 1

    t = 0

    def turn(name):
        nonlocal t
        plan.add(name, f"T{t % 2}")
        t += 1

    plan.add("xT", "X")
    plan.add("ctxT", "O")
    ring("first")
    ring("imp")
    for t_ in range(NT):
        for c in ("n", "a", "b"):
            ring(("kw", t_, c))
    plan.add("gate", "X")
    turn("latT")
    for t_ in range(NT):
        ring(("vw", t_))
    for g in range(4):
        turn(("kwT", 0, g))
    for c in ("n", "a", "b", "c"):
        ring(("q", 0, c))
    for g in range(4):
        turn(("kwT", 1, g))
    for c in ("n", "a", "b", "c"):
        ring(("q", 1, c))
    for t_ in range(NT):
        ring(("v1", t_))
    plan.add("pos", "X")
    for g in range(4):
        turn(("qT", 0, g))
    ring("xsel")
    for g in range(4):
        turn(("qT", 1, g))
    ring("vs")
    for c in ("n", "a", "b"):
        ring(("ks", c))
    for g in range(2):
        turn(("ksT", g))
    for h in range(NH):
        for half in range(2):
            plan.add(("s", h, half), f"S{2 * (h % 2) + half}")
        for half in range(2):
            plan.add(("pT", h, half), f"T{half}")
    for g in range(4):
        plan.add(("o", g), "O")
    plan.add("proj", "X")
    plan.add("x1T", "X")
    for n, name in enumerate(("kx", "vx", "qx")):
        plan.add(name, f"S{n}")
    n = 0
    for name in ("kxT", "qxT"):
        for t_ in range(NT):
            for g in range(2):
                plan.add((name, t_, g), f"T{n % 2}")
                n += 1
    for h in range(NH):
        plan.add(("sx", h), f"S{(h + 3) % 4}")
        plan.add(("pxT", h), f"T{h % 2}")
    for g in range(4):
        plan.add(("ox", g), "O")
    plan.add("projx", "X")
    return plan


def attention_block(nc, x2, w):
    ctx = ExitStack()
    with ctx:
        def sb(name, shape, dt=F32):
            return ctx.enter_context(nc.sbuf_tensor(name, shape, dt))

        def sem(name):
            return ctx.enter_context(nc.semaphore(name))

        BANKS = ("S0", "S1", "S2", "S3", "T0", "T1", "O", "X")
        pst = {b: ctx.enter_context(nc.psum_tensor(f"ps_{b}", [P, 512], F32)) for b in BANKS}
        plan = block_plan({b: sem(f"full_{b}") for b in BANKS}, {b: sem(f"free_{b}") for b in BANKS})

        def ps(name):
            return pst[plan.bank(name)]

        w_first = sb("w_first", [P, NC, PA])
        w_imp = sb("w_imp", [P, NC, P])
        w_q = sb("w_q", [QL, 4, HW])
        w_kw = sb("w_kw", [P, NC, 3, HW])
        w_vw = sb("w_vw", [P, NC, HW])
        w_ks = sb("w_ks", [P, NC, 3, HW])
        w_vs = sb("w_vs", [P, NC, HW])
        w_dv = sb("w_dv", [P, HW])
        w_proj = sb("w_proj", [P, 4, C])
        wx_q = sb("wx_q", [P, NC, C])
        wx_k = sb("wx_k", [P, NC, C])
        wx_v = sb("wx_v", [P, NC, C])
        wx_o = sb("wx_o", [P, 4, C])
        rows = sb("rows", [P, 4, C])
        g_q = sb("g_q", [P, QL])
        g_kv = sb("g_kv", [P, KL])
        cs = sb("cs", [P, 2, NT, HD])
        ident = sb("ident", [P, P])
        identb = sb("identb", [P, P], BF16)
        upper = sb("upper", [P, P])
        ones = sb("ones", [P, P])
        cmask = sb("cmask", [P, 2 * P])
        tie = sb("tie", [P, NT, T])
        count = sb("count", [P, KEEP])
        halves = sb("halves", [P, 4])

        xin = sb("xin", [P, NT, C])
        cin = sb("cin", [P, NT, C])
        mrow = sb("mrow", [P, T], U8)
        mcol = sb("mcol", [P, NT], U8)
        xT = sb("xT_sb", [P, NC, T])
        cT = sb("cT_sb", [P, NC, T])
        x1T = xT
        pa = sb("pa", [P, NT, PA])
        lat = sb("lat", [P, NT, QL])
        k1r = sb("k1r", [P, NT, P])
        ktmp = sb("ktmp", [P, 4, NT, HD])
        latT = sb("latT_sb", [P, 2, T])
        sq = sb("sq", [P, QL])
        ss = sb("ss", [P, 4])
        rs = sb("rs", [P, 4])
        gl = sb("gl", [P, 8])
        gate = sb("gate_sb", [P, 4])
        srow = sb("srow", [P, T])
        scol = sb("scol", [P, NT])
        rank = sb("rank", [P, NT])
        sel = sb("sel", [P, NT])
        pos = sb("pos_sb", [P, NT])
        pick = sb("pick", [P, NT, KEEP])
        xselT = sb("xselT", [P, NC, KEEP])
        rk = sb("rk", [P, 2, NH, QK])
        rq = sb("rq", [P, 2, NH, P])
        qT = sb("qT_sb", [P, NH, T])
        kT = sb("kT_sb", [QK, NH, KEEP + T])
        v1 = sb("v1_sb", [P, NT, HW])
        vw = sb("vw_sb", [P, NT, HW])
        vs = sb("vs_sb", [KEEP, HW])
        sm = sb("sm", [P, 2, SW])
        pr = sb("pr", [P, 3, SW])
        pT = sb("pT_sb", [P, 2, 1024])
        cmp1, cmp2 = (sm[:, k, 0:NT * T].rearrange("p (t n) -> p t n", t=NT) for k in range(2))
        rt = pr[:, :, :].rearrange("p a b -> p (a b)")[:, 0:4 * HW].rearrange("p (k n) -> p k n", k=4)
        q32, k32, rem, res = (pT[:, k // 2, 512 * (k % 2):512 * (k % 2) + 512].rearrange(
            "p (t c) -> p t c", t=NT) for k in range(4))
        mx = sb("mx", [P, 2, 6])
        nmx = sb("nmx", [P, 2, 6])
        den = sb("den", [P, 2, 6])
        rden = sb("rden", [P, 2, 6])
        oT = sb("oT", [P, 4, T])
        x1 = sb("x1", [P, NT, C])
        x1b = vw[:, 0, :].rearrange("p (t c) -> p t c", t=NT)
        st = sb("st", [P, NT, 8])
        mv = sb("mv", [P, NT, 2])
        ve = sb("ve", [P, NT])
        rstd = sb("rstd", [P, NT])
        split_q = rq[:, 0, :, :].rearrange("p h d -> p (h d)").bitcast(BF16).rearrange(
            "p (n s d) -> p n s d", s=SLOTS, d=XD)
        split_k = rq[:, 1, :, :].rearrange("p h d -> p (h d)").bitcast(BF16).rearrange(
            "p (n s d) -> p n s d", s=SLOTS, d=XD)
        qxT = qT[:, 0:8, :].rearrange("p h t -> p (h t)").bitcast(BF16).rearrange("p (h t) -> p h t", h=NH)
        kxT = qT[:, 8:16, :].rearrange("p h t -> p (h t)").bitcast(BF16).rearrange("p (h t) -> p h t", h=NH)
        vx = rk[:, 1, :, :].rearrange("p h d -> p (h d)")[:, 0:NT * HW].rearrange(
            "p (t h d) -> p t h d", t=NT, h=NH)
        fill = vw[:, 1, 0:T]
        mf = sb("mf", [P, NT])

        w_in = sem("weights_in")
        s_const = sem("consts_done")
        s_absorb = sem("absorbed_ps")
        s_absorbed = sem("absorbed_sb")
        s_wide = sem("imp_wide")
        x_in = Signal(sem("x_in"), 16)
        c_in = Signal(sem("ctx_in"), 48)
        first_sb = Signal(sem("first_sb"), 1)
        sumsq = Signal(sem("sumsq"), 1)
        rms_sb = Signal(sem("rms_sb"), 1)
        lat_sb = Signal(sem("lat_sb"), 1)
        gate_max = Signal(sem("gate_max"), 1)
        gate_exp = Signal(sem("gate_exp"), 1)
        gate_done = Signal(sem("gate_done"), 1)
        sel_sb = Signal(sem("sel_sb"), 1)
        pick_sb = Signal(sem("pick_sb"), 1)
        rope_in = Signal(sem("rope_in"), 5)
        rope_out = Signal(sem("rope_out"), 10, PRIMED)
        nope_sb = Signal(sem("nope_sb"), 7)
        ctx_turned = Signal(sem("ctx_turned"), 1)
        score_sb = Signal(sem("score_sb"), 2 * NH)
        exp_done = Signal(sem("exp_done"), 2 * NH)
        rden_sb = Signal(sem("rden_sb"), 2 * NH)
        prob_sb = Signal(sem("prob_sb"), 2 * NH)
        pv_done = Signal(sem("pv_done"), 2 * NH)
        x_used = Signal(sem("x_used"), 1, PRIMED)
        m_used = Signal(sem("mask_used"), 1, PRIMED)
        var_sb = Signal(sem("var_sb"), 2)
        rstd_sb = Signal(sem("rstd_sb"), 2)
        x1_sb = Signal(sem("x1_sb"), 1)
        x1b_sb = Signal(sem("x1b_sb"), 1)
        kx_part = Signal(sem("kx_part"), 1)
        qx_part = Signal(sem("qx_part"), 3)
        kx_sb = Signal(sem("kx_split"), 1)
        qx_sb = Signal(sem("qx_split"), 3)
        s_dve = sem("dve_chain")
        s_pass = sem("wait_carrier")

        UNITS = [("kw", 0), ("kw", 1), ("q", 0), ("q", 1), ("ks", 0)]

        def unit_rows(u):
            kind, t = UNITS[u]
            if kind == "q":
                return rq[:, t, :, :], P
            if kind == "kw":
                return rk[:, t, :, :], P
            return rk[0:KEEP, 0, :, :], KEEP

        def unit_fill(u, c):
            kind, t = UNITS[u]
            return ("ks", c) if kind == "ks" else (kind, t, c)

        N_WEIGHTS = 28
        block = ctx.enter_context(nc.Block())

        @block.sync
        def _(sp):
            n = 0

            def load(dst, src):
                nonlocal n
                sp.dma_start(dst, src, allow_slow_non_contiguous=True).then_inc(w_in, 16)
                n += 1

            load(pr[0:HD, :, :].rearrange("p a b -> p (a b)")[:, 0:NH * QL],
                 w["dq_nopeT"].rearrange("n h c -> n (h c)"))
            load(pr[0:HD, :, :].rearrange("p a b -> p (a b)")[:, NH * QL:NH * QL + HW],
                 w["dkT"].rearrange("n h c -> n (h c)"))
            load(w_first[:, :, 0:QL], w["cq"].rearrange("(c p) n -> p c n", p=P))
            load(w_first[:, :, QL:QL + KL], w["ckv"].rearrange("(c p) n -> p c n", p=P))
            load(w_first[:, :, QL + KL:QL + KL + RP], w["krope"].rearrange("(c p) n -> p c n", p=P))
            load(w_first[:, :, PA - 3:PA], w["gate"].rearrange("(c p) n -> p c n", p=P))
            load(w_imp[:, :, 0:1], w["imp"].rearrange("(c p) n -> p c n", p=P))
            load(g_q[:, :], w["g_q"].partition_broadcast(P))
            load(g_kv[:, :], w["g_kv"].partition_broadcast(P))
            load(cs[:, 0, :, :], w["cos"].rearrange("(t p) f -> p t f", p=P))
            load(cs[:, 1, :, :], w["sin"].rearrange("(t p) f -> p t f", p=P))
            load(w_q[:, 0:3, :], w["dq"].rearrange("c s n -> c s n"))
            load(w_kw[:, 0, :, :], w["wink"][0:P])
            load(w_kw[:, 1, :, :], w["wink"][P:C])
            load(w_vw[:, :, :], w["winv"].rearrange("(c p) n -> p c n", p=P))
            load(w_dv[QK:P, :], w["dv"])
            load(w_ks[:, 0, :, :], w["selk"][0:P])
            load(w_ks[:, 1, :, :], w["selk"][P:C])
            load(w_vs[:, :, :], w["selv"].rearrange("(c p) n -> p c n", p=P))
            load(w_proj[:, :, :], w["proj"].rearrange("(g p) n -> p g n", p=P))
            for dst, name in ((wx_q, "xqT"), (wx_k, "xkT"), (wx_v, "xvT")):
                load(dst[:, :, :], w[name].rearrange("(c p) n -> p c n", p=P))
            sp.wait_ge(s_const, 3)
            for j in range(4):
                load(wx_o[HD * j:HD * j + XD, :, :],
                     w["xoT"].rearrange("(g j d) n -> j d g n", g=4, j=4)[j])
            load(rows[:, :, :], w["rows"].partition_broadcast(P))
            assert n == N_WEIGHTS, n
            with sp.Fori(0, NB) as i:
                sp.wait_ge(x_used.sem, x_used.at(i, 0))
                sp.dma_start(xin[:, :, :], w["x"].rearrange("b (t p) c -> b p t c", p=P)[i]
                             ).then_inc(x_in.sem, 16)
                sp.wait_ge(m_used.sem, m_used.at(i, 0))
                sp.dma_start(cin[:, :, :], w["ctx"].rearrange("b (t p) c -> b p t c", p=P)[i]
                             ).then_inc(c_in.sem, 16)
                sp.dma_start(mrow[:, :], w["mask"][i].partition_broadcast(P)).then_inc(c_in.sem, 16)
                sp.dma_start(mcol[:, :], w["mask"].rearrange("b (t p) -> b p t", p=P)[i],
                             allow_slow_non_contiguous=True).then_inc(c_in.sem, 16)

        @block.gpsimd
        def _(pool):
            prime(pool, [rope_out.sem])
            ch = Chain(s_const)
            pool.memset(wx_o[:, :, :], 0.0).then_inc(ch.step(), 1)
            pool.memset(ones[:, :], 1.0).then_inc(ch.step(), 1)
            pool.memset(halves[:, :], -0.5).then_inc(ch.step(), 1)
            pool.wait_ge(ch.sem, ch.value())
            pool.affine_select(out=ident[:, :], in_=ones[:, :], compare_op=ALU.is_equal, fill=0.0,
                               base=0, pattern=[[-1, P]], channel_multiplier=1).then_inc(ch.step(), 1)
            pool.affine_select(out=upper[:, :], in_=ones[:, :], compare_op=ALU.is_ge, fill=0.0,
                               base=0, pattern=[[1, P]], channel_multiplier=-1).then_inc(ch.step(), 1)
            pool.memset(cmask[:, :], 0.0).then_inc(ch.step(), 1)
            pool.memset(tie[:, :, :], 1.0).then_inc(ch.step(), 1)
            pool.memset(k1r[:, :, :], 0.0).then_inc(ch.step(), 1)
            pool.iota(count[:, :], pattern=[[1, KEEP]], base=1, channel_multiplier=0,
                      allow_small_or_imprecise_dtypes=True).then_inc(ch.step(), 1)
            pool.wait_ge(ch.sem, ch.value())
            pool.tensor_copy(identb[:, :], ident[:, :]).then_inc(ch.step(), 1)
            pool.affine_select(out=cmask[:, P:2 * P], in_=cmask[:, P:2 * P], compare_op=ALU.is_ge,
                               fill=LOW, base=0, pattern=[[-1, P]], channel_multiplier=1).then_inc(ch.step(), 1)
            for t in range(NT):
                pool.affine_select(out=tie[:, t, :], in_=tie[:, t, :], compare_op=ALU.is_gt,
                                   fill=0.0, base=P * t, pattern=[[-1, T]], channel_multiplier=1).then_inc(ch.step(), 1)
            assert ch.n == CONSTS
            pool.wait_ge(w_in, 16 * N_WEIGHTS)
            with pool.Fori(0, NB) as i:
                pool.wait_ge(sumsq.sem, sumsq.at(i, 1))
                pool.tensor_tensor(rs[:, :], ss[:, :], halves[:, :], ALU.pow).then_inc(rms_sb.sem, 1)

                def rope_sums(u):
                    rows_, n = unit_rows(u)
                    if UNITS[u][0] == "ks":
                        pool.wait_ge(plan.full_sem(("kwT", 0, 3)), plan.after(("kwT", 0, 3), i))
                    r = rt[0:n, :, :].rearrange("p k (h d) -> p k h d", h=NH)
                    pool.wait_ge(rope_in.sem, rope_in.at(i, u + 1))
                    pool.tensor_tensor(rows_[:, :, HD:2 * HD], r[:, 0], r[:, 2], ALU.subtract
                                       ).then_inc(rope_out.sem, 1)
                    pool.wait_ge(plan.free_sem(unit_fill(u, "b")), plan.after(unit_fill(u, "b"), i))
                    pool.tensor_tensor(rows_[:, :, 2 * HD:3 * HD], r[:, 1], r[:, 3], ALU.add
                                       ).then_inc(rope_out.sem, 1)

                for u in range(5):
                    rope_sums(u)

                def normalise(h):
                    pool.wait_ge(rden_sb.sem, rden_sb.at(i, h + 1))
                    for n, (half, off, width, m, q, br) in enumerate(SEG):
                        p_ = pr[:, h % 3, SEG_AT[n]:SEG_AT[n] + width]
                        last = pool.tensor_tensor(p_, p_, rden[:, h % 2, n:n + 1].to_broadcast([P, width]),
                                                  ALU.mult)
                    last.then_inc(prob_sb.sem, 1)

                pool.wait_ge(plan.full_sem(("kwT", 1, 3)), plan.after(("kwT", 1, 3), i))
                pool.sem_inc(s_pass, 1)
                pool.memset(vx, 0.0)

                for h in range(NH):
                    normalise(h)

                pool.wait_ge(var_sb.sem, var_sb.at(i, 1))
                pool.tensor_tensor(rstd[:, :], ve[:, :], halves[:, 0:NT], ALU.pow).then_inc(rstd_sb.sem, 1)
                pool.wait_ge(x1_sb.sem, x1_sb.at(i, 1))
                pool.tensor_tensor(x1b[:, :, :], x1[:, :, :],
                                   rows[:, 3:4, :].to_broadcast([P, NT, C]), ALU.add
                                   ).then_inc(x1b_sb.sem, 1)

                def normalise_x(h):
                    pool.wait_ge(rden_sb.sem, rden_sb.at(i, NH + h + 1))
                    for q in range(NT):
                        p_ = pr[:, h % 3, T * q:T * q + T]
                        last = pool.tensor_tensor(p_, p_, rden[:, h % 2, q:q + 1].to_broadcast([P, T]),
                                                  ALU.mult)
                    last.then_inc(prob_sb.sem, 1)

                for h in range(NH):
                    normalise_x(h)
                pool.wait_ge(var_sb.sem, var_sb.at(i, 2))
                pool.tensor_tensor(rstd[:, :], ve[:, :], halves[:, 0:NT], ALU.pow).then_inc(rstd_sb.sem, 1)

        @block.scalar
        def _(act):
            act.wait_ge(s_absorb, 1)
            act.copy(w_q[:, 3, :], pst["S0"][0:QL, :]).then_inc(s_absorbed, 1)
            act.wait_ge(w_in, 16 * N_WEIGHTS)
            act.wait_ge(s_const, CONSTS)
            with act.Fori(0, NB) as i:
                def evacuate(name, dst, src, scale=None):
                    act.wait_ge(plan.full_sem(name), plan.after(name, i))
                    if scale is None:
                        ins = act.copy(dst, src)
                    else:
                        ins = act.activation(dst, src, ACT.Copy, scale=scale)
                    ins.then_inc(plan.free_sem(name), 1)
                    return ins

                evacuate("xT", xT[:, :, :], ps("xT")[:, :].rearrange("p (c t) -> p c t", c=NC))
                act.wait_ge(ctx_turned.sem, ctx_turned.at(i, 1))
                act.copy(cT[:, :, :], ps("ctxT")[:, :].rearrange("p (c t) -> p c t", c=NC)
                    ).then_inc(plan.free_sem("ctxT"), 1)
                evacuate("first", pa[:, :, :],
                         ps("first")[:, :].rearrange("p (t n) -> p t n", t=NT)[:, :, 0:PA])

                def nope(u):
                    rows_, n = unit_rows(u)
                    f = unit_fill(u, "n")
                    act.wait_ge(plan.full_sem(f), plan.after(f, i))
                    if UNITS[u][0] == "ks":
                        act.wait_ge(plan.full_sem(("kwT", 0, 3)), plan.after(("kwT", 0, 3), i))
                    act.copy(rows_[:, :, 0:HD],
                             ps(f)[0:n, :].rearrange("p (h d) -> p h d", h=NH)).then_inc(plan.free_sem(f), 1)

                nope(0)
                nope(1)
                act.wait_ge(gate_max.sem, gate_max.at(i, 1))
                act.activation(gl[:, 3:6], gl[:, 0:3], ACT.Exp, bias=gl[:, 6:7], scale=1.0 / T,
                               accum_out=gl[:, 7:8]).then_inc(gate_exp.sem, 1)
                act.wait_ge(gate_done.sem, gate_done.at(i, 1))
                for t in range(NT):
                    evacuate(("vw", t), vw[:, t, :], ps(("vw", t))[:, :], gate[:, 2:3])

                def key_turn(t, g):
                    f = ("kwT", t, g)
                    evacuate(f, kT[:, 4 * g:4 * g + 4, KEEP + P * t:KEEP + P * t + P],
                             ps(f)[0:QK, :].rearrange("p (h t) -> p h t", h=4))

                def query_turn(t, g):
                    f = ("qT", t, g)
                    evacuate(f, qT[:, 4 * g:4 * g + 4, P * t:P * t + P],
                             ps(f)[:, :].rearrange("p (h t) -> p h t", h=4))

                def absorbed(t):
                    f = ("q", t, "c")
                    evacuate(f, rq[:, t, :, QK:P], ps(f)[:, :].rearrange("p (h d) -> p h d", h=NH))

                key_turn(0, 0)
                key_turn(0, 2)
                nope(2)
                absorbed(0)
                key_turn(1, 0)
                key_turn(1, 2)
                nope(3)
                absorbed(1)
                for t in range(NT):
                    evacuate(("v1", t), v1[:, t, :], ps(("v1", t))[:, :], gate[:, 0:1])
                query_turn(0, 0)
                query_turn(0, 2)
                query_turn(1, 0)
                query_turn(1, 2)
                evacuate("vs", vs[:, :], ps("vs")[0:KEEP, :], gate[0:KEEP, 1:2])
                nope(4)
                evacuate(("ksT", 0), kT[:, 0:8, 0:KEEP],
                         ps(("ksT", 0))[0:QK, :].rearrange("p (h t) -> p h t", h=8))

                def exps(h):
                    act.wait_ge(score_sb.sem, score_sb.at(i, h + 1))
                    if h >= 3:
                        act.wait_ge(plan.full_sem(("pT", h - 3, 1)), plan.after(("pT", h - 3, 1), i))
                    for n, (half, off, width, m, q, br) in enumerate(SEG):
                        a = SEG_AT[n]
                        last = act.activation(pr[:, h % 3, a:a + width], sm[:, h % 2, a:a + width], ACT.Exp,
                                              bias=nmx[:, h % 2, n:n + 1], scale=ATT_SCALE,
                                              accum_out=den[:, h % 2, n:n + 1])
                    last.then_inc(exp_done.sem, 1)

                def turn_probs(h):
                    f = ("pT", h, 1)
                    if h >= 2:
                        act.wait_ge(pv_done.sem, pv_done.at(i, h - 1))
                    evacuate(f, pT[:, h % 2, 512:1024], ps(f)[:, :])

                def heads_out(name, g):
                    act.wait_ge(pv_done.sem, pv_done.at(i, 4 * g + 4 + (NH if name == "ox" else 0)))
                    act.copy(oT[:, g, :], ps((name, g))[:, 0:T]).then_inc(plan.free_sem((name, g)), 1)

                for h in range(NH + 3):
                    if h < NH:
                        exps(h)
                    if 2 <= h < NH + 2:
                        turn_probs(h - 2)
                    if h >= 3 and (h - 3) % 4 == 3:
                        heads_out("o", (h - 3) // 4)

                act.wait_ge(kx_part.sem, kx_part.at(i, 1))
                act.copy(split_k[:, :, 3:6, :], split_k[:, :, 0:3, :])
                act.copy(split_k[:, :, 6:8, :], split_k[:, :, 0:2, :]).then_inc(kx_sb.sem, 1)
                evacuate("x1T", x1T[:, :, :], ps("x1T")[:, :].rearrange("p (c t) -> p c t", c=NC))
                for part, (a, b) in enumerate(((1, 3), (4, 6), (7, 8))):
                    act.wait_ge(qx_part.sem, qx_part.at(i, part + 1))
                    act.copy(split_q[:, :, a:b, :],
                             split_q[:, :, a - 1:a, :].to_broadcast([P, NT * NH, b - a, XD])
                             ).then_inc(qx_sb.sem, 1)

                def split_turn(name, dst, t, g):
                    f = (name, t, g)
                    evacuate(f, dst[:, 8 * g:8 * g + 8, P * t:P * t + P],
                             ps(f)[:, :].bitcast(BF16).rearrange("p (h t) -> p h t", h=8))

                split_turn("kxT", kxT, 0, 1)
                split_turn("kxT", kxT, 1, 1)
                split_turn("qxT", qxT, 0, 1)
                split_turn("qxT", qxT, 1, 1)

                def exps_x(h):
                    act.wait_ge(score_sb.sem, score_sb.at(i, NH + h + 1))
                    if h >= 3:
                        act.wait_ge(plan.full_sem(("pxT", h - 3)), plan.after(("pxT", h - 3), i))
                    for q in range(NT):
                        last = act.activation(pr[:, h % 3, T * q:T * q + T], sm[:, h % 2, T * q:T * q + T],
                                              ACT.Exp, bias=nmx[:, h % 2, q:q + 1], scale=X_SCALE,
                                              accum_out=den[:, h % 2, q:q + 1])
                    last.then_inc(exp_done.sem, 1)

                def turn_probs_x(h):
                    if h % 2 == 0:
                        return
                    if h >= 2:
                        act.wait_ge(pv_done.sem, pv_done.at(i, NH + h - 1))
                    evacuate(("pxT", h), pT[:, h % 2, 0:512], ps(("pxT", h))[:, :])

                for h in range(NH + 3):
                    if h < NH:
                        exps_x(h)
                    if 2 <= h < NH + 2:
                        turn_probs_x(h - 2)
                    if h >= 3 and (h - 3) % 4 == 3:
                        heads_out("ox", (h - 3) // 4)

        @block.vector
        def _(dve):
            dve.memset(pst["T1"][:, :], 0.0).then_inc(s_wide, 1)
            prime(dve, [x_used.sem, m_used.sem])
            dve.wait_ge(w_in, 16 * N_WEIGHTS)
            dve.wait_ge(s_const, CONSTS)
            dve.tensor_copy(w_imp[:, :, 1:P], w_imp[:, :, 0:1].to_broadcast([P, NC, P - 1])
                            ).then_inc(s_wide, 1)
            with dve.Fori(0, NB) as i:
                c = Chain(s_dve, DVE_CHAIN, i)
                dve.wait_ge(plan.full_sem("imp"), plan.after("imp", i))
                dve.tensor_copy(srow[:, :], ps("imp")[:, 0:T]).then_inc(plan.free_sem("imp"), 1)

                dve.wait_ge(plan.free_sem("first"), plan.after("first", i))
                for t in range(NT):
                    dve.tensor_tensor_reduce(out=sq[:, 0:QL], in0=pa[:, t, 0:QL], in1=pa[:, t, 0:QL],
                                             scale=1.0, scalar=0.0, op0=ALU.mult, op1=ALU.add,
                                             accum_out=ss[:, t:t + 1]).then_inc(c.step(), 1)
                    dve.wait_ge(c.sem, c.value())
                    dve.tensor_tensor_reduce(out=sq[:, 0:KL], in0=pa[:, t, QL:QL + KL],
                                             in1=pa[:, t, QL:QL + KL],
                                             scale=1.0, scalar=0.0, op0=ALU.mult, op1=ALU.add,
                                             accum_out=ss[:, 2 + t:3 + t]).then_inc(c.step(), 1)
                    dve.wait_ge(c.sem, c.value())
                dve.tensor_scalar(ss[:, 0:2], ss[:, 0:2], 1.0 / QL, RMS_EPS, ALU.mult, ALU.add).then_inc(c.step(), 1)
                dve.tensor_scalar(ss[:, 2:4], ss[:, 2:4], 1.0 / KL, RMS_EPS, ALU.mult, ALU.add
                                  ).then_inc(sumsq.sem, 1)
                k0 = QL + KL
                xa, xb = pa[:, :, k0:k0 + HD], pa[:, :, k0 + HD:k0 + RP]
                cos, sin = cs[:, 0, :, :], cs[:, 1, :, :]
                for n, (v, f) in enumerate(((xa, cos), (xa, sin), (xb, sin), (xb, cos))):
                    dve.scalar_tensor_tensor(ktmp[:, n, :, :], v, 1.0 / NH, f, ALU.mult, ALU.mult).then_inc(c.step(), 1)
                dve.wait_ge(c.sem, c.value())
                dve.tensor_tensor(k1r[:, :, HD:2 * HD], ktmp[:, 0], ktmp[:, 2], ALU.subtract).then_inc(c.step(), 1)
                dve.tensor_tensor(k1r[:, :, 2 * HD:3 * HD], ktmp[:, 1], ktmp[:, 3], ALU.add).then_inc(c.step(), 1)
                dve.wait_ge(rms_sb.sem, rms_sb.at(i, 1))
                for t in range(NT):
                    dve.scalar_tensor_tensor(lat[:, t, :], pa[:, t, 0:QL], rs[:, t:t + 1], g_q[:, :],
                                             ALU.mult, ALU.mult).then_inc(c.step(), 1)
                    dve.scalar_tensor_tensor(k1r[:, t, 3 * HD:P], pa[:, t, QL:QL + KL],
                                             rs[:, 2 + t:3 + t], g_kv[:, :], ALU.mult, ALU.mult).then_inc(c.step(), 1)
                dve.wait_ge(c.sem, c.value())
                dve.sem_inc(lat_sb.sem, 1)

                def rope_products(u):
                    rows_, n = unit_rows(u)
                    t = UNITS[u][1]
                    for k, part in enumerate(("a", "b")):
                        f = unit_fill(u, part)
                        dve.wait_ge(plan.full_sem(f), plan.after(f, i))
                        src = ps(f)[0:n, :].rearrange("p (h d) -> p h d", h=NH)
                        for m in range(2):
                            table = cs[0:n, m if k == 0 else 1 - m, t:t + 1, :].to_broadcast([n, NH, HD])
                            dst = rt[0:n, 2 * k + m, :].rearrange("p (h d) -> p h d", h=NH)
                            if k == 0:
                                dve.wait_ge(rope_out.sem, rope_out.at(i, 2 * u - 1 + m if u else 0))
                            ins = dve.tensor_tensor(dst, src, table, ALU.mult)
                            if k == 1 and m == 0:
                                ins.then_inc(rope_in.sem, 1)
                            if m == 1:
                                ins.then_inc(plan.free_sem(f), 1)

                rope_products(0)

                dve.wait_ge(plan.full_sem("gate"), plan.after("gate", i))
                dve.tensor_copy(gl[:, 0:3], ps("gate")[:, 0:3]).then_inc(plan.free_sem("gate"), 1)
                dve.wait_ge(plan.free_sem("gate"), plan.after("gate", i))
                dve.tensor_reduce(gl[:, 6:7], gl[:, 0:3], AX, ALU.max).then_inc(c.step(), 1)
                dve.wait_ge(c.sem, c.value())
                dve.tensor_scalar(gl[:, 6:7], gl[:, 6:7], -1.0 / T, None, ALU.mult).then_inc(gate_max.sem, 1)

                dve.wait_ge(plan.full_sem("latT"), plan.after("latT", i))
                dve.tensor_copy(latT[0:QL, 0, :], ps("latT")[0:QL, 0:T])
                dve.tensor_copy(latT[:, 1, :], ps("latT")[:, T:2 * T]).then_inc(plan.free_sem("latT"), 1)
                dve.wait_ge(gate_exp.sem, gate_exp.at(i, 1))
                dve.reciprocal(gl[:, 6:7], gl[:, 7:8]).then_inc(c.step(), 1)
                dve.wait_ge(c.sem, c.value())
                dve.tensor_scalar(gate[:, 0:3], gl[:, 3:6], gl[:, 6:7], None, ALU.mult
                                  ).then_inc(gate_done.sem, 1)
                rope_products(1)

                def key_turn(t, g):
                    f = ("kwT", t, g)
                    dve.wait_ge(plan.full_sem(f), plan.after(f, i))
                    dve.tensor_copy(kT[:, 4 * g:4 * g + 4, KEEP + P * t:KEEP + P * t + P],
                                    ps(f)[0:QK, :].rearrange("p (h t) -> p h t", h=4)).then_inc(plan.free_sem(f), 1)

                def query_turn(t, g):
                    f = ("qT", t, g)
                    dve.wait_ge(plan.full_sem(f), plan.after(f, i))
                    dve.tensor_copy(qT[:, 4 * g:4 * g + 4, P * t:P * t + P],
                                    ps(f)[:, :].rearrange("p (h t) -> p h t", h=4)).then_inc(plan.free_sem(f), 1)

                key_turn(0, 1)
                key_turn(0, 3)
                rope_products(2)
                key_turn(1, 1)
                key_turn(1, 3)
                rope_products(3)

                dve.wait_ge(plan.free_sem("imp"), plan.after("imp", i))
                for t in range(NT):
                    dve.tensor_tensor(cmp1[:, t, 0:P], srow[:, P * t:P * t + P], ident[:, :], ALU.mult
                        ).then_inc(c.step(), 1)
                dve.wait_ge(c.sem, c.value())
                dve.tensor_reduce(scol[:, :], cmp1[:, :, 0:P], AX, ALU.add).then_inc(c.step(), 1)
                dve.wait_ge(c.sem, c.value())
                for t in range(NT):
                    dve.tensor_scalar(cmp1[:, t, :], srow[:, :], scol[:, t:t + 1], None, ALU.is_gt
                        ).then_inc(c.step(), 1)
                    dve.scalar_tensor_tensor(cmp2[:, t, :], srow[:, :], scol[:, t:t + 1], tie[:, t, :],
                                             ALU.is_equal, ALU.mult).then_inc(c.step(), 1)
                dve.wait_ge(c.sem, c.value())
                dve.tensor_tensor(cmp1[:, :, :], cmp1[:, :, :], cmp2[:, :, :], ALU.add).then_inc(c.step(), 1)
                dve.wait_ge(c.sem, c.value())
                dve.tensor_reduce(rank[:, :], cmp1[:, :, :], AX, ALU.add).then_inc(c.step(), 1)
                dve.wait_ge(c.sem, c.value())
                dve.tensor_scalar(sel[:, :], rank[:, :], float(KEEP), None, ALU.is_lt).then_inc(sel_sb.sem, 1)
                dve.wait_ge(plan.full_sem("pos"), plan.after("pos", i))
                dve.tensor_copy(pos[:, :], ps("pos")[:, 0:NT]).then_inc(plan.free_sem("pos"), 1)
                dve.wait_ge(plan.free_sem("pos"), plan.after("pos", i))
                for t in range(NT):
                    dve.tensor_scalar(pick[:, t, :], count[:, :], pos[:, t:t + 1], sel[:, t:t + 1],
                                      ALU.is_equal, ALU.mult).then_inc(c.step(), 1)
                dve.wait_ge(c.sem, c.value())
                dve.sem_inc(pick_sb.sem, 1)
                query_turn(0, 1)
                query_turn(0, 3)
                dve.wait_ge(plan.full_sem("xsel"), plan.after("xsel", i))
                dve.tensor_copy(xselT[:, :, :],
                                ps("xsel")[:, 0:NC * KEEP].rearrange("p (c k) -> p c k", c=NC)
                                    ).then_inc(plan.free_sem("xsel"), 1)
                query_turn(1, 1)
                query_turn(1, 3)
                rope_products(4)
                dve.wait_ge(plan.full_sem(("ksT", 1)), plan.after(("ksT", 1), i))
                dve.tensor_copy(kT[:, 8:16, 0:KEEP],
                                ps(("ksT", 1))[0:QK, :].rearrange("p (h t) -> p h t", h=8)
                                    ).then_inc(plan.free_sem(("ksT", 1)), 1)

                def scores(h):
                    if h >= 2:
                        dve.wait_ge(exp_done.sem, exp_done.at(i, h - 1))
                    for n, (half, off, width, m, q, br) in enumerate(SEG):
                        f = ("s", h, half)
                        if n in (0, 3):
                            dve.wait_ge(plan.full_sem(f), plan.after(f, i))
                            dve.sem_inc(s_pass, 1)
                        a = SEG_AT[n]
                        ins = dve.tensor_tensor_reduce(
                            out=sm[:, h % 2, a:a + width], in0=ps(f)[:, off:off + width],
                            in1=cmask[:, m:m + width], scale=1.0, scalar=LOW, op0=ALU.add, op1=ALU.max,
                            accum_out=mx[:, h % 2, n:n + 1])
                        if n in (2, 5):
                            ins.then_inc(plan.free_sem(f), 1)
                    dve.wait_ge(plan.free_sem(("s", h, 0)), plan.after(("s", h, 0), i))
                    dve.wait_ge(plan.free_sem(("s", h, 1)), plan.after(("s", h, 1), i))
                    dve.tensor_scalar(nmx[:, h % 2, :], mx[:, h % 2, :], -ATT_SCALE, None, ALU.mult
                                      ).then_inc(score_sb.sem, 1)

                def denominators(h, k, n):
                    dve.wait_ge(exp_done.sem, exp_done.at(i, k + 1))
                    if k >= 2:
                        dve.wait_ge(prob_sb.sem, prob_sb.at(i, k - 1))
                    dve.reciprocal(rden[:, h % 2, 0:n], den[:, h % 2, 0:n]).then_inc(rden_sb.sem, 1)

                def turn_probs(h):
                    f = ("pT", h, 0)
                    dve.wait_ge(plan.full_sem(f), plan.after(f, i))
                    if h >= 2:
                        dve.wait_ge(pv_done.sem, pv_done.at(i, h - 1))
                    dve.tensor_copy(pT[:, h % 2, 0:512], ps(f)[:, :]).then_inc(plan.free_sem(f), 1)

                for h in range(NH + 2):
                    if h < NH:
                        scores(h)
                    if 1 <= h < NH + 1:
                        denominators(h - 1, h - 1, 6)
                    if h >= 2:
                        turn_probs(h - 2)

                def layer_norm(k, f, base, out):
                    dve.wait_ge(plan.full_sem(f), plan.after(f, i))
                    ins = dve.tensor_tensor(res[:, :, :], ps(f)[:, :].rearrange("p (t c) -> p t c", t=NT),
                                            base[:, :, :], ALU.add)
                    ins.then_inc(plan.free_sem(f), 1)
                    dve.wait_ge(plan.free_sem(f), plan.after(f, i))
                    for t in range(NT):
                        dve.bn_stats(st[:, t, 0:6], res[:, t, :]).then_inc(c.step(), 1)
                    dve.wait_ge(c.sem, c.value())
                    dve.sem_inc(s_pass, 1)
                    for t in range(NT):
                        dve.bn_aggr(mv[:, t, :], st[:, t, 0:6]).then_inc(c.step(), 1)
                    dve.wait_ge(c.sem, c.value())
                    dve.tensor_scalar(ve[:, :], mv[:, :, 1:2].rearrange("p t o -> p (t o)"), LN_EPS, None,
                                      ALU.add).then_inc(var_sb.sem, 1)
                    dve.wait_ge(rstd_sb.sem, rstd_sb.at(i, k))
                    for t in range(NT):
                        dve.tensor_scalar(out(t), res[:, t, :], mv[:, t, 0:1], rstd[:, t:t + 1],
                                          ALU.subtract, ALU.mult).then_inc(c.step(), 1)
                    dve.wait_ge(c.sem, c.value())

                layer_norm(1, "proj", xin, lambda t: x1[:, t, :])
                dve.sem_inc(x_used.sem, 1)
                dve.sem_inc(x1_sb.sem, 1)

                dve.wait_ge(c_in.sem, c_in.at(i, 48))
                dve.tensor_scalar(fill, mrow[:, :], 1.0, -MASK_FILL / X_SCALE,
                                  ALU.subtract, ALU.mult).then_inc(c.step(), 1)
                dve.tensor_copy(mf[:, :], mcol[:, :]).then_inc(c.step(), 1)
                dve.wait_ge(c.sem, c.value())
                dve.sem_inc(m_used.sem, 1)

                def bias_row(k):
                    return rows[:, k:k + 1, :].to_broadcast([P, NT, C])

                def grouped(t):
                    return t[:, :, :].rearrange("p t (h d) -> p (t h) d", d=XD)

                dve.wait_ge(plan.full_sem("kx"), plan.after("kx", i))
                dve.tensor_tensor(k32[:, :, :], ps("kx")[:, :].rearrange("p (t c) -> p t c", t=NT),
                                  bias_row(1), ALU.add).then_inc(plan.free_sem("kx"), 1)
                dve.wait_ge(plan.free_sem("kx"), plan.after("kx", i))
                for t in range(NT):
                    dve.tensor_scalar(k32[:, t, :], k32[:, t, :], mf[:, t:t + 1], None, ALU.mult).then_inc(c.step(), 1)
                dve.wait_ge(c.sem, c.value())
                dve.tensor_copy(split_k[:, :, 0, :], grouped(k32)).then_inc(c.step(), 1)
                dve.wait_ge(c.sem, c.value())
                dve.tensor_tensor(grouped(rem), grouped(k32), split_k[:, :, 0, :], ALU.subtract).then_inc(c.step(), 1)
                dve.wait_ge(c.sem, c.value())
                dve.tensor_copy(split_k[:, :, 1, :], grouped(rem)).then_inc(c.step(), 1)
                dve.wait_ge(c.sem, c.value())
                dve.tensor_tensor(grouped(rem), grouped(rem), split_k[:, :, 1, :], ALU.subtract).then_inc(c.step(), 1)
                dve.wait_ge(c.sem, c.value())
                dve.tensor_copy(split_k[:, :, 2, :], grouped(rem)).then_inc(kx_part.sem, 1)
                dve.wait_ge(plan.full_sem("vx"), plan.after("vx", i))
                for t in range(NT):
                    ins = dve.tensor_tensor(vx[:, t, :, 0:XD],
                                            ps("vx")[:, C * t:C * t + C].rearrange("p (h d) -> p h d", d=XD),
                                            rows[:, 2, :].rearrange("p (h d) -> p h d", d=XD), ALU.add)
                ins.then_inc(plan.free_sem("vx"), 1)
                dve.wait_ge(plan.full_sem("qx"), plan.after("qx", i))
                dve.tensor_tensor(q32[:, :, :], ps("qx")[:, :].rearrange("p (t c) -> p t c", t=NT),
                                  bias_row(0), ALU.add).then_inc(plan.free_sem("qx"), 1)
                dve.wait_ge(kx_part.sem, kx_part.at(i, 1))
                dve.wait_ge(plan.free_sem("qx"), plan.after("qx", i))
                dve.tensor_copy(split_q[:, :, 0, :], grouped(q32)).then_inc(qx_part.sem, 1)
                dve.wait_ge(qx_part.sem, qx_part.at(i, 1))
                dve.tensor_tensor(grouped(rem), grouped(q32), split_q[:, :, 0, :], ALU.subtract).then_inc(c.step(), 1)
                dve.wait_ge(c.sem, c.value())
                dve.tensor_copy(split_q[:, :, 3, :], grouped(rem)).then_inc(qx_part.sem, 1)
                dve.wait_ge(qx_part.sem, qx_part.at(i, 2))
                dve.tensor_tensor(grouped(rem), grouped(rem), split_q[:, :, 3, :], ALU.subtract).then_inc(c.step(), 1)
                dve.wait_ge(c.sem, c.value())
                dve.tensor_copy(split_q[:, :, 6, :], grouped(rem)).then_inc(qx_part.sem, 1)

                def split_turn(name, dst, t, g):
                    f = (name, t, g)
                    dve.wait_ge(plan.full_sem(f), plan.after(f, i))
                    dve.tensor_copy(dst[:, 8 * g:8 * g + 8, P * t:P * t + P],
                                    ps(f)[:, :].bitcast(BF16).rearrange("p (h t) -> p h t", h=8)
                                        ).then_inc(plan.free_sem(f), 1)

                split_turn("kxT", kxT, 0, 0)
                split_turn("kxT", kxT, 1, 0)
                split_turn("qxT", qxT, 0, 0)
                split_turn("qxT", qxT, 1, 0)

                def scores_x(h):
                    dve.wait_ge(exp_done.sem, exp_done.at(i, NH + h - 1))
                    f = ("sx", h)
                    dve.wait_ge(plan.full_sem(f), plan.after(f, i))
                    dve.sem_inc(s_pass, 1)
                    for q in range(NT):
                        ins = dve.tensor_tensor_reduce(
                            out=sm[:, h % 2, T * q:T * q + T], in0=ps(f)[:, T * q:T * q + T],
                            in1=fill, scale=1.0, scalar=LOW, op0=ALU.add, op1=ALU.max,
                            accum_out=mx[:, h % 2, q:q + 1])
                    ins.then_inc(plan.free_sem(f), 1)
                    dve.wait_ge(plan.free_sem(f), plan.after(f, i))
                    dve.tensor_scalar(nmx[:, h % 2, 0:NT], mx[:, h % 2, 0:NT], -X_SCALE, None, ALU.mult
                                      ).then_inc(score_sb.sem, 1)

                def turn_probs_x(h):
                    if h % 2:
                        return
                    f = ("pxT", h)
                    dve.wait_ge(plan.full_sem(f), plan.after(f, i))
                    if h >= 2:
                        dve.wait_ge(pv_done.sem, pv_done.at(i, NH + h - 1))
                    dve.tensor_copy(pT[:, h % 2, 0:512], ps(f)[:, :]).then_inc(plan.free_sem(f), 1)

                for h in range(NH + 2):
                    if h < NH:
                        scores_x(h)
                    if 1 <= h < NH + 1:
                        denominators(h - 1, NH + h - 1, NT)
                    if h >= 2:
                        turn_probs_x(h - 2)
                dve.wait_ge(x1b_sb.sem, x1b_sb.at(i, 1))
                layer_norm(2, "projx", x1b, lambda t: x2[:, bass.ds(i * NT + t, 1), :].rearrange(
                    "p o c -> p (o c)"))
                c.close()

        @block.tensor
        def _(pe):
            prime(pe, [*plan.full.values(), *plan.free.values()])

            def mm(out, lhsT, rhs, start=True, stop=True):
                return pe.matmul(out, lhsT, rhs, start=start, stop=stop)

            pe.wait_ge(w_in, 16 * N_WEIGHTS)
            stage = pr[0:HD, :, :].rearrange("p a b -> p (a b)")
            for h in range(NH):
                last = mm(pst["S0"][0:QL, HD * h:HD * h + HD], stage[:, QL * h:QL * h + QL],
                          stage[:, NH * QL + HD * h:NH * QL + HD * h + HD])
            last.then_inc(s_absorb, 1)
            pe.wait_ge(s_absorbed, 1)
            pe.wait_ge(s_wide, 2)
            pe.wait_ge(s_const, CONSTS)
            with pe.Fori(0, NB) as i:
                def transpose4(name, pieces, idn):
                    pe.wait_ge(plan.free_sem(name), plan.before(name, i))
                    for out, in_ in pieces:
                        last = pe.transpose(out, in_, idn)
                    if plan.bank(name) != "O":
                        last.then_inc(plan.full_sem(name), 1)
                    return last

                def product(name, m, n, lhs, rhs):
                    pe.wait_ge(plan.free_sem(name), plan.before(name, i))
                    ks = len(lhs)
                    for k in range(ks):
                        last = mm(ps(name)[0:m, 0:n], lhs[k], rhs[k], k == 0, k == ks - 1)
                    last.then_inc(plan.full_sem(name), 1)

                def tok(xt, t):
                    return [xt[:, c, P * t:P * t + P] for c in range(NC)]

                pe.wait_ge(x_in.sem, x_in.at(i, 16))
                transpose4("xT", [(ps("xT")[:, T * c + P * t:T * c + P * t + P], xin[:, t, P * c:P * c + P])
                                  for c in range(NC) for t in range(NT)], ident[:, :])
                pe.wait_ge(c_in.sem, c_in.at(i, 48))
                last = transpose4("ctxT", [(ps("ctxT")[:, T * c + P * t:T * c + P * t + P], cin[:, t, P * c:P * c + P])
                                    for c in range(NC) for t in range(NT)], ident[:, :])
                last.then_inc(ctx_turned.sem, 1)
                pe.wait_ge(plan.free_sem("xT"), plan.after("xT", i))
                pe.wait_ge(plan.free_sem("first"), plan.before("first", i))
                for t in range(NT):
                    for c in range(NC):
                        last = mm(ps("first")[:, T * t:T * t + PA], xT[:, c, P * t:P * t + P], w_first[:, c, :],
                                  c == 0, c == NC - 1)
                last.then_inc(plan.full_sem("first"), 1)
                product("imp", P, T, [w_imp[:, c, :] for c in range(NC)], [xT[:, c, :] for c in range(NC)])
                for t in range(NT):
                    for s, part in enumerate(("n", "a", "b")):
                        product(("kw", t, part), P, HW, tok(xT, t), [w_kw[:, c, s, :] for c in range(NC)])
                pe.wait_ge(plan.free_sem("first"), plan.after("first", i))
                product("gate", P, 3, [ones[:, :]] * NT, [pa[:, t, PA - 3:PA] for t in range(NT)])
                pe.wait_ge(lat_sb.sem, lat_sb.at(i, 1))
                pe.wait_ge(plan.free_sem("latT"), plan.before("latT", i))
                for t in range(NT):
                    pe.transpose(ps("latT")[0:QL, P * t:P * t + P], lat[:, t, :], ident[:, :])
                for t in range(NT):
                    last = pe.transpose(ps("latT")[:, T + P * t:T + P * t + P], k1r[:, t, :], ident[:, :])
                last.then_inc(plan.full_sem("latT"), 1)
                for t in range(NT):
                    product(("vw", t), P, HW, tok(xT, t), [w_vw[:, c, :] for c in range(NC)])

                def turn_rows(u):
                    kind, t = UNITS[u]
                    rows_, n = unit_rows(u)
                    pe.wait_ge(plan.free_sem(unit_fill(u, "n")), plan.after(unit_fill(u, "n"), i))
                    if kind == "q":
                        pe.wait_ge(plan.free_sem(unit_fill(u, "c")), plan.after(unit_fill(u, "c"), i))
                    pe.wait_ge(rope_out.sem, rope_out.at(i, 2 * u + 2))
                    width = P if kind == "q" else QK
                    per = 8 if kind == "ks" else 4
                    for g in range(NH // per):
                        f = ("ksT", g) if kind == "ks" else (kind + "T", t, g)
                        pe.wait_ge(plan.free_sem(f), plan.before(f, i))
                        if kind == "ks":
                            pe.sem_inc(s_pass, 1)
                        for k in range(per):
                            last = pe.transpose(ps(f)[0:width, n * k:n * k + n], rows_[:, per * g + k, 0:width],
                                                ident[0:n, 0:n])
                        last.then_inc(plan.full_sem(f), 1)

                def queries(t):
                    for s, part in enumerate(("n", "a", "b", "c")):
                        product(("q", t, part), P, HW, [latT[0:QL, 0, P * t:P * t + P]], [w_q[:, s, :]])

                turn_rows(0)
                pe.wait_ge(plan.free_sem("latT"), plan.after("latT", i))
                queries(0)
                turn_rows(1)
                queries(1)
                for t in range(NT):
                    product(("v1", t), P, HW, [latT[QK:P, 1, P * t:P * t + P]], [w_dv[QK:P, :]])
                pe.wait_ge(sel_sb.sem, sel_sb.at(i, 1))
                pe.wait_ge(plan.free_sem("pos"), plan.before("pos", i))
                mm(ps("pos")[:, 0:1], upper[:, :], sel[:, 0:1])
                mm(ps("pos")[:, 1:2], ones[:, :], sel[:, 0:1], True, False)
                mm(ps("pos")[:, 1:2], upper[:, :], sel[:, 1:2], False, True).then_inc(plan.full_sem("pos"), 1)
                turn_rows(2)
                pe.wait_ge(pick_sb.sem, pick_sb.at(i, 1))
                pe.wait_ge(plan.free_sem("xsel"), plan.before("xsel", i))
                for c in range(NC):
                    for t in range(NT):
                        last = mm(ps("xsel")[:, KEEP * c:KEEP * c + KEEP], xin[:, t, P * c:P * c + P],
                                  pick[:, t, :], t == 0, t == NT - 1)
                last.then_inc(plan.full_sem("xsel"), 1)
                turn_rows(3)
                pe.wait_ge(plan.free_sem("xsel"), plan.after("xsel", i))
                chosen = [xselT[:, c, :] for c in range(NC)]
                product("vs", KEEP, HW, chosen, [w_vs[:, c, :] for c in range(NC)])
                for s, part in enumerate(("n", "a", "b")):
                    product(("ks", part), KEEP, HW, chosen, [w_ks[:, c, s, :] for c in range(NC)])
                turn_rows(4)

                def scores(h):
                    q0, q1 = (qT[:, h, P * q:P * q + P] for q in range(NT))
                    A, B = ps(("s", h, 0)), ps(("s", h, 1))
                    pe.wait_ge(plan.free_sem(("s", h, 0)), plan.before(("s", h, 0), i))
                    mm(A[:, 0:P], q0, latT[:, 1, 0:P])
                    mm(A[:, P:P + KEEP + T], q1[0:QK], kT[:, h, :]).then_inc(plan.full_sem(("s", h, 0)), 1)
                    pe.wait_ge(plan.free_sem(("s", h, 1)), plan.before(("s", h, 1), i))
                    mm(B[:, 0:KEEP + P], q0[0:QK], kT[:, h, 0:KEEP + P])
                    mm(B[:, KEEP + P:KEEP + P + T], q1, latT[:, 1, :]).then_inc(plan.full_sem(("s", h, 1)), 1)

                def turn_probs(h):
                    p = pr[:, h % 3, :]
                    pe.wait_ge(prob_sb.sem, prob_sb.at(i, h + 1))
                    for half, blocks in enumerate((
                            ((0, 0), (640, P), (768, 2 * P), (320, 3 * P)),
                            ((512, 0), (192, P), (448, 2 * P), (128, 3 * P)))):
                        f = ("pT", h, half)
                        pe.wait_ge(plan.free_sem(f), plan.before(f, i))
                        for n, (a, dst) in enumerate(blocks):
                            width = KEEP if half == 1 and n >= 2 else P
                            last = pe.transpose(ps(f)[0:width, dst:dst + P], p[:, a:a + width], ident[:, :])
                        last.then_inc(plan.full_sem(f), 1)

                def values(h):
                    j, g = h % 4, h // 4
                    if j == 0:
                        pe.wait_ge(plan.free_sem(("o", g)), plan.before(("o", g), i))
                    o = ps(("o", g))[HD * j:HD * j + HD, 0:T]
                    col = slice(HD * h, HD * h + HD)
                    q = pT[:, h % 2, :]
                    pe.wait_ge(plan.free_sem(("pT", h, 0)), plan.after(("pT", h, 0), i))
                    pe.wait_ge(plan.free_sem(("pT", h, 1)), plan.after(("pT", h, 1), i))
                    mm(o, v1[:, 0, col], q[:, 0:T], True, False)
                    mm(o[:, P:T], v1[:, 1, col], q[:, T:T + P], False, False)
                    mm(o[:, P:T], vw[:, 1, col], q[:, T + P:2 * T], False, False)
                    mm(o, vw[:, 0, col], q[:, 2 * T:3 * T], False, False)
                    last = mm(o, vs[:, col], q[0:KEEP, 3 * T:4 * T], False, True)
                    last.then_inc(pv_done.sem, 1)

                pe.wait_ge(plan.free_sem(("qT", 1, 3)), plan.after(("qT", 1, 3), i))
                pe.wait_ge(plan.free_sem(("qT", 1, 2)), plan.after(("qT", 1, 2), i))
                pe.wait_ge(plan.free_sem(("ksT", 1)), plan.after(("ksT", 1), i))
                pe.wait_ge(plan.free_sem(("ksT", 0)), plan.after(("ksT", 0), i))
                for h in range(NH + 3):
                    if h < NH:
                        scores(h)
                    if 2 <= h < NH + 2:
                        turn_probs(h - 2)
                    if h >= 3:
                        values(h - 3)

                def project(name, wo):
                    pe.wait_ge(plan.free_sem(name), plan.before(name, i))
                    last_heads = ("o" if name == "proj" else "ox", 3)
                    pe.wait_ge(plan.free_sem(last_heads), plan.after(last_heads, i))
                    for t in range(NT):
                        for g in range(4):
                            last = mm(ps(name)[:, T * t:T * t + C], oT[:, g, P * t:P * t + P], wo[:, g, :],
                                      g == 0, g == 3)
                    last.then_inc(plan.full_sem(name), 1)

                project("proj", w_proj)

                def linear(name, src, wt):
                    pe.wait_ge(plan.free_sem(name), plan.before(name, i))
                    for t in range(NT):
                        for c in range(NC):
                            last = mm(ps(name)[:, T * t:T * t + C], src[:, c, P * t:P * t + P], wt[:, c, :],
                                      c == 0, c == NC - 1)
                    last.then_inc(plan.full_sem(name), 1)

                linear("kx", cT, wx_k)
                linear("vx", cT, wx_v)
                pe.wait_ge(x1_sb.sem, x1_sb.at(i, 1))
                transpose4("x1T", [(ps("x1T")[:, T * c + P * t:T * c + P * t + P], x1[:, t, P * c:P * c + P])
                                   for c in range(NC) for t in range(NT)], ident[:, :])
                pe.wait_ge(plan.free_sem("x1T"), plan.after("x1T", i))
                linear("qx", x1T, wx_q)

                def turn_split(name, src):
                    for t in range(NT):
                        for g in range(2):
                            f = (name, t, g)
                            o = ps(f)[:, :].bitcast(BF16)
                            transpose4(f, [(o[:, P * k:P * k + P],
                                            src[:, NH * t + 8 * g + k, :, :].rearrange("p s d -> p (s d)"))
                                           for k in range(8)], identb[:, :])

                pe.wait_ge(kx_sb.sem, kx_sb.at(i, 1))
                turn_split("kxT", split_k)
                pe.wait_ge(qx_sb.sem, qx_sb.at(i, 3))
                turn_split("qxT", split_q)
                pe.wait_ge(plan.free_sem(("qxT", 1, 0)), plan.after(("qxT", 1, 0), i))
                pe.wait_ge(plan.free_sem(("qxT", 1, 1)), plan.after(("qxT", 1, 1), i))

                def scores_x(h):
                    f = ("sx", h)
                    pe.wait_ge(plan.free_sem(f), plan.before(f, i))
                    for q in range(NT):
                        last = mm(ps(f)[:, T * q:T * q + T], qxT[:, h, P * q:P * q + P], kxT[:, h, :])
                    last.then_inc(plan.full_sem(f), 1)

                def turn_probs_x(h):
                    pe.wait_ge(prob_sb.sem, prob_sb.at(i, NH + h + 1))
                    transpose4(("pxT", h), [(ps(("pxT", h))[:, T * k + P * q:T * k + P * q + P],
                                             pr[:, h % 3, T * q + P * k:T * q + P * k + P])
                                            for k in range(NT) for q in range(NT)], ident[:, :])

                def values_x(h):
                    j, g = h % 4, h // 4
                    if j == 0:
                        pe.wait_ge(plan.free_sem(("ox", g)), plan.before(("ox", g), i))
                    o = ps(("ox", g))[HD * j:HD * j + HD, 0:T]
                    pe.wait_ge(plan.free_sem(("pxT", h)), plan.after(("pxT", h), i))
                    for k in range(NT):
                        last = mm(o, vx[:, k, h, :], pT[:, h % 2, T * k:T * k + T], k == 0, k == NT - 1)
                    last.then_inc(pv_done.sem, 1)

                for h in range(NH + 3):
                    if h < NH:
                        scores_x(h)
                    if 2 <= h < NH + 2:
                        turn_probs_x(h - 2)
                    if h >= 3:
                        values_x(h - 3)
                project("projx", wx_o)


def expert_block(nc, x2, w, out):
    ctx = ExitStack()
    with ctx:
        def sb(name, shape, dt=F32):
            return ctx.enter_context(nc.sbuf_tensor(name, shape, dt))

        def sem(name):
            return ctx.enter_context(nc.semaphore(name))

        BANKS = ("H0", "H1", "H2", "H3", "Y0", "Y1", "Y2", "Y3")
        pst = {b: ctx.enter_context(nc.psum_tensor(f"ps_{b}", [P, 512], F32)) for b in BANKS}
        STEPS = 2 * NCH
        TT = CH // P

        pre = BankPlan({b: sem(f"pre_full_{b}") for b in BANKS}, {b: sem(f"pre_free_{b}") for b in BANKS})
        for j in range(NCH):
            for c in range(NC):
                pre.add(("x2T", j, c), f"H{(2 * j + c) % 4}")
        pre.add("route", "Y0")
        for j in range(4):
            pre.add(("rT", j), f"H{j}")
        for j in range(TILES // 2):
            pre.add(("b2", j), f"Y{j % 4}")
        plan = BankPlan({b: sem(f"exp_full_{b}") for b in BANKS}, {b: sem(f"exp_free_{b}") for b in BANKS})
        for s in range(STEPS):
            for ht in range(NHT):
                plan.add(("h", s, ht), f"H{ht % 4}")
            for tt in range(TT):
                plan.add(("y", s, tt), f"Y{tt}")

        x_hi = sb("x_hi", [P, NC, NTOK], F32R)
        x_lo = sb("x_lo", [P, NC, NTOK], F32R)
        w_raw = sb("w_raw", [P, 4, 1024])
        w_hi = sb("w_hi", [P, 2, 4, 1024], F32R)
        w_lo = sb("w_lo", [P, 2, 4, 1024], F32R)
        h_sb = sb("h_sb", [P, 4, CH])
        h_hi = sb("h_hi", [P, 2, NHT, CH], F32R)
        h_lo = sb("h_lo", [P, 2, NHT, CH], F32R)
        ident = sb("ident2", [P, P])
        r_raw = sb("r_raw", [P, NC, NE])
        r_hi = sb("r_hi", [P, NC, NE], F32R)
        r_lo = sb("r_lo", [P, NC, NE], F32R)
        b_r = sb("b_r", [P, NE])
        b1 = sb("b1_sb", [P, NE, NHT])
        b1c = sb("b1_now", [P, 2, NHT])
        b2 = sb("b2_sb", [NE, C])
        lower8 = sb("lower8", [P, NE, NE])
        rt = sb("route_t", [P, NE, TILES])
        rc = sb("route_now", [P, 2, TILES])
        half = sb("half2", [P, TILES])
        small = sb("small", [P, 6, TILES * NE])
        big = [h_sb[:, 2 * k:2 * k + 2, :].rearrange("p a b -> p (a b)") for k in range(2)]
        rT = h_sb[0:NE, :, :].rearrange("p a b -> p (a b)")
        st = sb("st2", [P, TILES, 6])
        mv = sb("mv2", [P, TILES, 2])
        ve = sb("ve2", [P, TILES])
        rstd = sb("rstd2", [P, TILES])

        s_in = sem("small_in")
        s_raw0 = sem("raw0_in")
        s_const = sem("consts2")
        s_hi = sem("x_hi_done")
        s_dve = sem("dve_chain2")
        s_exp = sem("route_exp")
        s_exp_in = sem("route_exp_in")
        s_router = sem("router_split")
        s_rt = sem("route_done")
        s_split0_hi, s_split0 = sem("split0_hi"), sem("split0")
        s_var, s_rstd, s_out_sb, s_out = sem("var2"), sem("rstd2_done"), sem("out_sb"), sem("out_dma")
        raw_in = Signal(sem("raw_in"), 64)
        w_hi_sb = Signal(sem("w_hi_sb"), 8)
        w_split = Signal(sem("w_split"), 8, PRIMED)
        now_sb = Signal(sem("now_sb"), 1)
        hi_sb = Signal(sem("hi_sb"), STEPS * NHT)
        lo_sb = Signal(sem("lo_sb"), STEPS * NHT, PRIMED)

        w1_v = w["W1"].rearrange("e (c p) h -> e p c h", p=P)
        w2_v = w["W2"].rearrange("e (t p) d -> e p t d", p=P)

        def turns(eng, body):
            with eng.Fori(0, NE // 2 - 1) as i:
                body(i, False)
            body(NE // 2 - 1, True)

        block = ctx.enter_context(nc.Block())

        @block.sync
        def _(sp):
            sp.dma_start(r_raw[:, :, :], w["Wr"].rearrange("(c p) e -> p c e", p=P)).then_inc(s_in, 16)
            sp.dma_start(b_r[:, :], w["br"].partition_broadcast(P)).then_inc(s_in, 16)
            sp.dma_start(b1[:, :, :], w["b1"]).then_inc(s_in, 16)
            sp.dma_start(b2[:, :], w["b2"]).then_inc(s_in, 16)

            def load(e, sem_):
                sp.dma_start(w_raw[:, 0:2, :], w1_v[e]).then_inc(sem_, 16)
                sp.dma_start(w_raw[:, 2:4, :].rearrange("p a (b d) -> p (a b) d", d=C), w2_v[e]
                             ).then_inc(sem_, 16)

            load(0, s_raw0)
            sp.wait_ge(s_split0, 4)

            def turn(i, last):
                sp.wait_ge(w_split.sem, w_split.at(i, 0))
                load(i * 2 + 1, raw_in.sem)
                if not last:
                    sp.wait_ge(w_split.sem, w_split.at(i, 4))
                    load(i * 2 + 2, raw_in.sem)

            turns(sp, turn)
            for q in range(4):
                sp.wait_ge(s_out_sb, q + 1)
                out_v = out.rearrange("b t c -> (b t) c").rearrange("(n p) c -> p n c", p=P)
                sp.dma_start(out_v[:, 4 * q:4 * q + 4, :],
                             x2[:, 4 * q:4 * q + 4, :]).then_inc(s_out, 16)
            sp.wait_ge(s_out, 64)

        @block.gpsimd
        def _(pool):
            prime(pool, [w_split.sem, lo_sb.sem])
            c = Chain(s_const)
            pool.memset(lower8[:, :, :], 1.0).then_inc(c.step(), 1)
            pool.memset(half[:, :], -0.5).then_inc(c.step(), 1)
            pool.memset(ident[:, :], 1.0).then_inc(c.step(), 1)
            pool.wait_ge(c.sem, c.value())
            pool.affine_select(out=ident[:, :], in_=ident[:, :], compare_op=ALU.is_equal, fill=0.0,
                               base=0, pattern=[[-1, P]], channel_multiplier=1).then_inc(c.step(), 1)
            pool.affine_select(out=lower8[:, :, :], in_=lower8[:, :, :], compare_op=ALU.is_gt, fill=0.0,
                               base=0, pattern=[[1, NE], [-1, NE]], channel_multiplier=0).then_inc(c.step(), 1)
            for piece in range(4):
                pool.wait_ge(s_split0_hi, piece + 1)
                pool.tensor_tensor(w_lo[:, 0, piece, :], w_raw[:, piece, :],
                                   w_hi[:, 0, piece, :].bitcast(F32), ALU.subtract).then_inc(s_split0, 1)

            def turn(i, last):
                for s in range(STEPS):
                    for ht in range(NHT):
                        pool.wait_ge(hi_sb.sem, hi_sb.at(i, NHT * s + ht + 1))
                        pool.tensor_tensor(h_lo[:, s % 2, ht, :], h_sb[:, ht % 4, :],
                                           h_hi[:, s % 2, ht, :].bitcast(F32), ALU.subtract
                                           ).then_inc(lo_sb.sem, 1)
                    if last and s >= NCH:
                        continue
                    pool.wait_ge(w_hi_sb.sem, w_hi_sb.at(i, s + 1))
                    nxt = 1 - s // NCH
                    pool.tensor_tensor(w_lo[:, nxt, s % 4, :], w_raw[:, s % 4, :],
                                       w_hi[:, nxt, s % 4, :].bitcast(F32), ALU.subtract
                                       ).then_inc(w_split.sem, 1)

            turns(pool, turn)
            pool.wait_ge(s_var, 1)
            pool.tensor_tensor(rstd[:, :], ve[:, :], half[:, :], ALU.pow).then_inc(s_rstd, 1)

        @block.scalar
        def _(act):
            for j in range(NCH):
                for c in range(NC):
                    f = ("x2T", j, c)
                    act.wait_ge(pre.full_sem(f), pre.after(f, 0))
                    act.copy(x_hi[:, c, CH * j:CH * j + CH], pst[pre.bank(f)][:, :]).then_inc(s_hi, 1)
            act.wait_ge(s_exp_in, 1)
            act.activation(small[:, 2, :], small[:, 1, :], ACT.Exp).then_inc(s_exp, 1)
            for j in range(4):
                f = ("rT", j)
                act.wait_ge(pre.full_sem(f), pre.after(f, 0))
                act.copy(rT[:, CH * j:CH * j + CH], pst[pre.bank(f)][0:NE, :]).then_inc(pre.free_sem(f), 1)

            def turn(i, last):
                act.wait_ge(now_sb.sem, now_sb.at(i, 1))
                for s in range(STEPS):
                    for ht in range(NHT):
                        f = ("h", s, ht)
                        n = NHT * s + ht
                        act.wait_ge(plan.full_sem(f), plan.after(f, i))
                        if n >= 4:
                            act.wait_ge(lo_sb.sem, lo_sb.at(i, n - 3))
                        else:
                            act.wait_ge(lo_sb.sem, lo_sb.at(i, 0))
                        ins = act.activation(h_sb[:, ht % 4, :], pst[plan.bank(f)][:, :], ACT.Relu,
                                             bias=b1c[:, s // NCH, ht:ht + 1])
                        ins.then_inc(plan.free_sem(f), 1)

            turns(act, turn)

        @block.vector
        def _(dve):
            c = Chain(s_dve)
            dve.wait_ge(s_in, 64)
            dve.tensor_copy(r_hi[:, :, :], r_raw[:, :, :]).then_inc(c.step(), 1)
            dve.wait_ge(c.sem, c.value())
            dve.tensor_tensor(r_lo[:, :, :], r_raw[:, :, :], r_hi[:, :, :].bitcast(F32), ALU.subtract
                              ).then_inc(s_router, 1)
            for j in range(NCH):
                for cc in range(NC):
                    f = ("x2T", j, cc)
                    dve.wait_ge(s_hi, 2 * j + cc + 1)
                    x_h = x_hi[:, cc, CH * j:CH * j + CH]
                    dve.tensor_tensor(x_lo[:, cc, CH * j:CH * j + CH], pst[pre.bank(f)][:, :],
                                      x_h.bitcast(F32), ALU.subtract).then_inc(pre.free_sem(f), 1)
            dve.wait_ge(s_raw0, 32)
            for piece in range(4):
                dve.tensor_copy(w_hi[:, 0, piece, :], w_raw[:, piece, :]).then_inc(s_split0_hi, 1)

            def sm(k):
                return small[:, k, :].rearrange("p (t e) -> p t e", e=NE)

            def pair(k, a):
                return sm(k)[:, :, :].unsqueeze(3 if a else 2).to_broadcast([P, TILES, NE, NE])

            dve.wait_ge(pre.full_sem("route"), pre.after("route", 0))
            ins = dve.tensor_tensor(sm(0), pst["Y0"][:, 0:TILES * NE].rearrange("p (t e) -> p t e", e=NE),
                                    b_r[:, :].unsqueeze(1).to_broadcast([P, TILES, NE]), ALU.add)
            ins.then_inc(pre.free_sem("route"), 1)
            dve.wait_ge(pre.free_sem("route"), pre.after("route", 0))
            v = [b.rearrange("p (t e f) -> p t e f", e=NE, f=NE) for b in big]
            dve.wait_ge(s_const, 5)
            dve.tensor_tensor(v[0], pair(0, False), pair(0, True), ALU.is_gt).then_inc(c.step(), 1)
            dve.tensor_tensor(v[1], pair(0, False), pair(0, True), ALU.is_equal).then_inc(c.step(), 1)
            dve.wait_ge(c.sem, c.value())
            dve.tensor_tensor(v[1], v[1], lower8[:, :, :].unsqueeze(1).to_broadcast([P, TILES, NE, NE]),
                              ALU.mult).then_inc(c.step(), 1)
            dve.wait_ge(c.sem, c.value())
            dve.tensor_tensor(v[0], v[0], v[1], ALU.add).then_inc(c.step(), 1)
            dve.wait_ge(c.sem, c.value())
            dve.tensor_reduce(small[:, 3, :], v[0].rearrange("p t e f -> p (t e) f"), AX, ALU.add).then_inc(c.step(), 1)
            dve.wait_ge(c.sem, c.value())
            dve.scalar_tensor_tensor(small[:, 4, :], small[:, 3, :], 2.0, small[:, 0, :],
                                     ALU.is_lt, ALU.mult).then_inc(c.step(), 1)
            dve.wait_ge(c.sem, c.value())
            dve.tensor_reduce(small[:, 5, 0:TILES], sm(4), AX, ALU.max).then_inc(c.step(), 1)
            dve.wait_ge(c.sem, c.value())
            dve.tensor_tensor(sm(1), sm(4), small[:, 5, 0:TILES].unsqueeze(2).to_broadcast([P, TILES, NE]),
                              ALU.subtract).then_inc(s_exp_in, 1)
            dve.wait_ge(s_exp, 1)
            dve.tensor_reduce(small[:, 5, 0:TILES], sm(2), AX, ALU.add).then_inc(c.step(), 1)
            dve.wait_ge(c.sem, c.value())
            dve.reciprocal(small[:, 5, TILES:2 * TILES], small[:, 5, 0:TILES]).then_inc(c.step(), 1)
            dve.wait_ge(c.sem, c.value())
            dve.tensor_tensor(sm(0), sm(2),
                              small[:, 5, TILES:2 * TILES].unsqueeze(2).to_broadcast([P, TILES, NE]),
                              ALU.mult).then_inc(c.step(), 1)
            dve.wait_ge(c.sem, c.value())
            dve.tensor_copy(rt[:, :, :], small[:, 0, :].rearrange("p (t e) -> p e t", e=NE)
                            ).then_inc(s_rt, 1)
            for j in range(TILES // 2):
                f = ("b2", j)
                dve.wait_ge(pre.full_sem(f), pre.after(f, 0))
                dve.tensor_tensor(
        x2[:, 2 * j:2 * j + 2, :], x2[:, 2 * j:2 * j + 2, :],
        pst[pre.bank(f)][:, :].rearrange("p (t c) -> p t c", t=2), ALU.add).then_inc(pre.free_sem(f), 1)
            dve.wait_ge(pre.free_sem(("b2", TILES // 2 - 1)), pre.after(("b2", TILES // 2 - 1), 0))
            dve.wait_ge(s_rt, 1)

            def turn(i, last):
                dve.wait_ge(plan.free["H3"], plan.turns("H3", i))
                dve.wait_ge(plan.free["Y3"], plan.turns("Y3", i))
                k = i * 2 if last else bass.ds(i * 2, 2)
                two = slice(k, k + 2) if last else k
                dve.tensor_copy(rc[:, :, :], rt[:, two, :])
                dve.tensor_copy(b1c[:, :, :], b1[:, two, :]).then_inc(now_sb.sem, 1)
                dve.wait_ge(now_sb.sem, now_sb.at(i, 1))

                def sums(s):
                    for tt in range(TT):
                        f = ("y", s, tt)
                        tile = TT * (s % NCH) + tt
                        dve.wait_ge(plan.full_sem(f), plan.after(f, i))
                        dve.scalar_tensor_tensor(
               x2[:, tile, :], pst[plan.bank(f)][:, 0:C], rc[:, s // NCH, tile:tile + 1],
               x2[:, tile, :], ALU.mult, ALU.add).then_inc(plan.free_sem(f), 1)

                for s in range(STEPS):
                    if s >= 2:
                        dve.wait_ge(plan.full_sem(("y", s - 2, TT - 1)), plan.after(("y", s - 2, TT - 1), i))
                    else:
                        dve.wait_ge(plan.full["Y3"], plan.turns("Y3", i))
                    for ht in range(NHT):
                        dve.wait_ge(plan.free_sem(("h", s, ht)), plan.after(("h", s, ht), i))
                        dve.tensor_copy(h_hi[:, s % 2, ht, :], h_sb[:, ht % 4, :]).then_inc(hi_sb.sem, 1)
                    if s:
                        sums(s - 1)
                    if last and s >= NCH:
                        continue
                    nxt = 1 - s // NCH
                    dve.wait_ge(raw_in.sem, raw_in.at(i, 32 * (s // NCH + 1)))
                    if s >= NCH:
                        dve.wait_ge(plan.full_sem(("y", NCH - 1, TT - 1)), plan.after(("y", NCH - 1, TT - 1), i))
                    dve.tensor_copy(w_hi[:, nxt, s % 4, :], w_raw[:, s % 4, :]).then_inc(w_hi_sb.sem, 1)
                sums(STEPS - 1)

            turns(dve, turn)

            dve.wait_ge(plan.free["Y3"], plan.turns("Y3", NE // 2))
            for t in range(TILES):
                dve.bn_stats(st[:, t, :], x2[:, t, :]).then_inc(c.step(), 1)
            dve.wait_ge(c.sem, c.value())
            for t in range(TILES):
                dve.bn_aggr(mv[:, t, :], st[:, t, :]).then_inc(c.step(), 1)
            dve.wait_ge(c.sem, c.value())
            dve.tensor_scalar(ve[:, :], mv[:, :, 1:2].rearrange("p t o -> p (t o)"), LN_EPS, None, ALU.add
                              ).then_inc(s_var, 1)
            dve.wait_ge(s_rstd, 1)
            for t in range(TILES):
                ins = dve.tensor_scalar(x2[:, t, :], x2[:, t, :], mv[:, t, 0:1], rstd[:, t:t + 1],
                                        ALU.subtract, ALU.mult)
                if t % 4 == 3:
                    ins.then_inc(s_out_sb, 1)

        @block.tensor
        def _(pe):
            for banks in (pre, plan):
                prime(pe, [*banks.full.values(), *banks.free.values()])
            def mm(out_, lhsT, rhs, start=True, stop=True):
                return pe.matmul(out_, lhsT, rhs, start=start, stop=stop)

            def split_terms(hi, lo):
                (a_hi, b_hi), (a_lo, b_lo) = hi, lo
                return ((a_hi, b_hi), (a_hi, b_lo), (a_lo, b_hi))

            pe.wait_ge(s_const, 5)
            for j in range(NCH):
                for c in range(NC):
                    f = ("x2T", j, c)
                    pe.wait_ge(pre.free_sem(f), pre.before(f, 0))
                    for k in range(TT):
                        last = pe.transpose(pst[pre.bank(f)][:, P * k:P * k + P],
                                            x2[:, TT * j + k, P * c:P * c + P], ident[:, :])
                    last.then_inc(pre.full_sem(f), 1)
            pe.wait_ge(s_router, 1)
            pe.wait_ge(pre.free_sem(("x2T", NCH - 1, NC - 1)), pre.after(("x2T", NCH - 1, NC - 1), 0))
            for t in range(TILES):
                tok = slice(P * t, P * t + P)
                terms = [x for c in range(NC) for x in split_terms(
                    (x_hi[:, c, tok], r_hi[:, c, :]), (x_lo[:, c, tok], r_lo[:, c, :]))]
                for n, (a, b) in enumerate(terms):
                    last = mm(pst["Y0"][:, NE * t:NE * t + NE], a, b, n == 0, n == len(terms) - 1)
            last.then_inc(pre.full_sem("route"), 1)
            pe.wait_ge(s_rt, 1)
            for j in range(4):
                f = ("rT", j)
                pe.wait_ge(pre.free_sem(f), pre.before(f, 0))
                for k in range(TT):
                    t = TT * j + k
                    last = pe.transpose(pst[pre.bank(f)][0:NE, P * k:P * k + P],
                                        small[:, 0, NE * t:NE * t + NE], ident[:, :])
                last.then_inc(pre.full_sem(f), 1)
            for j in range(TILES // 2):
                f = ("b2", j)
                pe.wait_ge(pre.free_sem(f), pre.before(f, 0))
                pe.wait_ge(pre.free_sem(("rT", j // 2)), pre.after(("rT", j // 2), 0))
                for k in range(2):
                    t = 2 * j + k
                    last = mm(pst[pre.bank(f)][:, C * k:C * k + C], rT[:, P * t:P * t + P], b2[:, :])
                last.then_inc(pre.full_sem(f), 1)
            pe.wait_ge(s_split0, 4)
            for j in range(4):
                pe.wait_ge(pre.free_sem(("b2", TILES // 2 - 4 + j)), pre.after(("b2", TILES // 2 - 4 + j), 0))

            def turn(i, last_turn):
                def hidden(s):
                    e, j = s // NCH, s % NCH
                    tok = slice(CH * j, CH * j + CH)
                    if s == 0:
                        pe.wait_ge(w_split.sem, w_split.at(i, 0))
                    if s == NCH:
                        pe.wait_ge(w_split.sem, w_split.at(i, 4))
                    for ht in range(NHT):
                        f = ("h", s, ht)
                        pe.wait_ge(plan.free_sem(f), plan.before(f, i))
                        col = slice(P * ht, P * ht + P)
                        terms = [x for c in range(NC) for x in split_terms(
                            (w_hi[:, e, c, col], x_hi[:, c, tok]), (w_lo[:, e, c, col], x_lo[:, c, tok]))]
                        for n, (a, b) in enumerate(terms):
                            last = mm(pst[plan.bank(f)][:, :], a, b, n == 0, n == len(terms) - 1)
                        last.then_inc(plan.full_sem(f), 1)

                def outputs(s):
                    e = s // NCH
                    pe.wait_ge(lo_sb.sem, lo_sb.at(i, NHT * s + NHT))
                    for tt in range(TT):
                        f = ("y", s, tt)
                        tok = slice(P * tt, P * tt + P)
                        pe.wait_ge(plan.free_sem(f), plan.before(f, i))
                        terms = []
                        for ht in range(NHT):
                            row = slice(C * (ht % 4), C * (ht % 4) + C)
                            terms += split_terms(
                                (h_hi[:, s % 2, ht, tok], w_hi[:, e, 2 + ht // 4, row]),
                                (h_lo[:, s % 2, ht, tok], w_lo[:, e, 2 + ht // 4, row]))
                        for n, (a, b) in enumerate(terms):
                            last = mm(pst[plan.bank(f)][:, 0:C], a, b, n == 0, n == len(terms) - 1)
                        last.then_inc(plan.full_sem(f), 1)

                for s in range(STEPS):
                    hidden(s)
                    if s:
                        outputs(s - 1)
                outputs(STEPS - 1)

            turns(pe, turn)


def build(nc, w, out):
    with nc.sbuf_tensor("x2", [P, TILES, C], F32) as x2:
        attention_block(nc, x2, w)
        expert_block(nc, x2, w, out)


def _layouts(a):
    def heads(x, parts):
        return x.reshape(x.shape[0], NH, parts, HD).transpose(0, 2, 1, 3).reshape(x.shape[0], parts, HW)

    f = 1.0 / np.float32(10000.0) ** (np.arange(0, RP, 2, dtype=np.float32) / np.float32(RP))
    angle = np.outer(np.arange(T, dtype=np.float32), f.astype(np.float32)).astype(np.float32)
    g = {k: np.asarray(v) for k, v in a.items()}
    at, xa, ff = "L0_attn_w_", "L0_xattn_", "L0_ffn_"
    return {
        "x": g["x"], "ctx": g["ctx_1024"], "mask": g["mask_BxS2_bf1"].view(np.uint8),
        "cq": g[at + "cq"], "ckv": g[at + "ckv"], "krope": g[at + "krope"], "gate": g[at + "gate"],
        "imp": g[at + "imp"], "g_q": g["L0_attn_g_qnorm"], "g_kv": g["L0_attn_g_kvnorm"],
        "cos": np.cos(angle), "sin": np.sin(angle),
        "dq_nopeT": g[at + "dq_nope"].reshape(QL, NH, HD).transpose(2, 1, 0),
        "dkT": g[at + "dk_nope"].reshape(KL, NH, HD).transpose(2, 1, 0),
        "dq": np.concatenate([heads(g[at + "dq_nope"], 1), heads(g[at + "dq_rope"], 2)], axis=1),
        "wink": heads(g[at + "wink"], 3), "winv": g[at + "winv"], "dv": g[at + "dv"],
        "selk": heads(g[at + "selk"], 3), "selv": g[at + "selv"], "proj": g[at + "proj"],
        "xqT": g[xa + "Wq"].T, "xkT": g[xa + "Wk"].T, "xvT": g[xa + "Wv"].T, "xoT": g[xa + "Wo"].T,
        "rows": np.stack([g[xa + "bq"], g[xa + "bk"], g[xa + "bv"], g[xa + "bo"]]),
        "W1": g[ff + "W1"], "W2": g[ff + "W2"], "Wr": g[ff + "Wr"], "br": g[ff + "br"],
        "b1": g[ff + "b1"].reshape(NE, NHT, P).transpose(2, 0, 1), "b2": g[ff + "b2"],
    }


def kernel(**inputs):
    import concourse.bacc as bacc
    from concourse.bass_utils import run_bass_kernel_spmd

    nc = bacc.Bacc("TRN2", target_bir_lowering=False, num_devices=1)
    arrays, w = {}, {}
    for name, a in _layouts(inputs).items():
        a = np.ascontiguousarray(a)
        arrays[f"in_{name}"] = a
        w[name] = nc.dram_tensor(f"in_{name}", a.shape, mybir.dt.from_np(a.dtype), kind="ExternalInput").ap()
    out = nc.dram_tensor("out_0", (NB, T, C), F32, kind="ExternalOutput").ap()
    build(nc, w, out)
    r = run_bass_kernel_spmd(nc, [arrays], core_ids=[0])
    return r.results[0]["out_0"]
```

```python
from contextlib import ExitStack

import numpy as np

import concourse.bass as bass
from concourse import mybir

F32 = mybir.dt.float32
F32R = mybir.dt.float32r
BF16 = mybir.dt.bfloat16
U8 = mybir.dt.uint8
ALU = mybir.AluOpType
ACT = mybir.ActivationFunctionType
AX = mybir.AxisListType.X

P = 128
NB, T, C = 8, 256, 256
NT = T // P
NC = C // P
NH = 16
HD = 32
QK = 3 * HD
HW = NH * HD
QL, KL = 96, 32
KEEP = 64
RP = 2 * HD
PA = QL + KL + RP + 3
XD = 16
SLOTS = 8
NE, HID = 8, 1024
NTOK = NB * T
TILES = NTOK // P
NHT = HID // P
CONSTS = 14
FRONT_STEPS = 28
CROSS_STEPS = 18
CH = 512
NCH = NTOK // CH
LOW = -3.0e38
MASK_FILL = -1.0e8
BREATHERS = (5, 9, 13)
HEAD_START = 2
VECTOR_TURNS = (0, 4, 8, 12)
ATT_SCALE = 1.0 / float(np.sqrt(np.float32(QK)))
X_SCALE = 1.0 / float(np.sqrt(np.float32(XD)))
LN_EPS, RMS_EPS = 1e-5, 1e-6

SEG = [(0, 0, 128, 128, 0, 0), (0, 128, 64, 0, 1, 1), (0, 192, 256, 0, 1, 2),
       (1, 0, 64, 0, 0, 1), (1, 64, 128, 128, 0, 2), (1, 192, 256, 0, 1, 0)]
SEG_AT = [0, 128, 192, 448, 512, 640]
SW = 896


PRIMED = 1


def prime(eng, sems):
    for s in sems:
        eng.sem_inc(s, PRIMED)


class Signal:

    def __init__(self, sem, per, base=0):
        self.sem, self.per, self.base = sem, per, base

    def at(self, i, k):
        return i * self.per + (k + self.base)


class BankPlan:

    def __init__(self, full, free):
        self.full, self.free = full, free
        self.place, self.count, self.ahead = {}, {}, {}

    def add(self, name, bank, ahead=False):
        assert ahead or not self.ahead.get(bank), (name, bank)
        self.place[name] = (bank, self.count.get(bank, 0), ahead)
        self.count[bank] = self.count.get(bank, 0) + 1
        self.ahead[bank] = self.ahead.get(bank, 0) + ahead

    def bank(self, name):
        return self.place[name][0]

    def full_sem(self, name):
        return self.full[self.bank(name)]

    def free_sem(self, name):
        return self.free[self.bank(name)]

    def before(self, name, i):
        b, k, ahead = self.place[name]
        k -= self.count[b] if ahead else 0
        return i * self.count[b] + (k + self.ahead[b] + PRIMED)

    def after(self, name, i):
        return self.before(name, i) + 1

    def turns(self, bank, i):
        return i * self.count[bank] + (self.ahead[bank] + PRIMED)


class Chain:

    def __init__(self, sem, per=0, i=0):
        self.sem, self.per, self.i, self.n = sem, per, i, 0

    def step(self):
        self.n += 1
        return self.sem

    def value(self):
        return self.i * self.per + self.n

    def close(self):
        assert self.n == self.per, (self.n, self.per)


def interleave(main, side):
    for n, _ in enumerate(main):
        if n not in BREATHERS:
            next(side, None)
    for _ in side:
        pass


def block_plan(full, free):
    plan = BankPlan(full, free)
    for h in range(NH):
        for half in range(2):
            if h >= HEAD_START:
                plan.add(("s", h, half), f"S{2 * (h % 2) + half}")
        for half in range(2):
            plan.add(("pT", h, half), f"T{half}")
    for g in range(4):
        plan.add(("o", g), ("X", "O")[g % 2])
    plan.add("proj", "S0")
    plan.add("ctxT", "O")
    plan.add("kx", "S0")
    plan.add("vx", "S1")
    plan.add("x1T", "T0")
    plan.add("qx", "S0")
    n = 0
    for name in ("kxT", "qxT"):
        for t in range(NT):
            for g in range(2):
                plan.add((name, t, g), ("T0", "S1", "S0")[n % 3])
                n += 1
    for h in range(NH):
        plan.add(("sx", h), f"S{h % 2}")
        plan.add(("pxT", h), "T0")
    for g in range(4):
        plan.add(("ox", g), "O")
    plan.add("projx", "T0")

    for n, name in enumerate((
            "first", "imp", ("kw", 0, "a"), ("kw", 0, "b"), ("kw", 0, "n"), "gate",
            ("kw", 1, "a"), ("kw", 1, "b"), ("kw", 1, "n"), ("vw", 0), ("vw", 1),
            ("q", 0, "a"), ("q", 0, "b"), ("q", 0, "n"), ("q", 0, "c"),
            ("q", 1, "a"), ("q", 1, "b"), ("q", 1, "n"), ("q", 1, "c"),
            ("v1", 0), "pos", ("v1", 1), "xsel", ("ks", "a"), ("ks", "b"), ("ks", "n"), "vs")):
        plan.add(name, f"S{2 + n % 2}", ahead=True)
    for n, name in enumerate((
            "xT", ("kwT", 0, 0), ("kwT", 0, 1), ("kwT", 0, 2), "latT", ("kwT", 0, 3),
            *(("kwT", 1, g) for g in range(4)), *(("qT", t, g) for t in range(NT) for g in range(4)),
            ("ksT", 0), ("ksT", 1))):
        plan.add(name, ("X", "T1")[n % 2], ahead=True)
    for h in range(HEAD_START):
        for half in range(2):
            plan.add(("s", h, half), f"S{2 * (h % 2) + half}", ahead=True)
    return plan


def attention_block(nc, x2_rows, w):
    ctx = ExitStack()
    with ctx:
        def sb(name, shape, dt=F32):
            return ctx.enter_context(nc.sbuf_tensor(name, shape, dt))

        def sem(name):
            return ctx.enter_context(nc.semaphore(name))

        BANKS = ("S0", "S1", "S2", "S3", "T0", "T1", "O", "X")
        pst = {b: ctx.enter_context(nc.psum_tensor(f"ps_{b}", [P, 512], F32)) for b in BANKS}
        plan = block_plan({b: sem(f"full_{b}") for b in BANKS}, {b: sem(f"free_{b}") for b in BANKS})

        def ps(name):
            return pst[plan.bank(name)]

        w_first = sb("w_first", [P, NC, PA])
        w_imp = sb("w_imp", [P, NC, 1])
        w_q = sb("w_q", [QL, 4, HW])
        w_kw = sb("w_kw", [P, NC, 3, HW])
        w_vw = sb("w_vw", [P, NC, HW])
        w_ks = sb("w_ks", [P, NC, 3, HW])
        w_vs = sb("w_vs", [P, NC, HW])
        w_dv = sb("w_dv", [P, HW])
        w_proj = sb("w_proj", [P, 4, C])
        wx_q = sb("wx_q", [P, NC, C])
        wx_k = sb("wx_k", [P, NC, C])
        wx_v = sb("wx_v", [P, NC, C])
        wx_o = sb("wx_o", [P, 4, C])
        rows = sb("rows", [P, 4, C])
        g_q = sb("g_q", [P, QL])
        g_kv = sb("g_kv", [P, KL])
        cs = sb("cs", [P, 2, NT, HD])
        ident = sb("ident", [P, P])
        identb = sb("identb", [P, P], BF16)
        upper = sb("upper", [P, P])
        ones = sb("ones", [P, P])
        cmask = sb("cmask", [P, 2 * P])
        tie = sb("tie", [P, NT, T])
        count = sb("count", [P, KEEP])
        halves = sb("halves", [P, 4])

        xin = sb("xin", [P, NT, C])
        cin = sb("cin", [P, NT, C])
        mrow = sb("mrow", [P, T], U8)
        mcol = sb("mcol", [P, NT], U8)
        xT = sb("xT_sb", [P, NC, T])
        cT = sb("cT_sb", [P, NC, T])
        x1T = cT
        pa = sb("pa", [P, NT, PA])
        xres = sb("xres", [P, NT, C])
        lat = sb("lat", [P, NT, QL])
        k1r = sb("k1r", [P, NT, P])
        ktmp = sb("ktmp", [P, 4, NT, HD])
        latT = sb("latT_sb", [P, 2, T])
        sq = ktmp[:, :, :, :].rearrange("p k t d -> p (k t d)")[:, 0:QL]
        ss = sb("ss", [P, 4])
        rs = sb("rs", [P, 4])
        gl = sb("gl", [P, 8])
        gate = sb("gate_sb", [P, 4])
        srow = sb("srow", [P, T])
        scol = sb("scol", [P, NT])
        rank = sb("rank", [P, NT])
        sel = sb("sel", [P, NT])
        pos = sb("pos_sb", [P, NT])
        pick = ktmp[:, :, :, :].rearrange("p k t d -> p (k t d)")[:, 0:NT * KEEP].rearrange(
            "p (t k) -> p t k", t=NT)
        xselT = lat[:, :, :].rearrange("p t n -> p (t n)")[:, 0:NC * KEEP].rearrange("p (c k) -> p c k", c=NC)
        rot = sb("rot", [P, 2, NH, P])
        qT = sb("qT_sb", [P, NH, T])
        kT = sb("kT_sb", [QK, NH, KEEP + T])
        v1 = sb("v1_sb", [P, NT, HW])
        vw = sb("vw_sb", [P, NT, HW])
        vs = sb("vs_sb", [KEEP, HW])
        sm = sb("sm", [P, 2, SW])
        pr = sb("pr", [P, 3, SW])
        pT = sb("pT_sb", [P, 2, 1024])
        sm_flat, pr_flat, pT_flat = (b.rearrange("p a b -> p (a b)") for b in (sm[:, :, :], pr[:, :, :], pT[:, :, :]))
        smx = sm_flat[:, 0:2 * NT * T].rearrange("p (k n) -> p k n", k=2)
        prx = pr_flat[:, 0:3 * NT * T].rearrange("p (k n) -> p k n", k=3)
        pTx = pT_flat[:, 0:2 * NT * T].rearrange("p (k n) -> p k n", k=2)
        cmp1 = sm_flat[:, 2 * NT * T:3 * NT * T].rearrange("p (t n) -> p t n", t=NT)
        lin32 = cmp1
        rem = sb("rem", [P, NT, C])
        cmp2 = rem
        fill = sm_flat[:, 3 * NT * T:3 * NT * T + T]
        rt = [pr_flat[:, 3 * NT * T:3 * NT * T + HW], pr_flat[:, 3 * NT * T + HW:3 * NT * T + 2 * HW],
              pT_flat[:, 2 * NT * T:2 * NT * T + HW], pT_flat[:, 2 * NT * T + HW:2 * NT * T + 2 * HW]]
        mx = sb("mx", [P, 2, 6])
        nmx = sb("nmx", [P, 2, 6])
        den = sb("den", [P, 2, 6])
        rden = sb("rden", [P, 2, 6])
        oT = sb("oT", [P, 4, T])
        x1 = sb("x1", [P, NT, C])
        st = sb("st", [P, NT, 8])
        mv = sb("mv", [P, NT, 2])
        ve = sb("ve", [P, NT])
        rstd = sb("rstd", [P, NT])
        split = sb("split", [P, NT * NH, SLOTS, XD], BF16)
        qxT = sb("qxT", [P, NH, T], BF16)
        kxT = sb("kxT", [P, NH, T], BF16)
        vx = sb("vx", [P, NT, (NH + 1) * XD])
        mf = sb("mf", [P, NT])

        w_first_in, w_mid_in, w_late_in = sem("first_weights_in"), sem("mid_weights_in"), sem("late_weights_in")
        s_const = sem("consts_done")
        s_absorb = sem("absorbed_ps")
        s_absorbed = sem("absorbed_sb")
        s_wide = sem("imp_wide")
        x_in = Signal(sem("x_in"), 16)
        c_in = Signal(sem("ctx_in"), 48)
        first_sb = Signal(sem("first_sb"), 1)
        sumsq = Signal(sem("sumsq"), 1)
        rms_sb = Signal(sem("rms_sb"), 1)
        lat_sb = Signal(sem("lat_sb"), 1)
        gate_max = Signal(sem("gate_max"), 1)
        gate_exp = Signal(sem("gate_exp"), 1)
        gate_done = Signal(sem("gate_done"), 1)
        sel_sb = Signal(sem("sel_sb"), 1)
        pick_sb = Signal(sem("pick_sb"), 1)
        rope_in = Signal(sem("rope_in"), 5)
        rope_out = Signal(sem("rope_out"), 10, PRIMED)
        nope_sb = Signal(sem("nope_sb"), 7)
        ctx_turned = Signal(sem("ctx_turned"), 1)
        score_sb = Signal(sem("score_sb"), 2 * NH)
        exp_done = Signal(sem("exp_done"), 2 * NH)
        rden_sb = Signal(sem("rden_sb"), 2 * NH)
        prob_sb = Signal(sem("prob_sb"), 2 * NH)
        pv_done = Signal(sem("pv_done"), 2 * NH)
        xres_sb = Signal(sem("xres_sb"), 1)
        x2_sb = Signal(sem("x2_sb"), 1)
        x2_out = Signal(sem("x2_out"), 16, PRIMED)
        m_used = Signal(sem("mask_used"), 1)
        var_sb = Signal(sem("var_sb"), 2)
        rstd_sb = Signal(sem("rstd_sb"), 2)
        x1_sb = Signal(sem("x1_sb"), 1)
        x1b_sb = Signal(sem("x1b_sb"), 1)
        kx_part = Signal(sem("kx_part"), 1)
        qx_part = Signal(sem("qx_part"), 3)
        kx_sb = Signal(sem("kx_split"), 1)
        qx_sb = Signal(sem("qx_split"), 3)
        s_dve = sem("dve_chain")
        s_front = sem("dve_front_chain")
        s_pass = sem("wait_carrier")

        UNITS = [("kw", 0), ("kw", 1), ("q", 0), ("q", 1), ("ks", 0)]

        def unit_rows(u):
            kind, t = UNITS[u]
            return (rot[0:KEEP, u % 2, :, :], KEEP) if kind == "ks" else (rot[:, u % 2, :, :], P)

        def last_turn(u):
            kind, t = UNITS[u]
            return ("ksT", 1) if kind == "ks" else (kind + "T", t, 3)

        def unit_fill(u, c):
            kind, t = UNITS[u]
            return ("ks", c) if kind == "ks" else (kind, t, c)

        N_FIRST, N_MID, N_LATE = 11, 5, 12
        block = ctx.enter_context(nc.Block())

        @block.sync
        def _(sp):
            n = 0

            def load(dst, src):
                nonlocal n
                n += 1
                signal = w_first_in if n <= N_FIRST else w_mid_in if n <= N_FIRST + N_MID else w_late_in
                sp.dma_start(dst, src, allow_slow_non_contiguous=True).then_inc(signal, 16)

            prime(sp, [x2_out.sem])
            sp.dma_start(xin[:, :, :], w["x"].rearrange("b (t p) c -> b p t c", p=P)[0]).then_inc(x_in.sem, 16)
            load(pr[0:HD, :, :].rearrange("p a b -> p (a b)")[:, 0:NH * QL],
                 w["dq_nopeT"].rearrange("n h c -> n (h c)"))
            load(pr[0:HD, :, :].rearrange("p a b -> p (a b)")[:, NH * QL:NH * QL + HW],
                 w["dkT"].rearrange("n h c -> n (h c)"))
            load(w_first[:, :, 0:QL], w["cq"].rearrange("(c p) n -> p c n", p=P))
            load(w_first[:, :, QL:QL + KL], w["ckv"].rearrange("(c p) n -> p c n", p=P))
            load(w_first[:, :, QL + KL:QL + KL + RP], w["krope"].rearrange("(c p) n -> p c n", p=P))
            load(w_first[:, :, PA - 3:PA], w["gate"].rearrange("(c p) n -> p c n", p=P))
            load(w_imp[:, :, 0:1], w["imp"].rearrange("(c p) n -> p c n", p=P))
            load(g_q[:, :], w["g_q"].partition_broadcast(P))
            load(g_kv[:, :], w["g_kv"].partition_broadcast(P))
            load(cs[:, 0, :, :], w["cos"].rearrange("(t p) f -> p t f", p=P))
            load(cs[:, 1, :, :], w["sin"].rearrange("(t p) f -> p t f", p=P))
            load(w_q[:, 0:3, :], w["dq"].rearrange("c s n -> c s n"))
            load(w_kw[:, 0, :, :], w["wink"][0:P])
            load(w_kw[:, 1, :, :], w["wink"][P:C])
            load(w_vw[:, :, :], w["winv"].rearrange("(c p) n -> p c n", p=P))
            load(w_dv[QK:P, :], w["dv"])
            load(w_ks[:, 0, :, :], w["selk"][0:P])
            load(w_ks[:, 1, :, :], w["selk"][P:C])
            load(w_vs[:, :, :], w["selv"].rearrange("(c p) n -> p c n", p=P))
            load(w_proj[:, :, :], w["proj"].rearrange("(g p) n -> p g n", p=P))
            for dst, name in ((wx_q, "xqT"), (wx_k, "xkT"), (wx_v, "xvT")):
                load(dst[:, :, :], w[name].rearrange("(c p) n -> p c n", p=P))
            sp.wait_ge(s_const, 4)
            for j in range(4):
                load(wx_o[HD * j:HD * j + XD, :, :],
                     w["xoT"].rearrange("(g j d) n -> j d g n", g=4, j=4)[j])
            load(rows[:, :, :], w["rows"].partition_broadcast(P))
            assert n == N_FIRST + N_MID + N_LATE, n

            x_rows = w["x"].rearrange("b (t p) c -> b p t c", p=P)
            ctx_rows = w["ctx"].rearrange("b (t p) c -> b p t c", p=P)
            mask_cols = w["mask"].rearrange("b (t p) -> b p t", p=P)

            def load_ctx(i, ahead):
                sp.dma_start(cin[:, :, :], ctx_rows[ahead:NB][i]).then_inc(c_in.sem, 16)
                sp.dma_start(mrow[:, :], w["mask"][ahead:NB][i].partition_broadcast(P)).then_inc(c_in.sem, 16)
                sp.dma_start(mcol[:, :], mask_cols[ahead:NB][i], allow_slow_non_contiguous=True
                             ).then_inc(c_in.sem, 16)

            def turn(i, load_x):
                sp.wait_ge(ctx_turned.sem, ctx_turned.at(i, 1))
                sp.sem_inc(s_pass, 1)
                sp.wait_ge(m_used.sem, m_used.at(i, 1))
                sp.sem_inc(s_pass, 1)
                load_ctx(i, 1)
                if load_x:
                    sp.wait_ge(plan.full_sem("xsel"), plan.after("xsel", i + 1))
                    sp.sem_inc(s_pass, 1)
                    sp.wait_ge(xres_sb.sem, xres_sb.at(i + 1, 1))
                    sp.sem_inc(s_pass, 1)
                    sp.dma_start(xin[:, :, :], x_rows[2:NB][i]).then_inc(x_in.sem, 16)
                sp.wait_ge(x2_sb.sem, x2_sb.at(i, 1))
                sp.sem_inc(s_pass, 1)
                sp.dma_start(x2_rows[i], x1[:, :, :]).then_inc(x2_out.sem, 16)

            load_ctx(0, 0)
            sp.wait_ge(plan.full_sem("xsel"), plan.after("xsel", 0))
            sp.wait_ge(xres_sb.sem, xres_sb.at(0, 1))
            sp.dma_start(xin[:, :, :], x_rows[1]).then_inc(x_in.sem, 16)
            with sp.Fori(0, NB - 2) as i:
                turn(i, True)
            turn(NB - 2, False)
            sp.wait_ge(x2_sb.sem, x2_sb.at(NB - 1, 1))
            sp.dma_start(x2_rows[NB - 1], x1[:, :, :]).then_inc(x2_out.sem, 16)
            sp.wait_ge(x2_out.sem, x2_out.at(NB, 0))

        @block.gpsimd
        def _(pool):
            prime(pool, [rope_out.sem])
            ch = Chain(s_const)
            pool.memset(wx_o[:, :, :], 0.0).then_inc(ch.step(), 1)
            pool.memset(ones[:, :], 1.0).then_inc(ch.step(), 1)
            pool.memset(vx[:, :, :], 0.0).then_inc(ch.step(), 1)
            pool.memset(halves[:, :], -0.5).then_inc(ch.step(), 1)
            pool.wait_ge(ch.sem, ch.value())
            pool.affine_select(out=ident[:, :], in_=ones[:, :], compare_op=ALU.is_equal, fill=0.0,
                               base=0, pattern=[[-1, P]], channel_multiplier=1).then_inc(ch.step(), 1)
            pool.affine_select(out=upper[:, :], in_=ones[:, :], compare_op=ALU.is_ge, fill=0.0,
                               base=0, pattern=[[1, P]], channel_multiplier=-1).then_inc(ch.step(), 1)
            pool.memset(cmask[:, :], 0.0).then_inc(ch.step(), 1)
            pool.memset(tie[:, :, :], 1.0).then_inc(ch.step(), 1)
            pool.memset(k1r[:, :, :], 0.0).then_inc(ch.step(), 1)
            pool.iota(count[:, :], pattern=[[1, KEEP]], base=1, channel_multiplier=0,
                      allow_small_or_imprecise_dtypes=True).then_inc(ch.step(), 1)
            pool.wait_ge(ch.sem, ch.value())
            pool.tensor_copy(identb[:, :], ident[:, :]).then_inc(ch.step(), 1)
            pool.affine_select(out=cmask[:, P:2 * P], in_=cmask[:, P:2 * P], compare_op=ALU.is_ge,
                               fill=LOW, base=0, pattern=[[-1, P]], channel_multiplier=1).then_inc(ch.step(), 1)
            for t in range(NT):
                pool.affine_select(out=tie[:, t, :], in_=tie[:, t, :], compare_op=ALU.is_gt,
                                   fill=0.0, base=P * t, pattern=[[-1, T]], channel_multiplier=1).then_inc(ch.step(), 1)
            assert ch.n == CONSTS
            pool.wait_ge(w_first_in, 16 * N_FIRST)

            def front(i):
                for _ in range(4):
                    yield
                pool.wait_ge(sumsq.sem, sumsq.at(i, 1))
                pool.tensor_tensor(rs[:, :], ss[:, :], halves[:, :], ALU.pow).then_inc(rms_sb.sem, 1)

                def rope_sums(u):
                    rows_, n = unit_rows(u)
                    if u >= 2:
                        pool.wait_ge(plan.full_sem(last_turn(u - 2)), plan.after(last_turn(u - 2), i))
                    r = [b[0:n].rearrange("p (h d) -> p h d", h=NH) for b in rt]
                    pool.wait_ge(rope_in.sem, rope_in.at(i, u + 1))
                    pool.tensor_tensor(rows_[:, :, HD:2 * HD], r[0], r[2], ALU.subtract
                                       ).then_inc(rope_out.sem, 1)
                    pool.wait_ge(plan.free_sem(unit_fill(u, "b")), plan.after(unit_fill(u, "b"), i))
                    pool.tensor_tensor(rows_[:, :, 2 * HD:3 * HD], r[1], r[3], ALU.add
                                       ).then_inc(rope_out.sem, 1)

                yield
                for stage in range(5, 20):
                    if stage in (5, 7, 11, 13, 19):
                        rope_sums((5, 7, 11, 13, 19).index(stage))
                    yield

            def normalise(i, h):
                pool.wait_ge(rden_sb.sem, rden_sb.at(i, h + 1))
                for n, (half, off, width, m, q, br) in enumerate(SEG):
                    p_ = pr[:, h % 3, SEG_AT[n]:SEG_AT[n] + width]
                    last = pool.tensor_tensor(p_, p_, rden[:, h % 2, n:n + 1].to_broadcast([P, width]),
                                              ALU.mult)
                last.then_inc(prob_sb.sem, 1)

            def heads(i):
                for h in range(1, NH):
                    normalise(i, h)
                    if h >= NH - 2:
                        yield
                for _ in range(3):
                    yield

            def cross(i, following):
                pool.wait_ge(var_sb.sem, var_sb.at(i, 1))
                pool.tensor_tensor(rstd[:, :], ve[:, :], halves[:, 0:NT], ALU.pow).then_inc(rstd_sb.sem, 1)
                yield
                yield
                pool.wait_ge(plan.full_sem("x1T"), plan.after("x1T", i))
                pool.tensor_tensor(x1[:, :, :], x1[:, :, :],
                                   rows[:, 3:4, :].to_broadcast([P, NT, C]), ALU.add
                                   ).then_inc(x1b_sb.sem, 1)

                yield

                def normalise_x(h):
                    pool.wait_ge(rden_sb.sem, rden_sb.at(i, NH + h + 1))
                    for q in range(NT):
                        p_ = prx[:, h % 3, T * q:T * q + T]
                        last = pool.tensor_tensor(p_, p_, rden[:, h % 2, q:q + 1].to_broadcast([P, T]),
                                                  ALU.mult)
                    last.then_inc(prob_sb.sem, 1)

                for _ in range(3, 7):
                    yield
                for h in range(NH + 3):
                    if 1 <= h < NH + 1:
                        normalise_x(h - 1)
                    yield
                if following is not None:
                    normalise(following, 0)
                pool.wait_ge(var_sb.sem, var_sb.at(i, 2))
                pool.tensor_tensor(rstd[:, :], ve[:, :], halves[:, 0:NT], ALU.pow).then_inc(rstd_sb.sem, 1)


            def row(i, following):
                yield from heads(i)
                yield from cross(i, following)

            for _ in front(0):
                pass
            normalise(0, 0)
            with pool.Fori(0, NB - 1) as i:
                interleave(row(i, i + 1), front(i + 1))
            for _ in row(NB - 1, None):
                pass

        @block.scalar
        def _(act):
            act.wait_ge(s_absorb, 1)
            act.copy(w_q[:, 3, :], pst["S0"][0:QL, :]).then_inc(s_absorbed, 1)
            act.wait_ge(w_first_in, 16 * N_FIRST)
            act.wait_ge(s_const, CONSTS)

            def evacuate(i, name, dst, src, scale=None):
                act.wait_ge(plan.full_sem(name), plan.after(name, i))
                if scale is None:
                    ins = act.copy(dst, src)
                else:
                    ins = act.activation(dst, src, ACT.Copy, scale=scale)
                ins.then_inc(plan.free_sem(name), 1)
                return ins

            def front(i):
                def nope(u):
                    rows_, n = unit_rows(u)
                    f = unit_fill(u, "n")
                    act.wait_ge(plan.full_sem(f), plan.after(f, i))
                    if u >= 2:
                        act.wait_ge(plan.full_sem(last_turn(u - 2)), plan.after(last_turn(u - 2), i))
                    act.copy(rows_[:, :, 0:HD],
                             ps(f)[0:n, :].rearrange("p (h d) -> p h d", h=NH)).then_inc(plan.free_sem(f), 1)

                def key_turn(t, g):
                    f = ("kwT", t, g)
                    evacuate(i, f, kT[:, 4 * g:4 * g + 4, KEEP + P * t:KEEP + P * t + P],
                             ps(f)[0:QK, :].rearrange("p (h t) -> p h t", h=4))

                def query_turn(t, g):
                    f = ("qT", t, g)
                    evacuate(i, f, qT[:, 4 * g:4 * g + 4, P * t:P * t + P],
                             ps(f)[:, :].rearrange("p (h t) -> p h t", h=4))

                def absorbed(t):
                    f = ("q", t, "c")
                    evacuate(i, f, rot[:, t, :, QK:P], ps(f)[:, :].rearrange("p (h d) -> p h d", h=NH))

                def values_out(name, t, dst, scale):
                    evacuate(i, (name, t), dst[:, t, :], ps((name, t))[:, :], scale)

                yield
                evacuate(i, "xT", xT[:, :, :], ps("xT")[:, :].rearrange("p (c t) -> p c t", c=NC))
                yield
                yield
                evacuate(i, "first", pa[:, :, :],
                         ps("first")[:, :].rearrange("p (t n) -> p t n", t=NT)[:, :, 0:PA])
                yield
                yield
                nope(0)
                act.wait_ge(gate_max.sem, gate_max.at(i, 1))
                act.activation(gl[:, 3:6], gl[:, 0:3], ACT.Exp, bias=gl[:, 6:7], scale=1.0 / T,
                               accum_out=gl[:, 7:8]).then_inc(gate_exp.sem, 1)
                yield
                yield
                nope(1)
                key_turn(0, 0)
                yield
                act.wait_ge(gate_done.sem, gate_done.at(i, 1))
                values_out("vw", 0, vw, gate[:, 2:3])
                key_turn(0, 2)
                yield
                values_out("vw", 1, vw, gate[:, 2:3])
                key_turn(1, 0)
                yield
                key_turn(1, 2)
                yield
                nope(2)
                absorbed(0)
                yield
                if not isinstance(i, int):
                    act.wait_ge(plan.free_sem("proj"), plan.after("proj", i - 1))
                act.copy(xres[:, :, :], xin[:, :, :]).then_inc(xres_sb.sem, 1)
                yield
                nope(3)
                absorbed(1)
                query_turn(0, 0)
                yield
                values_out("v1", 0, v1, gate[:, 0:1])
                query_turn(0, 2)
                yield
                values_out("v1", 1, v1, gate[:, 0:1])
                query_turn(1, 0)
                yield
                query_turn(1, 2)
                yield
                yield
                yield
                nope(4)
                evacuate(i, "vs", vs[:, :], ps("vs")[0:KEEP, :], gate[0:KEEP, 1:2])
                yield
                yield
                evacuate(i, ("ksT", 0), kT[:, 0:8, 0:KEEP],
                         ps(("ksT", 0))[0:QK, :].rearrange("p (h t) -> p h t", h=8))

            def heads_out(i, name, g):
                act.wait_ge(pv_done.sem, pv_done.at(i, 4 * g + 4 + (NH if name == "ox" else 0)))
                act.copy(oT[:, g, :], ps((name, g))[:, 0:T]).then_inc(plan.free_sem((name, g)), 1)

            def heads(i):
                def exps(h):
                    act.wait_ge(score_sb.sem, score_sb.at(i, h + 1))
                    if h >= 3:
                        act.wait_ge(plan.full_sem(("pT", h - 3, 1)), plan.after(("pT", h - 3, 1), i))
                    for n, (half, off, width, m, q, br) in enumerate(SEG):
                        a = SEG_AT[n]
                        last = act.activation(pr[:, h % 3, a:a + width], sm[:, h % 2, a:a + width], ACT.Exp,
                                              bias=nmx[:, h % 2, n:n + 1], scale=ATT_SCALE,
                                              accum_out=den[:, h % 2, n:n + 1])
                    last.then_inc(exp_done.sem, 1)

                def turn_probs(h):
                    f = ("pT", h, 1)
                    if h >= 2:
                        act.wait_ge(pv_done.sem, pv_done.at(i, h - 1))
                    evacuate(i, f, pT[:, h % 2, 512:1024], ps(f)[:, :])

                for h in range(NH + 4):
                    if 3 <= h < NH + 3:
                        turn_probs(h - 3)
                    if h < NH:
                        exps(h)
                    if h >= 4 and (h - 4) % 4 == 3:
                        heads_out(i, "o", (h - 4) // 4)
                    if h >= NH - 1:
                        yield

            def cross(i):
                act.wait_ge(ctx_turned.sem, ctx_turned.at(i, 1))
                act.copy(cT[:, :, :], ps("ctxT")[:, :].rearrange("p (c t) -> p c t", c=NC)
                         ).then_inc(plan.free_sem("ctxT"), 1)
                yield
                yield
                evacuate(i, "x1T", x1T[:, :, :], ps("x1T")[:, :].rearrange("p (c t) -> p c t", c=NC))
                act.wait_ge(kx_part.sem, kx_part.at(i, 1))
                act.copy(split[:, :, 3:6, :], split[:, :, 0:3, :])
                act.copy(split[:, :, 6:8, :], split[:, :, 0:2, :]).then_inc(kx_sb.sem, 1)
                yield
                yield

                def split_turn(name, dst, t, g):
                    f = (name, t, g)
                    evacuate(i, f, dst[:, 8 * g:8 * g + 8, P * t:P * t + P],
                             ps(f)[:, :].bitcast(BF16).rearrange("p (h t) -> p h t", h=8))

                split_turn("kxT", kxT, 0, 1)
                split_turn("kxT", kxT, 1, 1)
                yield
                for part, (a, b) in enumerate(((1, 3), (4, 6), (7, 8))):
                    act.wait_ge(qx_part.sem, qx_part.at(i, part + 1))
                    act.copy(split[:, :, a:b, :],
                             split[:, :, a - 1:a, :].to_broadcast([P, NT * NH, b - a, XD])
                             ).then_inc(qx_sb.sem, 1)
                yield
                split_turn("qxT", qxT, 0, 1)
                split_turn("qxT", qxT, 1, 1)
                yield

                def exps_x(h):
                    act.wait_ge(score_sb.sem, score_sb.at(i, NH + h + 1))
                    if h >= 3:
                        act.wait_ge(plan.full_sem(("pxT", h - 3)), plan.after(("pxT", h - 3), i))
                    for q in range(NT):
                        last = act.activation(prx[:, h % 3, T * q:T * q + T], smx[:, h % 2, T * q:T * q + T],
                                              ACT.Exp, bias=nmx[:, h % 2, q:q + 1], scale=X_SCALE,
                                              accum_out=den[:, h % 2, q:q + 1])
                    last.then_inc(exp_done.sem, 1)

                def turn_probs_x(h):
                    if h in VECTOR_TURNS:
                        return
                    if h >= 2:
                        act.wait_ge(pv_done.sem, pv_done.at(i, NH + h - 1))
                    evacuate(i, ("pxT", h), pTx[:, h % 2, :], ps(("pxT", h))[:, :])

                for h in range(NH + 4):
                    if 3 <= h < NH + 3:
                        turn_probs_x(h - 3)
                    if h < NH:
                        exps_x(h)
                    if h >= 4 and (h - 4) % 4 == 3:
                        heads_out(i, "ox", (h - 4) // 4)
                    yield

            def row(i):
                yield from heads(i)
                yield from cross(i)

            for _ in front(0):
                pass
            with act.Fori(0, NB - 1) as i:
                interleave(row(i), front(i + 1))
            for _ in row(NB - 1):
                pass

        @block.vector
        def _(dve):
            dve.memset(pst["T1"][:, :], 0.0).then_inc(s_wide, 1)
            dve.wait_ge(w_first_in, 16 * N_FIRST)
            dve.wait_ge(s_const, CONSTS)

            def front(i):
                c = Chain(s_front, FRONT_STEPS, i)

                def rope_products(u, k):
                    rows_, n = unit_rows(u)
                    t = UNITS[u][1]
                    f = unit_fill(u, "ab"[k])
                    dve.wait_ge(plan.full_sem(f), plan.after(f, i))
                    src = ps(f)[0:n, :].rearrange("p (h d) -> p h d", h=NH)
                    for m in range(2):
                        table = cs[0:n, m if k == 0 else 1 - m, t:t + 1, :].to_broadcast([n, NH, HD])
                        dst = rt[2 * k + m][0:n].rearrange("p (h d) -> p h d", h=NH)
                        if k == 0:
                            dve.wait_ge(rope_out.sem, rope_out.at(i, 2 * u - 1 + m if u else 0))
                        ins = dve.tensor_tensor(dst, src, table, ALU.mult)
                        if k == 1 and m == 0:
                            ins.then_inc(rope_in.sem, 1)
                        if m == 1:
                            ins.then_inc(plan.free_sem(f), 1)

                def key_turn(t, g):
                    f = ("kwT", t, g)
                    dve.wait_ge(plan.full_sem(f), plan.after(f, i))
                    dve.tensor_copy(kT[:, 4 * g:4 * g + 4, KEEP + P * t:KEEP + P * t + P],
                                    ps(f)[0:QK, :].rearrange("p (h t) -> p h t", h=4)).then_inc(plan.free_sem(f), 1)

                def query_turn(t, g):
                    f = ("qT", t, g)
                    dve.wait_ge(plan.full_sem(f), plan.after(f, i))
                    dve.tensor_copy(qT[:, 4 * g:4 * g + 4, P * t:P * t + P],
                                    ps(f)[:, :].rearrange("p (h t) -> p h t", h=4)).then_inc(plan.free_sem(f), 1)

                for _ in range(3):
                    yield
                dve.wait_ge(plan.full_sem("imp"), plan.after("imp", i))
                dve.tensor_copy(srow[:, :], ps("imp")[:, 0:T]).then_inc(plan.free_sem("imp"), 1)
                yield

                dve.wait_ge(plan.free_sem("first"), plan.after("first", i))
                for t in range(NT):
                    dve.tensor_tensor_reduce(out=sq[:, 0:QL], in0=pa[:, t, 0:QL], in1=pa[:, t, 0:QL],
                                             scale=1.0, scalar=0.0, op0=ALU.mult, op1=ALU.add,
                                             accum_out=ss[:, t:t + 1]).then_inc(c.step(), 1)
                    dve.wait_ge(c.sem, c.value())
                    dve.tensor_tensor_reduce(out=sq[:, 0:KL], in0=pa[:, t, QL:QL + KL],
                                             in1=pa[:, t, QL:QL + KL],
                                             scale=1.0, scalar=0.0, op0=ALU.mult, op1=ALU.add,
                                             accum_out=ss[:, 2 + t:3 + t]).then_inc(c.step(), 1)
                    dve.wait_ge(c.sem, c.value())
                dve.tensor_scalar(ss[:, 0:2], ss[:, 0:2], 1.0 / QL, RMS_EPS, ALU.mult, ALU.add).then_inc(c.step(), 1)
                dve.tensor_scalar(ss[:, 2:4], ss[:, 2:4], 1.0 / KL, RMS_EPS, ALU.mult, ALU.add
                                  ).then_inc(sumsq.sem, 1)
                rope_products(0, 0)
                rope_products(0, 1)
                yield
                dve.wait_ge(plan.full_sem("gate"), plan.after("gate", i))
                dve.tensor_copy(gl[:, 0:3], ps("gate")[:, 0:3]).then_inc(plan.free_sem("gate"), 1)
                dve.wait_ge(plan.free_sem("gate"), plan.after("gate", i))
                dve.tensor_reduce(gl[:, 6:7], gl[:, 0:3], AX, ALU.max).then_inc(c.step(), 1)
                dve.wait_ge(c.sem, c.value())
                dve.tensor_scalar(gl[:, 6:7], gl[:, 6:7], -1.0 / T, None, ALU.mult).then_inc(gate_max.sem, 1)
                k0 = QL + KL
                xa, xb = pa[:, :, k0:k0 + HD], pa[:, :, k0 + HD:k0 + RP]
                cos, sin = cs[:, 0, :, :], cs[:, 1, :, :]
                for n, (v, f) in enumerate(((xa, cos), (xa, sin), (xb, sin), (xb, cos))):
                    dve.scalar_tensor_tensor(ktmp[:, n, :, :], v, 1.0 / NH, f, ALU.mult, ALU.mult).then_inc(c.step(), 1)
                dve.wait_ge(c.sem, c.value())
                dve.tensor_tensor(k1r[:, :, HD:2 * HD], ktmp[:, 0], ktmp[:, 2], ALU.subtract).then_inc(c.step(), 1)
                dve.tensor_tensor(k1r[:, :, 2 * HD:3 * HD], ktmp[:, 1], ktmp[:, 3], ALU.add).then_inc(c.step(), 1)
                dve.wait_ge(rms_sb.sem, rms_sb.at(i, 1))
                for t in range(NT):
                    dve.scalar_tensor_tensor(lat[:, t, :], pa[:, t, 0:QL], rs[:, t:t + 1], g_q[:, :],
                                             ALU.mult, ALU.mult).then_inc(c.step(), 1)
                    dve.scalar_tensor_tensor(k1r[:, t, 3 * HD:P], pa[:, t, QL:QL + KL],
                                             rs[:, 2 + t:3 + t], g_kv[:, :], ALU.mult, ALU.mult).then_inc(c.step(), 1)
                dve.wait_ge(c.sem, c.value())
                dve.sem_inc(lat_sb.sem, 1)
                yield
                rope_products(1, 0)
                rope_products(1, 1)
                dve.wait_ge(gate_exp.sem, gate_exp.at(i, 1))
                dve.reciprocal(gl[:, 6:7], gl[:, 7:8]).then_inc(c.step(), 1)
                dve.wait_ge(c.sem, c.value())
                dve.tensor_scalar(gate[:, 0:3], gl[:, 3:6], gl[:, 6:7], None, ALU.mult
                                  ).then_inc(gate_done.sem, 1)
                yield
                key_turn(0, 1)
                yield

                dve.wait_ge(plan.full_sem("latT"), plan.after("latT", i))
                dve.tensor_copy(latT[0:QL, 0, :], ps("latT")[0:QL, 0:T])
                dve.tensor_copy(latT[:, 1, :], ps("latT")[:, T:2 * T]).then_inc(plan.free_sem("latT"), 1)
                yield
                key_turn(0, 3)
                yield
                key_turn(1, 1)
                rope_products(2, 0)
                rope_products(2, 1)
                yield
                key_turn(1, 3)
                dve.wait_ge(plan.free_sem("imp"), plan.after("imp", i))
                for t in range(NT):
                    dve.tensor_tensor(cmp1[:, t, 0:P], srow[:, P * t:P * t + P], ident[:, :], ALU.mult
                        ).then_inc(c.step(), 1)
                dve.wait_ge(c.sem, c.value())
                dve.tensor_reduce(scol[:, :], cmp1[:, :, 0:P], AX, ALU.add).then_inc(c.step(), 1)
                dve.wait_ge(c.sem, c.value())
                for t in range(NT):
                    dve.tensor_scalar(cmp1[:, t, :], srow[:, :], scol[:, t:t + 1], None, ALU.is_gt
                        ).then_inc(c.step(), 1)
                    dve.scalar_tensor_tensor(cmp2[:, t, :], srow[:, :], scol[:, t:t + 1], tie[:, t, :],
                                             ALU.is_equal, ALU.mult).then_inc(c.step(), 1)
                dve.wait_ge(c.sem, c.value())
                dve.tensor_tensor(cmp1[:, :, :], cmp1[:, :, :], cmp2[:, :, :], ALU.add).then_inc(c.step(), 1)
                dve.wait_ge(c.sem, c.value())
                dve.tensor_reduce(rank[:, :], cmp1[:, :, :], AX, ALU.add).then_inc(c.step(), 1)
                dve.wait_ge(c.sem, c.value())
                dve.tensor_scalar(sel[:, :], rank[:, :], float(KEEP), None, ALU.is_lt).then_inc(sel_sb.sem, 1)
                yield
                rope_products(3, 0)
                rope_products(3, 1)
                yield
                query_turn(0, 1)
                yield
                query_turn(0, 3)
                dve.wait_ge(plan.full_sem("pos"), plan.after("pos", i))
                dve.tensor_copy(pos[:, :], ps("pos")[:, 0:NT]).then_inc(plan.free_sem("pos"), 1)
                dve.wait_ge(plan.free_sem("pos"), plan.after("pos", i))
                for t in range(NT):
                    dve.tensor_scalar(pick[:, t, :], count[:, :], pos[:, t:t + 1], sel[:, t:t + 1],
                                      ALU.is_equal, ALU.mult).then_inc(c.step(), 1)
                dve.wait_ge(c.sem, c.value())
                dve.sem_inc(pick_sb.sem, 1)
                yield
                query_turn(1, 1)
                yield
                dve.wait_ge(plan.full_sem("xsel"), plan.after("xsel", i))
                dve.tensor_copy(xselT[:, :, :],
                                ps("xsel")[:, 0:NC * KEEP].rearrange("p (c k) -> p c k", c=NC)
                                    ).then_inc(plan.free_sem("xsel"), 1)
                query_turn(1, 3)
                yield
                yield
                rope_products(4, 0)
                rope_products(4, 1)
                yield
                yield
                yield
                dve.wait_ge(plan.full_sem(("ksT", 1)), plan.after(("ksT", 1), i))
                dve.tensor_copy(kT[:, 8:16, 0:KEEP],
                                ps(("ksT", 1))[0:QK, :].rearrange("p (h t) -> p h t", h=8)
                                    ).then_inc(plan.free_sem(("ksT", 1)), 1)

                c.close()

            def denominators(i, h, k, n):
                dve.wait_ge(exp_done.sem, exp_done.at(i, k + 1))
                if k >= 2:
                    dve.wait_ge(prob_sb.sem, prob_sb.at(i, k - 1))
                dve.reciprocal(rden[:, h % 2, 0:n], den[:, h % 2, 0:n]).then_inc(rden_sb.sem, 1)

            def scores(i, h):
                if h >= 2:
                    dve.wait_ge(exp_done.sem, exp_done.at(i, h - 1))
                for n, (half, off, width, m, q, br) in enumerate(SEG):
                    f = ("s", h, half)
                    if n in (0, 3):
                        dve.wait_ge(plan.full_sem(f), plan.after(f, i))
                        dve.sem_inc(s_pass, 1)
                    a = SEG_AT[n]
                    ins = dve.tensor_tensor_reduce(
                        out=sm[:, h % 2, a:a + width], in0=ps(f)[:, off:off + width],
                        in1=cmask[:, m:m + width], scale=1.0, scalar=LOW, op0=ALU.add, op1=ALU.max,
                        accum_out=mx[:, h % 2, n:n + 1])
                    if n in (2, 5):
                        ins.then_inc(plan.free_sem(f), 1)
                dve.wait_ge(plan.free_sem(("s", h, 0)), plan.after(("s", h, 0), i))
                dve.wait_ge(plan.free_sem(("s", h, 1)), plan.after(("s", h, 1), i))
                dve.tensor_scalar(nmx[:, h % 2, :], mx[:, h % 2, :], -ATT_SCALE, None, ALU.mult
                                  ).then_inc(score_sb.sem, 1)

            def heads(i):
                def turn_probs(h):
                    f = ("pT", h, 0)
                    dve.wait_ge(plan.full_sem(f), plan.after(f, i))
                    if h >= 2:
                        dve.wait_ge(pv_done.sem, pv_done.at(i, h - 1))
                    dve.tensor_copy(pT[:, h % 2, 0:512], ps(f)[:, :]).then_inc(plan.free_sem(f), 1)

                for h in range(NH + 3):
                    if HEAD_START <= h < NH:
                        scores(i, h)
                    if 2 <= h < NH + 1:
                        denominators(i, h - 1, h - 1, 6)
                    if h >= 3:
                        turn_probs(h - 3)
                    if h >= NH - 1:
                        yield
                yield

            def residual_stats(i, c, f, base):
                dve.wait_ge(plan.full_sem(f), plan.after(f, i))
                dve.tensor_tensor(x1[:, :, :], ps(f)[:, :].rearrange("p (t c) -> p t c", t=NT),
                                  base[:, :, :], ALU.add).then_inc(plan.free_sem(f), 1)
                dve.wait_ge(plan.free_sem(f), plan.after(f, i))
                for t in range(NT):
                    dve.bn_stats(st[:, t, 0:6], x1[:, t, :]).then_inc(c.step(), 1)
                dve.wait_ge(c.sem, c.value())
                dve.sem_inc(s_pass, 1)
                for t in range(NT):
                    dve.bn_aggr(mv[:, t, :], st[:, t, 0:6]).then_inc(c.step(), 1)
                dve.wait_ge(c.sem, c.value())
                dve.tensor_scalar(ve[:, :], mv[:, :, 1:2].rearrange("p t o -> p (t o)"), LN_EPS, None,
                                  ALU.add).then_inc(var_sb.sem, 1)

            def normalise(i, k, done):
                dve.wait_ge(rstd_sb.sem, rstd_sb.at(i, k))
                for t in range(NT):
                    last = dve.tensor_scalar(x1[:, t, :], x1[:, t, :], mv[:, t, 0:1], rstd[:, t:t + 1],
                                             ALU.subtract, ALU.mult)
                last.then_inc(done.sem, 1)

            def cross(i, following):
                c = Chain(s_dve, CROSS_STEPS, i)
                dve.wait_ge(xres_sb.sem, xres_sb.at(i, 1))
                dve.wait_ge(x2_out.sem, x2_out.at(i, 0))
                residual_stats(i, c, "proj", xres)
                yield
                normalise(i, 1, x1_sb)

                dve.wait_ge(c_in.sem, c_in.at(i, 48))
                dve.tensor_scalar(fill, mrow[:, :], 1.0, -MASK_FILL / X_SCALE,
                                  ALU.subtract, ALU.mult).then_inc(c.step(), 1)
                dve.tensor_copy(mf[:, :], mcol[:, :]).then_inc(c.step(), 1)
                dve.wait_ge(c.sem, c.value())
                dve.sem_inc(m_used.sem, 1)

                def bias_row(k):
                    return rows[:, k:k + 1, :].to_broadcast([P, NT, C])

                def grouped(t):
                    return t[:, :, :].rearrange("p t (h d) -> p (t h) d", d=XD)

                dve.wait_ge(plan.full_sem("kx"), plan.after("kx", i))
                dve.tensor_tensor(lin32[:, :, :], ps("kx")[:, :].rearrange("p (t c) -> p t c", t=NT),
                                  bias_row(1), ALU.add).then_inc(plan.free_sem("kx"), 1)
                dve.wait_ge(plan.free_sem("kx"), plan.after("kx", i))
                for t in range(NT):
                    dve.tensor_scalar(lin32[:, t, :], lin32[:, t, :], mf[:, t:t + 1], None, ALU.mult
                                      ).then_inc(c.step(), 1)
                dve.wait_ge(c.sem, c.value())
                yield
                dve.tensor_copy(split[:, :, 0, :], grouped(lin32)).then_inc(c.step(), 1)
                dve.wait_ge(c.sem, c.value())
                dve.tensor_tensor(grouped(rem), grouped(lin32), split[:, :, 0, :], ALU.subtract).then_inc(c.step(), 1)
                dve.wait_ge(c.sem, c.value())
                dve.tensor_copy(split[:, :, 1, :], grouped(rem)).then_inc(c.step(), 1)
                dve.wait_ge(c.sem, c.value())
                dve.tensor_tensor(grouped(rem), grouped(rem), split[:, :, 1, :], ALU.subtract).then_inc(c.step(), 1)
                dve.wait_ge(c.sem, c.value())
                dve.tensor_copy(split[:, :, 2, :], grouped(rem)).then_inc(kx_part.sem, 1)
                yield
                dve.wait_ge(plan.full_sem("vx"), plan.after("vx", i))
                for t in range(NT):
                    ins = dve.tensor_tensor(vx[:, t, 0:C].rearrange("p (h d) -> p h d", d=XD),
                                            ps("vx")[:, C * t:C * t + C].rearrange("p (h d) -> p h d", d=XD),
                                            rows[:, 2, :].rearrange("p (h d) -> p h d", d=XD), ALU.add)
                ins.then_inc(plan.free_sem("vx"), 1)
                dve.wait_ge(plan.full_sem("qx"), plan.after("qx", i))
                dve.tensor_tensor(lin32[:, :, :], ps("qx")[:, :].rearrange("p (t c) -> p t c", t=NT),
                                  bias_row(0), ALU.add).then_inc(plan.free_sem("qx"), 1)
                yield

                def split_turn(name, dst, t, g):
                    f = (name, t, g)
                    dve.wait_ge(plan.full_sem(f), plan.after(f, i))
                    dve.tensor_copy(dst[:, 8 * g:8 * g + 8, P * t:P * t + P],
                                    ps(f)[:, :].bitcast(BF16).rearrange("p (h t) -> p h t", h=8)
                                        ).then_inc(plan.free_sem(f), 1)

                split_turn("kxT", kxT, 0, 0)
                split_turn("kxT", kxT, 1, 0)
                yield
                dve.wait_ge(plan.full_sem(("kxT", 1, 1)), plan.after(("kxT", 1, 1), i))
                dve.wait_ge(kx_part.sem, kx_part.at(i, 1))
                dve.wait_ge(plan.free_sem("qx"), plan.after("qx", i))
                dve.tensor_copy(split[:, :, 0, :], grouped(lin32)).then_inc(qx_part.sem, 1)
                dve.wait_ge(qx_part.sem, qx_part.at(i, 1))
                dve.tensor_tensor(grouped(rem), grouped(lin32), split[:, :, 0, :], ALU.subtract).then_inc(c.step(), 1)
                dve.wait_ge(c.sem, c.value())
                dve.tensor_copy(split[:, :, 3, :], grouped(rem)).then_inc(qx_part.sem, 1)
                dve.wait_ge(qx_part.sem, qx_part.at(i, 2))
                dve.tensor_tensor(grouped(rem), grouped(rem), split[:, :, 3, :], ALU.subtract).then_inc(c.step(), 1)
                dve.wait_ge(c.sem, c.value())
                dve.tensor_copy(split[:, :, 6, :], grouped(rem)).then_inc(qx_part.sem, 1)
                yield
                split_turn("qxT", qxT, 0, 0)
                split_turn("qxT", qxT, 1, 0)
                yield

                def scores_x(h):
                    dve.wait_ge(exp_done.sem, exp_done.at(i, NH + h - 1))
                    f = ("sx", h)
                    dve.wait_ge(plan.full_sem(f), plan.after(f, i))
                    dve.sem_inc(s_pass, 1)
                    for q in range(NT):
                        ins = dve.tensor_tensor_reduce(
                            out=smx[:, h % 2, T * q:T * q + T], in0=ps(f)[:, T * q:T * q + T],
                            in1=fill, scale=1.0, scalar=LOW, op0=ALU.add, op1=ALU.max,
                            accum_out=mx[:, h % 2, q:q + 1])
                    ins.then_inc(plan.free_sem(f), 1)
                    dve.wait_ge(plan.free_sem(f), plan.after(f, i))
                    dve.tensor_scalar(nmx[:, h % 2, 0:NT], mx[:, h % 2, 0:NT], -X_SCALE, None, ALU.mult
                                      ).then_inc(score_sb.sem, 1)

                def turn_probs_x(h):
                    if h not in VECTOR_TURNS:
                        return
                    f = ("pxT", h)
                    dve.wait_ge(plan.full_sem(f), plan.after(f, i))
                    if h >= 2:
                        dve.wait_ge(pv_done.sem, pv_done.at(i, NH + h - 1))
                    dve.tensor_copy(pTx[:, h % 2, :], ps(f)[:, :]).then_inc(plan.free_sem(f), 1)

                for h in range(NH + 4):
                    if h < NH:
                        scores_x(h)
                    if 1 <= h < NH + 1:
                        denominators(i, h - 1, NH + h - 1, NT)
                    if 3 <= h < NH + 3:
                        turn_probs_x(h - 3)
                    if following is not None and NH < h <= NH + HEAD_START:
                        dve.wait_ge(exp_done.sem, exp_done.at(i, 2 * NH))
                        scores(following, h - NH - 1)
                    yield
                if following is not None:
                    denominators(following, 0, 0, 6)
                dve.wait_ge(x1b_sb.sem, x1b_sb.at(i, 1))
                residual_stats(i, c, "projx", x1)
                normalise(i, 2, x2_sb)
                c.close()

            def row(i, following):
                yield from heads(i)
                yield from cross(i, following)

            for _ in front(0):
                pass
            for h in range(HEAD_START):
                scores(0, h)
            denominators(0, 0, 0, 6)
            with dve.Fori(0, NB - 1) as i:
                interleave(row(i, i + 1), front(i + 1))
            for _ in row(NB - 1, None):
                pass

        @block.tensor
        def _(pe):
            prime(pe, [*plan.full.values(), *plan.free.values()])

            def mm(out, lhsT, rhs, start=True, stop=True):
                return pe.matmul(out, lhsT, rhs, start=start, stop=stop)

            pe.wait_ge(w_first_in, 16 * N_FIRST)
            stage = pr[0:HD, :, :].rearrange("p a b -> p (a b)")
            for h in range(NH):
                last = mm(pst["S0"][0:QL, HD * h:HD * h + HD], stage[:, QL * h:QL * h + QL],
                          stage[:, NH * QL + HD * h:NH * QL + HD * h + HD])
            last.then_inc(s_absorb, 1)
            pe.wait_ge(s_absorbed, 1)
            pe.wait_ge(s_wide, 1)
            pe.wait_ge(s_const, CONSTS)

            def transpose4(i, name, pieces, idn):
                pe.wait_ge(plan.free_sem(name), plan.before(name, i))
                for out, in_ in pieces:
                    last = pe.transpose(out, in_, idn)
                if plan.bank(name) != "O":
                    last.then_inc(plan.full_sem(name), 1)
                return last

            def product(i, name, m, n, lhs, rhs):
                pe.wait_ge(plan.free_sem(name), plan.before(name, i))
                ks = len(lhs)
                for k in range(ks):
                    last = mm(ps(name)[0:m, 0:n], lhs[k], rhs[k], k == 0, k == ks - 1)
                last.then_inc(plan.full_sem(name), 1)

            def tok(xt, t):
                return [xt[:, c, P * t:P * t + P] for c in range(NC)]

            def front(i):
                def turn_rows(u, groups):
                    kind, t = UNITS[u]
                    rows_, n = unit_rows(u)
                    pe.wait_ge(plan.free_sem(unit_fill(u, "n")), plan.after(unit_fill(u, "n"), i))
                    if kind == "q":
                        pe.wait_ge(plan.free_sem(unit_fill(u, "c")), plan.after(unit_fill(u, "c"), i))
                    pe.wait_ge(rope_out.sem, rope_out.at(i, 2 * u + 2))
                    width = P if kind == "q" else QK
                    per = 8 if kind == "ks" else 4
                    for g in groups:
                        f = ("ksT", g) if kind == "ks" else (kind + "T", t, g)
                        pe.wait_ge(plan.free_sem(f), plan.before(f, i))
                        if kind == "ks":
                            pe.sem_inc(s_pass, 1)
                        for k in range(per):
                            last = pe.transpose(ps(f)[0:width, n * k:n * k + n], rows_[:, per * g + k, 0:width],
                                                ident[0:n, 0:n])
                        last.then_inc(plan.full_sem(f), 1)

                def keys(t, s):
                    product(i, ("kw", t, "nab"[s]), P, HW, tok(xT, t), [w_kw[:, c, s, :] for c in range(NC)])

                def window_values(t):
                    product(i, ("vw", t), P, HW, tok(xT, t), [w_vw[:, c, :] for c in range(NC)])

                def queries(t, s):
                    product(i, ("q", t, "nabc"[s]), P, HW, [latT[0:QL, 0, P * t:P * t + P]], [w_q[:, s, :]])

                def selected_keys(s):
                    product(i, ("ks", "nab"[s]), KEEP, HW, [xselT[:, c, :] for c in range(NC)],
                            [w_ks[:, c, s, :] for c in range(NC)])

                def latent_values(t):
                    product(i, ("v1", t), P, HW, [latT[QK:P, 1, P * t:P * t + P]], [w_dv[QK:P, :]])

                pe.wait_ge(x_in.sem, x_in.at(i, 16))
                transpose4(i, "xT", [(ps("xT")[:, T * c + P * t:T * c + P * t + P], xin[:, t, P * c:P * c + P])
                                  for c in range(NC) for t in range(NT)], ident[:, :])
                yield
                yield
                pe.wait_ge(plan.free_sem("xT"), plan.after("xT", i))
                pe.wait_ge(plan.free_sem("first"), plan.before("first", i))
                for t in range(NT):
                    for c in range(NC):
                        last = mm(ps("first")[:, T * t:T * t + PA], xT[:, c, P * t:P * t + P], w_first[:, c, :],
                                  c == 0, c == NC - 1)
                last.then_inc(plan.full_sem("first"), 1)
                product(i, "imp", P, T, [w_imp[:, c, :].to_broadcast([P, P]) for c in range(NC)],
                        [xT[:, c, :] for c in range(NC)])
                yield
                if isinstance(i, int):
                    pe.wait_ge(w_mid_in, 16 * N_MID)
                keys(0, 1)
                keys(0, 2)
                yield
                keys(0, 0)
                pe.wait_ge(plan.free_sem("first"), plan.after("first", i))
                product(i, "gate", P, 3, [ones[:, :]] * NT, [pa[:, t, PA - 3:PA] for t in range(NT)])
                yield
                keys(1, 1)
                keys(1, 2)
                yield
                keys(1, 0)
                turn_rows(0, (0, 1))
                yield
                window_values(0)
                turn_rows(0, (2,))
                pe.wait_ge(lat_sb.sem, lat_sb.at(i, 1))
                pe.wait_ge(plan.free_sem("latT"), plan.before("latT", i))
                for t in range(NT):
                    pe.transpose(ps("latT")[0:QL, P * t:P * t + P], lat[:, t, :], ident[:, :])
                for t in range(NT):
                    last = pe.transpose(ps("latT")[:, T + P * t:T + P * t + P], k1r[:, t, :], ident[:, :])
                last.then_inc(plan.full_sem("latT"), 1)
                yield
                window_values(1)
                turn_rows(0, (3,))
                turn_rows(1, (0,))
                yield
                turn_rows(1, (1, 2))
                pe.wait_ge(plan.free_sem("latT"), plan.after("latT", i))
                queries(0, 1)
                queries(0, 2)
                yield
                turn_rows(1, (3,))
                queries(0, 0)
                queries(0, 3)
                yield
                queries(1, 1)
                queries(1, 2)
                yield
                turn_rows(2, (0, 1))
                queries(1, 0)
                queries(1, 3)
                yield
                turn_rows(2, (2, 3))
                latent_values(0)
                pe.wait_ge(sel_sb.sem, sel_sb.at(i, 1))
                pe.wait_ge(plan.free_sem("pos"), plan.before("pos", i))
                mm(ps("pos")[:, 0:1], upper[:, :], sel[:, 0:1])
                mm(ps("pos")[:, 1:2], ones[:, :], sel[:, 0:1], True, False)
                mm(ps("pos")[:, 1:2], upper[:, :], sel[:, 1:2], False, True).then_inc(plan.full_sem("pos"), 1)
                yield
                latent_values(1)
                turn_rows(3, (0, 1))
                yield
                pe.wait_ge(pick_sb.sem, pick_sb.at(i, 1))
                pe.wait_ge(plan.free_sem("xsel"), plan.before("xsel", i))
                for c in range(NC):
                    for t in range(NT):
                        last = mm(ps("xsel")[:, KEEP * c:KEEP * c + KEEP], xin[:, t, P * c:P * c + P],
                                  pick[:, t, :], t == 0, t == NT - 1)
                last.then_inc(plan.full_sem("xsel"), 1)
                turn_rows(3, (2, 3))
                yield
                yield
                if isinstance(i, int):
                    pe.wait_ge(w_late_in, 16 * N_LATE)
                pe.wait_ge(plan.free_sem("xsel"), plan.after("xsel", i))
                selected_keys(1)
                selected_keys(2)
                yield
                selected_keys(0)
                product(i, "vs", KEEP, HW, [xselT[:, c, :] for c in range(NC)], [w_vs[:, c, :] for c in range(NC)])
                yield
                yield
                turn_rows(4, (0, 1))

            def scores(i, h):
                q0, q1 = (qT[:, h, P * q:P * q + P] for q in range(NT))
                A, B = ps(("s", h, 0)), ps(("s", h, 1))
                pe.wait_ge(plan.free_sem(("s", h, 0)), plan.before(("s", h, 0), i))
                mm(A[:, 0:P], q0, latT[:, 1, 0:P])
                mm(A[:, P:P + KEEP + T], q1[0:QK], kT[:, h, :]).then_inc(plan.full_sem(("s", h, 0)), 1)
                pe.wait_ge(plan.free_sem(("s", h, 1)), plan.before(("s", h, 1), i))
                mm(B[:, 0:KEEP + P], q0[0:QK], kT[:, h, 0:KEEP + P])
                mm(B[:, KEEP + P:KEEP + P + T], q1, latT[:, 1, :]).then_inc(plan.full_sem(("s", h, 1)), 1)

            def head_start(i, h):
                if h == 0:
                    pe.wait_ge(plan.free_sem(("qT", 1, 3)), plan.after(("qT", 1, 3), i))
                    pe.wait_ge(plan.free_sem(("qT", 1, 2)), plan.after(("qT", 1, 2), i))
                    pe.wait_ge(plan.free_sem(("ksT", 1)), plan.after(("ksT", 1), i))
                    pe.wait_ge(plan.free_sem(("ksT", 0)), plan.after(("ksT", 0), i))
                scores(i, h)

            def heads(i):
                def turn_probs(h):
                    p = pr[:, h % 3, :]
                    pe.wait_ge(prob_sb.sem, prob_sb.at(i, h + 1))
                    for half, blocks in enumerate((
                            ((0, 0), (640, P), (768, 2 * P), (320, 3 * P)),
                            ((512, 0), (192, P), (448, 2 * P), (128, 3 * P)))):
                        f = ("pT", h, half)
                        pe.wait_ge(plan.free_sem(f), plan.before(f, i))
                        for n, (a, dst) in enumerate(blocks):
                            width = KEEP if half == 1 and n >= 2 else P
                            last = pe.transpose(ps(f)[0:width, dst:dst + P], p[:, a:a + width], ident[:, :])
                        last.then_inc(plan.full_sem(f), 1)

                def values(h):
                    j, g = h % 4, h // 4
                    if j == 0:
                        pe.wait_ge(plan.free_sem(("o", g)), plan.before(("o", g), i))
                    o = ps(("o", g))[HD * j:HD * j + HD, 0:T]
                    col = slice(HD * h, HD * h + HD)
                    q = pT[:, h % 2, :]
                    pe.wait_ge(plan.free_sem(("pT", h, 0)), plan.after(("pT", h, 0), i))
                    pe.wait_ge(plan.free_sem(("pT", h, 1)), plan.after(("pT", h, 1), i))
                    if j == 3 and plan.bank(("o", g)) == "X":
                        pe.sem_inc(plan.full_sem(("o", g)), 1)
                    mm(o, v1[:, 0, col], q[:, 0:T], True, False)
                    mm(o[:, P:T], v1[:, 1, col], q[:, T:T + P], False, False)
                    mm(o[:, P:T], vw[:, 1, col], q[:, T + P:2 * T], False, False)
                    mm(o, vw[:, 0, col], q[:, 2 * T:3 * T], False, False)
                    last = mm(o, vs[:, col], q[0:KEEP, 3 * T:4 * T], False, True)
                    last.then_inc(pv_done.sem, 1)

                for h in range(NH + 4):
                    if HEAD_START <= h < NH:
                        scores(i, h)
                    if 3 <= h < NH + 3:
                        turn_probs(h - 3)
                    if h >= 4:
                        values(h - 4)
                    if h >= NH:
                        yield

            def project(i, name, wo):
                pe.wait_ge(plan.free_sem(name), plan.before(name, i))
                last_heads = ("o" if name == "proj" else "ox", 3)
                pe.wait_ge(plan.free_sem(last_heads), plan.after(last_heads, i))
                for t in range(NT):
                    for g in range(4):
                        last = mm(ps(name)[:, T * t:T * t + C], oT[:, g, P * t:P * t + P], wo[:, g, :],
                                  g == 0, g == 3)
                last.then_inc(plan.full_sem(name), 1)

            def cross(i, following):
                project(i, "proj", w_proj)
                pe.wait_ge(c_in.sem, c_in.at(i, 48))
                last = transpose4(i, "ctxT", [(ps("ctxT")[:, T * c + P * t:T * c + P * t + P],
                                               cin[:, t, P * c:P * c + P])
                                    for c in range(NC) for t in range(NT)], ident[:, :])
                last.then_inc(ctx_turned.sem, 1)
                yield

                def linear(name, src, wt):
                    pe.wait_ge(plan.free_sem(name), plan.before(name, i))
                    for t in range(NT):
                        for c in range(NC):
                            last = mm(ps(name)[:, T * t:T * t + C], src[:, c, P * t:P * t + P], wt[:, c, :],
                                      c == 0, c == NC - 1)
                    last.then_inc(plan.full_sem(name), 1)

                pe.wait_ge(plan.free_sem("ctxT"), plan.after("ctxT", i))
                linear("kx", cT, wx_k)
                linear("vx", cT, wx_v)
                yield
                pe.wait_ge(x1_sb.sem, x1_sb.at(i, 1))
                transpose4(i, "x1T", [(ps("x1T")[:, T * c + P * t:T * c + P * t + P], x1[:, t, P * c:P * c + P])
                                   for c in range(NC) for t in range(NT)], ident[:, :])
                yield
                pe.wait_ge(plan.free_sem("x1T"), plan.after("x1T", i))
                linear("qx", x1T, wx_q)
                yield

                def turn_split(name, src):
                    for t in range(NT):
                        for g in range(2):
                            f = (name, t, g)
                            o = ps(f)[:, :].bitcast(BF16)
                            transpose4(i, f, [(o[:, P * k:P * k + P],
                                            src[:, NH * t + 8 * g + k, :, :].rearrange("p s d -> p (s d)"))
                                           for k in range(8)], identb[:, :])

                pe.wait_ge(kx_sb.sem, kx_sb.at(i, 1))
                turn_split("kxT", split)
                yield
                yield
                pe.wait_ge(qx_sb.sem, qx_sb.at(i, 3))
                turn_split("qxT", split)
                yield
                pe.wait_ge(plan.free_sem(("qxT", 1, 0)), plan.after(("qxT", 1, 0), i))
                pe.wait_ge(plan.free_sem(("qxT", 1, 1)), plan.after(("qxT", 1, 1), i))

                def scores_x(h):
                    f = ("sx", h)
                    pe.wait_ge(plan.free_sem(f), plan.before(f, i))
                    for q in range(NT):
                        last = mm(ps(f)[:, T * q:T * q + T], qxT[:, h, P * q:P * q + P], kxT[:, h, :])
                    last.then_inc(plan.full_sem(f), 1)

                def turn_probs_x(h):
                    pe.wait_ge(prob_sb.sem, prob_sb.at(i, NH + h + 1))
                    transpose4(i, ("pxT", h), [(ps(("pxT", h))[:, T * k + P * q:T * k + P * q + P],
                                             prx[:, h % 3, T * q + P * k:T * q + P * k + P])
                                            for k in range(NT) for q in range(NT)], ident[:, :])

                def values_x(h):
                    j, g = h % 4, h // 4
                    if j == 0:
                        pe.wait_ge(plan.free_sem(("ox", g)), plan.before(("ox", g), i))
                    o = ps(("ox", g))[HD * j:HD * j + HD, 0:T]
                    pe.wait_ge(plan.free_sem(("pxT", h)), plan.after(("pxT", h), i))
                    for k in range(NT):
                        last = mm(o, vx[:, k, XD * h:XD * h + HD], pTx[:, h % 2, T * k:T * k + T], k == 0, k == NT - 1)
                    last.then_inc(pv_done.sem, 1)

                for h in range(NH + 4):
                    if h < NH:
                        scores_x(h)
                    if 3 <= h < NH + 3:
                        turn_probs_x(h - 3)
                    if h >= 4:
                        values_x(h - 4)
                    if following is not None and NH <= h < NH + HEAD_START:
                        head_start(following, h - NH)
                    yield
                project(i, "projx", wx_o)

            def row(i, following):
                yield from heads(i)
                yield from cross(i, following)

            for _ in front(0):
                pass
            for h in range(HEAD_START):
                head_start(0, h)
            with pe.Fori(0, NB - 1) as i:
                interleave(row(i, i + 1), front(i + 1))
            for _ in row(NB - 1, None):
                pass


def expert_block(nc, x2_rows, w, out):
    ctx = ExitStack()
    with ctx:
        def sb(name, shape, dt=F32):
            return ctx.enter_context(nc.sbuf_tensor(name, shape, dt))

        def sem(name):
            return ctx.enter_context(nc.semaphore(name))

        BANKS = ("H0", "H1", "H2", "H3", "Y0", "Y1", "Y2", "Y3")
        pst = {b: ctx.enter_context(nc.psum_tensor(f"ps_{b}", [P, 512], F32)) for b in BANKS}
        STEPS = 2 * NCH
        TT = CH // P

        pre = BankPlan({b: sem(f"pre_full_{b}") for b in BANKS}, {b: sem(f"pre_free_{b}") for b in BANKS})
        for j in range(NCH):
            for c in range(NC):
                pre.add(("x2T", j, c), f"H{(2 * j + c) % 4}")
        for j in range(NCH):
            pre.add(("scores", j), f"Y{j}")
        pre.add("route", "Y0")
        for j in range(4):
            pre.add(("rT", j), f"H{j}")
        for j in range(TILES // 2):
            pre.add(("b2", j), f"Y{j % 4}")
        plan = BankPlan({b: sem(f"exp_full_{b}") for b in BANKS}, {b: sem(f"exp_free_{b}") for b in BANKS})
        for s in range(STEPS):
            for ht in range(NHT):
                plan.add(("h", s, ht), f"H{ht % 4}")
            for tt in range(TT):
                plan.add(("y", s, tt), f"Y{tt}")

        x2 = sb("x2", [P, TILES, C])
        x_hi = sb("x_hi", [P, NC, NTOK], F32R)
        x_lo = sb("x_lo", [P, NC, NTOK], F32R)
        w_raw = sb("w_raw", [P, 4, 1024])
        w_hi = sb("w_hi", [P, 2, 4, 1024], F32R)
        w_lo = sb("w_lo", [P, 2, 4, 1024], F32R)
        h_sb = sb("h_sb", [P, 4, CH])
        h_hi = sb("h_hi", [P, 2, NHT, CH], F32R)
        h_lo = sb("h_lo", [P, 2, NHT, CH], F32R)
        ident = sb("ident2", [P, P])
        r_raw = sb("r_raw", [P, NC, NE])
        r_hi = sb("r_hi", [P, NC, NE], F32R)
        r_lo = sb("r_lo", [P, NC, NE], F32R)
        b_r = sb("b_r", [P, NE])
        b1 = sb("b1_sb", [P, NE, NHT])
        b1c = sb("b1_now", [P, 2, NHT])
        b2 = sb("b2_sb", [NE, C])
        lower8 = sb("lower8", [P, NE, NE])
        rt = sb("route_t", [P, NE, TILES])
        rc = sb("route_now", [P, 2, TILES])
        half = sb("half2", [P, TILES])
        small = sb("small", [P, 6, TILES * NE])
        big = [h_sb[:, 2 * k:2 * k + 2, :].rearrange("p a b -> p (a b)") for k in range(2)]
        scT = rT = h_sb[0:NE, :, :].rearrange("p a b -> p (a b)")
        st = sb("st2", [P, TILES, 6])
        mv = sb("mv2", [P, TILES, 2])
        ve = sb("ve2", [P, TILES])
        rstd = sb("rstd2", [P, TILES])

        s_in = sem("small_in")
        s_x2 = [sem(f"x2_in_{j}") for j in range(NCH)]
        s_raw0 = sem("raw0_in")
        s_const = sem("consts2")
        s_hi = sem("x_hi_done")
        s_dve = sem("dve_chain2")
        s_exp = sem("route_exp")
        s_exp_in = sem("route_exp_in")
        s_router = sem("router_split")
        s_rt = sem("route_done")
        s_split0_hi, s_split0 = sem("split0_hi"), sem("split0")
        s_var, s_rstd, s_out_sb, s_out = sem("var2"), sem("rstd2_done"), sem("out_sb"), sem("out_dma")
        raw_in = Signal(sem("raw_in"), 64)
        w_hi_sb = Signal(sem("w_hi_sb"), 8)
        w_split = Signal(sem("w_split"), 8, PRIMED)
        now_sb = Signal(sem("now_sb"), 1)
        hi_sb = Signal(sem("hi_sb"), STEPS * NHT)
        lo_sb = Signal(sem("lo_sb"), STEPS * NHT, PRIMED)

        w1_v = w["W1"].rearrange("e (c p) h -> e p c h", p=P)
        w2_v = w["W2"].rearrange("e (t p) d -> e p t d", p=P)

        def turns(eng, body):
            with eng.Fori(0, NE // 2 - 1) as i:
                body(i, False)
            body(NE // 2 - 1, True)

        block = ctx.enter_context(nc.Block())

        @block.sync
        def _(sp):
            for j in range(NCH):
                sp.dma_start(x2[:, TT * j:TT * j + TT, :].rearrange("p (b t) c -> p b t c", t=NT),
                             x2_rows[TT // NT * j:TT // NT * (j + 1)].rearrange("b p t c -> p b t c")
                             ).then_inc(s_x2[j], 16)
            sp.dma_start(r_raw[:, :, :], w["Wr"].rearrange("(c p) e -> p c e", p=P)).then_inc(s_in, 16)
            sp.dma_start(b_r[:, :], w["br"].partition_broadcast(P)).then_inc(s_in, 16)
            sp.dma_start(b1[:, :, :], w["b1"]).then_inc(s_in, 16)
            sp.dma_start(b2[:, :], w["b2"]).then_inc(s_in, 16)

            def load(e, sem_):
                sp.dma_start(w_raw[:, 0:2, :], w1_v[e]).then_inc(sem_, 16)
                sp.dma_start(w_raw[:, 2:4, :].rearrange("p a (b d) -> p (a b) d", d=C), w2_v[e]
                             ).then_inc(sem_, 16)

            load(0, s_raw0)
            sp.wait_ge(s_split0, 4)

            def turn(i, last):
                sp.wait_ge(w_split.sem, w_split.at(i, 0))
                load(i * 2 + 1, raw_in.sem)
                if not last:
                    sp.wait_ge(w_split.sem, w_split.at(i, 4))
                    load(i * 2 + 2, raw_in.sem)

            turns(sp, turn)
            for q in range(4):
                sp.wait_ge(s_out_sb, q + 1)
                out_v = out.rearrange("b t c -> (b t) c").rearrange("(n p) c -> p n c", p=P)
                sp.dma_start(out_v[:, 4 * q:4 * q + 4, :],
                             x2[:, 4 * q:4 * q + 4, :]).then_inc(s_out, 16)
            sp.wait_ge(s_out, 64)

        @block.gpsimd
        def _(pool):
            prime(pool, [w_split.sem, lo_sb.sem])
            c = Chain(s_const)
            pool.memset(lower8[:, :, :], 1.0).then_inc(c.step(), 1)
            pool.memset(half[:, :], -0.5).then_inc(c.step(), 1)
            pool.memset(ident[:, :], 1.0).then_inc(c.step(), 1)
            pool.wait_ge(c.sem, c.value())
            pool.affine_select(out=ident[:, :], in_=ident[:, :], compare_op=ALU.is_equal, fill=0.0,
                               base=0, pattern=[[-1, P]], channel_multiplier=1).then_inc(c.step(), 1)
            pool.affine_select(out=lower8[:, :, :], in_=lower8[:, :, :], compare_op=ALU.is_gt, fill=0.0,
                               base=0, pattern=[[1, NE], [-1, NE]], channel_multiplier=0).then_inc(c.step(), 1)
            for piece in range(4):
                pool.wait_ge(s_split0_hi, piece + 1)
                pool.tensor_tensor(w_lo[:, 0, piece, :], w_raw[:, piece, :],
                                   w_hi[:, 0, piece, :].bitcast(F32), ALU.subtract).then_inc(s_split0, 1)

            def rstds(j):
                tiles = slice(TT * j, TT * j + TT)
                pool.wait_ge(s_var, j + 1)
                pool.tensor_tensor(rstd[:, tiles], ve[:, tiles], half[:, tiles], ALU.pow).then_inc(s_rstd, 1)

            def turn(i, last):
                for s in range(STEPS):
                    for ht in range(NHT):
                        pool.wait_ge(hi_sb.sem, hi_sb.at(i, NHT * s + ht + 1))
                        pool.tensor_tensor(h_lo[:, s % 2, ht, :], h_sb[:, ht % 4, :],
                                           h_hi[:, s % 2, ht, :].bitcast(F32), ALU.subtract
                                           ).then_inc(lo_sb.sem, 1)
                    if last and s > NCH:
                        rstds(s - 1 - NCH)
                    if last and s >= NCH:
                        continue
                    pool.wait_ge(w_hi_sb.sem, w_hi_sb.at(i, s + 1))
                    nxt = 1 - s // NCH
                    pool.tensor_tensor(w_lo[:, nxt, s % 4, :], w_raw[:, s % 4, :],
                                       w_hi[:, nxt, s % 4, :].bitcast(F32), ALU.subtract
                                       ).then_inc(w_split.sem, 1)

            turns(pool, turn)
            rstds(NCH - 1)

        @block.scalar
        def _(act):
            for j in range(NCH):
                for c in range(NC):
                    f = ("x2T", j, c)
                    act.wait_ge(pre.full_sem(f), pre.after(f, 0))
                    act.copy(x_hi[:, c, CH * j:CH * j + CH], pst[pre.bank(f)][:, :]).then_inc(s_hi, 1)
            for j in range(NCH):
                f = ("scores", j)
                act.wait_ge(pre.full_sem(f), pre.after(f, 0))
                act.copy(scT[:, CH * j:CH * j + CH], pst[pre.bank(f)][0:NE, :]).then_inc(pre.free_sem(f), 1)
            act.wait_ge(s_exp_in, 1)
            act.activation(small[:, 2, :], small[:, 1, :], ACT.Exp).then_inc(s_exp, 1)
            for j in range(4):
                f = ("rT", j)
                act.wait_ge(pre.full_sem(f), pre.after(f, 0))
                act.copy(rT[:, CH * j:CH * j + CH], pst[pre.bank(f)][0:NE, :]).then_inc(pre.free_sem(f), 1)

            def turn(i, last):
                act.wait_ge(now_sb.sem, now_sb.at(i, 1))
                for s in range(STEPS):
                    for ht in range(NHT):
                        f = ("h", s, ht)
                        n = NHT * s + ht
                        act.wait_ge(plan.full_sem(f), plan.after(f, i))
                        if n >= 4:
                            act.wait_ge(lo_sb.sem, lo_sb.at(i, n - 3))
                        else:
                            act.wait_ge(lo_sb.sem, lo_sb.at(i, 0))
                        ins = act.activation(h_sb[:, ht % 4, :], pst[plan.bank(f)][:, :], ACT.Relu,
                                             bias=b1c[:, s // NCH, ht:ht + 1])
                        ins.then_inc(plan.free_sem(f), 1)

            turns(act, turn)

        @block.vector
        def _(dve):
            c = Chain(s_dve)
            dve.wait_ge(s_in, 64)
            dve.tensor_copy(r_hi[:, :, :], r_raw[:, :, :]).then_inc(c.step(), 1)
            dve.wait_ge(c.sem, c.value())
            dve.tensor_tensor(r_lo[:, :, :], r_raw[:, :, :], r_hi[:, :, :].bitcast(F32), ALU.subtract
                              ).then_inc(s_router, 1)
            for j in range(NCH):
                for cc in range(NC):
                    f = ("x2T", j, cc)
                    dve.wait_ge(s_hi, 2 * j + cc + 1)
                    x_h = x_hi[:, cc, CH * j:CH * j + CH]
                    dve.tensor_tensor(x_lo[:, cc, CH * j:CH * j + CH], pst[pre.bank(f)][:, :],
                                      x_h.bitcast(F32), ALU.subtract).then_inc(pre.free_sem(f), 1)
            dve.wait_ge(s_raw0, 32)
            for piece in range(4):
                dve.tensor_copy(w_hi[:, 0, piece, :], w_raw[:, piece, :]).then_inc(s_split0_hi, 1)

            def sm(k):
                return small[:, k, :].rearrange("p (t e) -> p t e", e=NE)

            def pair(k, a):
                return sm(k)[:, :, :].unsqueeze(3 if a else 2).to_broadcast([P, TILES, NE, NE])

            dve.wait_ge(pre.full_sem("route"), pre.after("route", 0))
            ins = dve.tensor_tensor(sm(0), pst["Y0"][:, 0:TILES * NE].rearrange("p (t e) -> p t e", e=NE),
                                    b_r[:, :].unsqueeze(1).to_broadcast([P, TILES, NE]), ALU.add)
            ins.then_inc(pre.free_sem("route"), 1)
            dve.wait_ge(pre.free_sem("route"), pre.after("route", 0))
            v = [b.rearrange("p (t e f) -> p t e f", e=NE, f=NE) for b in big]
            dve.wait_ge(s_const, 5)
            dve.tensor_tensor(v[0], pair(0, False), pair(0, True), ALU.is_gt).then_inc(c.step(), 1)
            dve.tensor_tensor(v[1], pair(0, False), pair(0, True), ALU.is_equal).then_inc(c.step(), 1)
            dve.wait_ge(c.sem, c.value())
            dve.tensor_tensor(v[1], v[1], lower8[:, :, :].unsqueeze(1).to_broadcast([P, TILES, NE, NE]),
                              ALU.mult).then_inc(c.step(), 1)
            dve.wait_ge(c.sem, c.value())
            dve.tensor_tensor(v[0], v[0], v[1], ALU.add).then_inc(c.step(), 1)
            dve.wait_ge(c.sem, c.value())
            dve.tensor_reduce(small[:, 3, :], v[0].rearrange("p t e f -> p (t e) f"), AX, ALU.add).then_inc(c.step(), 1)
            dve.wait_ge(c.sem, c.value())
            dve.scalar_tensor_tensor(small[:, 4, :], small[:, 3, :], 2.0, small[:, 0, :],
                                     ALU.is_lt, ALU.mult).then_inc(c.step(), 1)
            dve.wait_ge(c.sem, c.value())
            dve.tensor_reduce(small[:, 5, 0:TILES], sm(4), AX, ALU.max).then_inc(c.step(), 1)
            dve.wait_ge(c.sem, c.value())
            dve.tensor_tensor(sm(1), sm(4), small[:, 5, 0:TILES].unsqueeze(2).to_broadcast([P, TILES, NE]),
                              ALU.subtract).then_inc(s_exp_in, 1)
            dve.wait_ge(s_exp, 1)
            dve.tensor_reduce(small[:, 5, 0:TILES], sm(2), AX, ALU.add).then_inc(c.step(), 1)
            dve.wait_ge(c.sem, c.value())
            dve.reciprocal(small[:, 5, TILES:2 * TILES], small[:, 5, 0:TILES]).then_inc(c.step(), 1)
            dve.wait_ge(c.sem, c.value())
            dve.tensor_tensor(sm(0), sm(2),
                              small[:, 5, TILES:2 * TILES].unsqueeze(2).to_broadcast([P, TILES, NE]),
                              ALU.mult).then_inc(c.step(), 1)
            dve.wait_ge(c.sem, c.value())
            dve.tensor_copy(rt[:, :, :], small[:, 0, :].rearrange("p (t e) -> p e t", e=NE)
                            ).then_inc(s_rt, 1)
            for j in range(TILES // 2):
                f = ("b2", j)
                dve.wait_ge(pre.full_sem(f), pre.after(f, 0))
                dve.tensor_tensor(
                    x2[:, 2 * j:2 * j + 2, :], x2[:, 2 * j:2 * j + 2, :],
                    pst[pre.bank(f)][:, :].rearrange("p (t c) -> p t c", t=2), ALU.add
                    ).then_inc(pre.free_sem(f), 1)
            dve.wait_ge(pre.free_sem(("b2", TILES // 2 - 1)), pre.after(("b2", TILES // 2 - 1), 0))
            dve.wait_ge(s_rt, 1)

            def statistics(j):
                tiles = range(TT * j, TT * j + TT)
                for tt in range(TT):
                    f = ("y", STEPS - NCH + j, tt)
                    dve.wait_ge(plan.free_sem(f), plan.after(f, NE // 2 - 1))
                for t in tiles:
                    dve.bn_stats(st[:, t, :], x2[:, t, :]).then_inc(c.step(), 1)
                dve.wait_ge(c.sem, c.value())
                for t in tiles:
                    dve.bn_aggr(mv[:, t, :], st[:, t, :]).then_inc(c.step(), 1)
                dve.wait_ge(c.sem, c.value())
                dve.tensor_scalar(ve[:, TT * j:TT * j + TT], mv[:, TT * j:TT * j + TT, 1:2].rearrange(
                    "p t o -> p (t o)"), LN_EPS, None, ALU.add).then_inc(s_var, 1)

            def norm(j):
                dve.wait_ge(s_rstd, j + 1)
                for t in range(TT * j, TT * j + TT):
                    ins = dve.tensor_scalar(x2[:, t, :], x2[:, t, :], mv[:, t, 0:1], rstd[:, t:t + 1],
                                            ALU.subtract, ALU.mult)
                ins.then_inc(s_out_sb, 1)

            def turn(i, last):
                dve.wait_ge(plan.free["H3"], plan.turns("H3", i))
                dve.wait_ge(plan.free["Y3"], plan.turns("Y3", i))
                k = i * 2 if last else bass.ds(i * 2, 2)
                two = slice(k, k + 2) if last else k
                dve.tensor_copy(rc[:, :, :], rt[:, two, :])
                dve.tensor_copy(b1c[:, :, :], b1[:, two, :]).then_inc(now_sb.sem, 1)
                dve.wait_ge(now_sb.sem, now_sb.at(i, 1))

                def sums(s):
                    for tt in range(TT):
                        f = ("y", s, tt)
                        tile = TT * (s % NCH) + tt
                        dve.wait_ge(plan.full_sem(f), plan.after(f, i))
                        dve.scalar_tensor_tensor(
                            x2[:, tile, :], pst[plan.bank(f)][:, 0:C], rc[:, s // NCH, tile:tile + 1],
                            x2[:, tile, :], ALU.mult, ALU.add).then_inc(plan.free_sem(f), 1)

                def next_weights(s):
                    dve.wait_ge(raw_in.sem, raw_in.at(i, 32 * (s // NCH + 1)))
                    dve.tensor_copy(w_hi[:, 1 - s // NCH, s % 4, :], w_raw[:, s % 4, :]
                                    ).then_inc(w_hi_sb.sem, 1)

                for s in range(STEPS):
                    if s >= 2:
                        dve.wait_ge(plan.full_sem(("y", s - 2, TT - 1)), plan.after(("y", s - 2, TT - 1), i))
                    else:
                        dve.wait_ge(plan.full["Y3"], plan.turns("Y3", i))
                    for ht in range(NHT):
                        dve.wait_ge(plan.free_sem(("h", s, ht)), plan.after(("h", s, ht), i))
                        dve.tensor_copy(h_hi[:, s % 2, ht, :], h_sb[:, ht % 4, :]).then_inc(hi_sb.sem, 1)
                    if s < NCH:
                        next_weights(s)
                    if s:
                        sums(s - 1)
                    if s >= NCH and not last:
                        dve.wait_ge(plan.full_sem(("y", NCH - 1, TT - 1)), plan.after(("y", NCH - 1, TT - 1), i))
                        next_weights(s)
                    if s > NCH and last:
                        statistics(s - 1 - NCH)
                        if s > NCH + 1:
                            norm(s - 2 - NCH)
                sums(STEPS - 1)
                if last:
                    statistics(NCH - 1)
                    norm(NCH - 2)
                    norm(NCH - 1)

            turns(dve, turn)

        @block.tensor
        def _(pe):
            for banks in (pre, plan):
                prime(pe, [*banks.full.values(), *banks.free.values()])
            def mm(out_, lhsT, rhs, start=True, stop=True):
                return pe.matmul(out_, lhsT, rhs, start=start, stop=stop)

            def split_terms(hi, lo):
                (a_hi, b_hi), (a_lo, b_lo) = hi, lo
                return ((a_hi, b_hi), (a_hi, b_lo), (a_lo, b_hi))

            pe.wait_ge(s_const, 5)
            for j in range(NCH):
                pe.wait_ge(s_x2[j], 16)
                for c in range(NC):
                    f = ("x2T", j, c)
                    pe.wait_ge(pre.free_sem(f), pre.before(f, 0))
                    for k in range(TT):
                        last = pe.transpose(pst[pre.bank(f)][:, P * k:P * k + P],
                                            x2[:, TT * j + k, P * c:P * c + P], ident[:, :])
                    last.then_inc(pre.full_sem(f), 1)
            pe.wait_ge(s_router, 1)
            pe.wait_ge(pre.free_sem(("x2T", NCH - 1, NC - 1)), pre.after(("x2T", NCH - 1, NC - 1), 0))
            for j in range(NCH):
                f = ("scores", j)
                tok = slice(CH * j, CH * j + CH)
                terms = [x for c in range(NC) for x in split_terms(
                    (r_hi[:, c, :], x_hi[:, c, tok]), (r_lo[:, c, :], x_lo[:, c, tok]))]
                pe.wait_ge(pre.free_sem(f), pre.before(f, 0))
                for n, (a, b) in enumerate(terms):
                    last = mm(pst[pre.bank(f)][0:NE, :], a, b, n == 0, n == len(terms) - 1)
                last.then_inc(pre.full_sem(f), 1)
            for j in range(NCH):
                pe.wait_ge(pre.free_sem(("scores", j)), pre.after(("scores", j), 0))
                for t in range(TT * j, TT * j + TT):
                    last = pe.transpose(pst["Y0"][:, NE * t:NE * t + NE], scT[:, P * t:P * t + P],
                                        ident[0:NE, 0:NE])
            last.then_inc(pre.full_sem("route"), 1)
            pe.wait_ge(s_rt, 1)
            for j in range(4):
                f = ("rT", j)
                pe.wait_ge(pre.free_sem(f), pre.before(f, 0))
                for k in range(TT):
                    t = TT * j + k
                    last = pe.transpose(pst[pre.bank(f)][0:NE, P * k:P * k + P],
                                        small[:, 0, NE * t:NE * t + NE], ident[:, :])
                last.then_inc(pre.full_sem(f), 1)
            for j in range(TILES // 2):
                f = ("b2", j)
                pe.wait_ge(pre.free_sem(f), pre.before(f, 0))
                pe.wait_ge(pre.free_sem(("rT", j // 2)), pre.after(("rT", j // 2), 0))
                for k in range(2):
                    t = 2 * j + k
                    last = mm(pst[pre.bank(f)][:, C * k:C * k + C], rT[:, P * t:P * t + P], b2[:, :])
                last.then_inc(pre.full_sem(f), 1)
            pe.wait_ge(s_split0, 4)
            for j in range(4):
                pe.wait_ge(pre.free_sem(("b2", TILES // 2 - 4 + j)), pre.after(("b2", TILES // 2 - 4 + j), 0))

            def turn(i, last_turn):
                def hidden(s):
                    e, j = s // NCH, s % NCH
                    tok = slice(CH * j, CH * j + CH)
                    if s == 0:
                        pe.wait_ge(w_split.sem, w_split.at(i, 0))
                    if s == NCH:
                        pe.wait_ge(w_split.sem, w_split.at(i, 4))
                    for ht in range(NHT):
                        f = ("h", s, ht)
                        pe.wait_ge(plan.free_sem(f), plan.before(f, i))
                        col = slice(P * ht, P * ht + P)
                        terms = [x for c in range(NC) for x in split_terms(
                            (w_hi[:, e, c, col], x_hi[:, c, tok]), (w_lo[:, e, c, col], x_lo[:, c, tok]))]
                        for n, (a, b) in enumerate(terms):
                            last = mm(pst[plan.bank(f)][:, :], a, b, n == 0, n == len(terms) - 1)
                        last.then_inc(plan.full_sem(f), 1)

                def outputs(s):
                    e = s // NCH
                    pe.wait_ge(lo_sb.sem, lo_sb.at(i, NHT * s + NHT))
                    for tt in range(TT):
                        f = ("y", s, tt)
                        tok = slice(P * tt, P * tt + P)
                        pe.wait_ge(plan.free_sem(f), plan.before(f, i))
                        terms = []
                        for ht in range(NHT):
                            row = slice(C * (ht % 4), C * (ht % 4) + C)
                            terms += split_terms(
                                (h_hi[:, s % 2, ht, tok], w_hi[:, e, 2 + ht // 4, row]),
                                (h_lo[:, s % 2, ht, tok], w_lo[:, e, 2 + ht // 4, row]))
                        for n, (a, b) in enumerate(terms):
                            last = mm(pst[plan.bank(f)][:, 0:C], a, b, n == 0, n == len(terms) - 1)
                        last.then_inc(plan.full_sem(f), 1)

                for s in range(STEPS):
                    hidden(s)
                    if s:
                        outputs(s - 1)
                outputs(STEPS - 1)

            turns(pe, turn)


def build(nc, w, out):
    x2_rows = nc.dram_tensor("x2_rows", (NB, P, NT, C), F32, kind="Internal").ap()
    attention_block(nc, x2_rows, w)
    expert_block(nc, x2_rows, w, out)


def _layouts(a):
    def heads(x, parts):
        return x.reshape(x.shape[0], NH, parts, HD).transpose(0, 2, 1, 3).reshape(x.shape[0], parts, HW)

    f = 1.0 / np.float32(10000.0) ** (np.arange(0, RP, 2, dtype=np.float32) / np.float32(RP))
    angle = np.outer(np.arange(T, dtype=np.float32), f.astype(np.float32)).astype(np.float32)
    g = {k: np.asarray(v) for k, v in a.items()}
    at, xa, ff = "L0_attn_w_", "L0_xattn_", "L0_ffn_"
    return {
        "x": g["x"], "ctx": g["ctx_1024"], "mask": g["mask_BxS2_bf1"].view(np.uint8),
        "cq": g[at + "cq"], "ckv": g[at + "ckv"], "krope": g[at + "krope"], "gate": g[at + "gate"],
        "imp": g[at + "imp"], "g_q": g["L0_attn_g_qnorm"], "g_kv": g["L0_attn_g_kvnorm"],
        "cos": np.cos(angle), "sin": np.sin(angle),
        "dq_nopeT": g[at + "dq_nope"].reshape(QL, NH, HD).transpose(2, 1, 0),
        "dkT": g[at + "dk_nope"].reshape(KL, NH, HD).transpose(2, 1, 0),
        "dq": np.concatenate([heads(g[at + "dq_nope"], 1), heads(g[at + "dq_rope"], 2)], axis=1),
        "wink": heads(g[at + "wink"], 3), "winv": g[at + "winv"], "dv": g[at + "dv"],
        "selk": heads(g[at + "selk"], 3), "selv": g[at + "selv"], "proj": g[at + "proj"],
        "xqT": g[xa + "Wq"].T, "xkT": g[xa + "Wk"].T, "xvT": g[xa + "Wv"].T, "xoT": g[xa + "Wo"].T,
        "rows": np.stack([g[xa + "bq"], g[xa + "bk"], g[xa + "bv"], g[xa + "bo"]]),
        "W1": g[ff + "W1"], "W2": g[ff + "W2"], "Wr": g[ff + "Wr"], "br": g[ff + "br"],
        "b1": g[ff + "b1"].reshape(NE, NHT, P).transpose(2, 0, 1), "b2": g[ff + "b2"],
    }


def kernel(**inputs):
    import concourse.bacc as bacc
    from concourse.bass_utils import run_bass_kernel_spmd

    nc = bacc.Bacc("TRN2", target_bir_lowering=False, num_devices=1)
    arrays, w = {}, {}
    for name, a in _layouts(inputs).items():
        a = np.ascontiguousarray(a)
        arrays[f"in_{name}"] = a
        w[name] = nc.dram_tensor(f"in_{name}", a.shape, mybir.dt.from_np(a.dtype), kind="ExternalInput").ap()
    out = nc.dram_tensor("out_0", (NB, T, C), F32, kind="ExternalOutput").ap()
    build(nc, w, out)
    r = run_bass_kernel_spmd(nc, [arrays], core_ids=[0])
    return r.results[0]["out_0"]
```
